# Optimizing a Trainium2 kernel written in Bass

```python
import numpy as np
import jax
import jax.numpy as jnp

def _softmax(x, axis=-1):
    return jax.nn.softmax(x, axis=axis)

def _gelu(x):
    return jax.nn.gelu(x, approximate=True)

def _silu(x):
    return jax.nn.silu(x)

def _sigmoid(x):
    return jax.nn.sigmoid(x)

def _layernorm(x, axis=-1, eps=1e-05):
    m = jnp.mean(x, axis=axis, keepdims=True)
    v = jnp.var(x, axis=axis, keepdims=True)
    return (x - m) / jnp.sqrt(v + eps)

def _scatter_add(tgt, idx, src, axis=0):
    return tgt.at[idx].add(src)

def _segment_sum(src, seg, n):
    return jax.ops.segment_sum(src, seg, n)
kernel_name = 'mk_seq_postln_d2_jaxref_r8_632a3b'

def setup_inputs(seed: int=0):
    np.random.seed(seed)
    _w = jnp.asarray

    def _L0_attn_setup():
        import jax, jax.numpy as jnp
        import numpy as np
        import math
        DIM = 128
        NUM_HEADS = 16
        HEAD_DIM = 64

        def _rope(q, k, seq_len, head_dim):
            half = head_dim // 2
            pos = jnp.arange(seq_len, dtype=jnp.float32)[:, None]
            freq = 1.0 / 10000.0 ** (jnp.arange(half, dtype=jnp.float32) / half)
            angles = pos * freq[None, :]
            sin = jnp.sin(angles)[None, None]
            cos = jnp.cos(angles)[None, None]

            def rot(t):
                t = t.reshape(*t.shape[:-1], half, 2)
                t0, t1 = (t[..., 0], t[..., 1])
                r0 = t0 * cos - t1 * sin
                r1 = t1 * cos + t0 * sin
                return jnp.stack([r0, r1], axis=-1).reshape(*t0.shape[:-1], head_dim)
            return (rot(q), rot(k))
        key = jax.random.key(seed)
        k1, k2, k3 = jax.random.split(key, 3)
        B, S = (2, 256)
        x = jax.random.normal(k1, (B, S, DIM), dtype=jnp.float32)
        qkv_w = jax.random.normal(k2, (DIM, 3 * NUM_HEADS * HEAD_DIM), dtype=jnp.float32) * 0.02
        qkv_b = jnp.zeros((3 * NUM_HEADS * HEAD_DIM,), dtype=jnp.float32)
        out_w = jax.random.normal(k3, (NUM_HEADS * HEAD_DIM, DIM), dtype=jnp.float32) * 0.02
        out_b = jnp.zeros((DIM,), dtype=jnp.float32)
        return {'x': x, 'qkv_w': qkv_w, 'qkv_b': qkv_b, 'out_w': out_w, 'out_b': out_b}
    _L0_attn_in = _L0_attn_setup()

    def _L0_ffn_setup():
        import jax, jax.numpy as jnp
        import numpy as np
        DIM = 128
        DEPTH = 2
        HEADS = 8
        DIM_HEAD = 64
        WINDOW = 64
        INNER = HEADS * DIM_HEAD
        HID = int(DIM * 4 * 2 / 3)
        B, N = (2, 1024)
        QK_SCALE = 8.0

        def shift_token(t):
            t1, t2 = jnp.split(t, 2, axis=-1)
            t2 = jnp.pad(t2, ((0, 0), (1, 0), (0, 0)))[:, :-1]
            return jnp.concatenate([t1, t2], axis=-1)

        def l2norm(t):
            return t / jnp.clip(jnp.linalg.norm(t, axis=-1, keepdims=True), 1e-12)

        def rotate_half(x):
            x1, x2 = jnp.split(x, 2, axis=-1)
            return jnp.concatenate([-x2, x1], axis=-1)

        def rotary_xpos(q, k):
            n = q.shape[-2]
            half_idx = jnp.arange(0, DIM_HEAD, 2, dtype=jnp.float32)
            inv_freq = 1.0 / 10000.0 ** (half_idx / DIM_HEAD)
            t = jnp.arange(n, dtype=jnp.float32)
            freqs = t[:, None] * inv_freq[None, :]
            freqs = jnp.concatenate([freqs, freqs], axis=-1)
            base = (half_idx + 0.4 * DIM_HEAD) / (1.4 * DIM_HEAD)
            power = (t - n // 2) / float(WINDOW // 2)
            scale = base[None, :] ** power[:, None]
            scale = jnp.concatenate([scale, scale], axis=-1)
            cos, sin = (jnp.cos(freqs), jnp.sin(freqs))
            q = q * cos * scale + rotate_half(q) * sin * scale
            k = k * cos / scale + rotate_half(k) * sin / scale
            return (q, k)

        def local_attention(q, k, v):
            b, h, n, d = q.shape
            w = n // WINDOW
            bq = q.reshape(b, h, w, WINDOW, d) * QK_SCALE
            bk = k.reshape(b, h, w, WINDOW, d)
            bv = v.reshape(b, h, w, WINDOW, d)

            def look_around(t):
                p = jnp.pad(t, ((0, 0), (0, 0), (1, 0), (0, 0), (0, 0)))
                return jnp.concatenate([p[:, :, :w], p[:, :, 1:]], axis=3)
            bk, bv = (look_around(bk), look_around(bv))
            bt = jnp.arange(n).reshape(w, WINDOW)
            btp = jnp.pad(bt, ((1, 0), (0, 0)), constant_values=-1)
            btk = jnp.concatenate([btp[:w], btp[1:]], axis=1)
            sim = jnp.einsum('bhwid,bhwjd->bhwij', bq, bk)
            i = bt[:, :, None]
            j = btk[:, None, :]
            mask = (i < j) | (i > j + WINDOW) | (j == -1)
            sim = jnp.where(mask, -jnp.finfo(sim.dtype).max, sim)
            attn = jax.nn.softmax(sim, axis=-1)
            out = jnp.einsum('bhwij,bhwjd->bhwid', attn, bv)
            return out.reshape(b, h, n, d)

        def _layer(x, wqkv, qs, ksc, wo, lg, lb, w1, b1, w2, b2):
            b, n, _ = x.shape
            h = shift_token(x)
            qkv = h @ wqkv
            q, k, v = jnp.split(qkv, 3, axis=-1)
            to_heads = lambda t: t.reshape(b, n, HEADS, DIM_HEAD).transpose(0, 2, 1, 3)
            q, k, v = (to_heads(q), to_heads(k), to_heads(v))
            q = l2norm(q) * qs
            k = l2norm(k) * ksc
            q, k = rotary_xpos(q, k)
            o = local_attention(q, k, v)
            o = o.transpose(0, 2, 1, 3).reshape(b, n, INNER)
            x = x + o @ wo
            h = shift_token(x)
            mu = h.mean(-1, keepdims=True)
            var = h.var(-1, keepdims=True)
            h = (h - mu) / jnp.sqrt(var + 1e-05) * lg + lb
            h = h @ w1 + b1
            a, g = jnp.split(h, 2, axis=-1)
            h = a * jax.nn.gelu(g, approximate=False)
            x = x + h @ w2 + b2
            return x
        key = jax.random.key(seed)
        ks = jax.random.split(key, 6)
        return {'x': jax.random.normal(ks[0], (B, N, DIM), jnp.float32), 'wqkv': jax.random.normal(ks[1], (DEPTH, DIM, 3 * INNER), jnp.float32) * 0.02, 'q_scale': jnp.ones((DEPTH, DIM_HEAD), jnp.float32), 'k_scale': jnp.ones((DEPTH, DIM_HEAD), jnp.float32), 'wo': jax.random.normal(ks[2], (DEPTH, INNER, DIM), jnp.float32) * 0.02, 'ln_g': jnp.ones((DEPTH, DIM), jnp.float32), 'ln_b': jnp.zeros((DEPTH, DIM), jnp.float32), 'w1': jax.random.normal(ks[3], (DEPTH, DIM, 2 * HID), jnp.float32) * 0.02, 'b1': jnp.zeros((DEPTH, 2 * HID), jnp.float32), 'w2': jax.random.normal(ks[4], (DEPTH, HID, DIM), jnp.float32) * 0.02, 'b2': jnp.zeros((DEPTH, DIM), jnp.float32)}
    _L0_ffn_in = _L0_ffn_setup()

    def _L1_attn_setup():
        import jax, jax.numpy as jnp
        import numpy as np
        D_MODEL = 128
        N_HEADS = 16
        KEY_DIM = D_MODEL // 2
        VAL_DIM = D_MODEL
        HEAD_QK = KEY_DIM // N_HEADS
        HEAD_V = VAL_DIM // N_HEADS
        PROJ_LR = 32
        GATE_LR = 64
        EPS = 1e-05
        key = jax.random.key(seed)
        ks = jax.random.split(key, 16)
        s = 0.02
        B, T = (4, 128)
        return {'x': jax.random.normal(ks[0], (B, T, D_MODEL), jnp.float32), 'mu_x': jax.random.normal(ks[1], (D_MODEL,), jnp.float32) * s, 'W_x1': jax.random.normal(ks[2], (D_MODEL, 5 * PROJ_LR), jnp.float32) * s, 'W_x2': jax.random.normal(ks[3], (D_MODEL, 5, PROJ_LR), jnp.float32) * s, 'x_bias': jax.random.normal(ks[4], (5, D_MODEL), jnp.float32) * s, 'W_r': jax.random.normal(ks[5], (D_MODEL, KEY_DIM), jnp.float32) * s, 'W_w1': jax.random.normal(ks[6], (D_MODEL, GATE_LR), jnp.float32) * s, 'W_w2': jax.random.normal(ks[7], (GATE_LR, KEY_DIM), jnp.float32) * s, 'b_w2': jax.random.normal(ks[8], (KEY_DIM,), jnp.float32) * s, 'W_k': jax.random.normal(ks[9], (D_MODEL, KEY_DIM), jnp.float32) * s, 'W_v': jax.random.normal(ks[10], (D_MODEL, VAL_DIM), jnp.float32) * s, 'W_g': jax.random.normal(ks[11], (D_MODEL, VAL_DIM), jnp.float32) * s, 'u': jax.random.normal(ks[12], (N_HEADS, HEAD_QK), jnp.float32) * s, 'gn_w': jnp.ones((VAL_DIM,), jnp.float32), 'gn_b': jnp.zeros((VAL_DIM,), jnp.float32), 'W_o': jax.random.normal(ks[13], (VAL_DIM, D_MODEL), jnp.float32) * s}
    _L1_attn_in = _L1_attn_setup()

    def _L1_ffn_setup():
        import jax, jax.numpy as jnp
        import numpy as np
        DIM = 128
        HIDDEN = 384
        SCALE = 1.0 / 127.0

        def _dequant(w_int, dtype):
            return w_int.astype(dtype) * jnp.asarray(SCALE, dtype)
        key = jax.random.key(seed)
        k_x, k_g, k_u, k_d = jax.random.split(key, 4)
        x = jax.random.normal(k_x, (4, 256, DIM), dtype=jnp.float32)
        w_gate = jax.random.randint(k_g, (HIDDEN, DIM), -127, 128, dtype=jnp.int32)
        w_up = jax.random.randint(k_u, (HIDDEN, DIM), -127, 128, dtype=jnp.int32)
        w_down = jax.random.randint(k_d, (DIM, HIDDEN), -127, 128, dtype=jnp.int32)
        return {'x': x, 'w_gate': w_gate, 'w_up': w_up, 'w_down': w_down}
    _L1_ffn_in = _L1_ffn_setup()
    _d = {'L0_attn_x': _L0_attn_in['x'], 'L0_attn_qkv_w': _L0_attn_in['qkv_w'], 'L0_attn_qkv_b': _L0_attn_in['qkv_b'], 'L0_attn_out_w': _L0_attn_in['out_w'], 'L0_attn_out_b': _L0_attn_in['out_b'], 'L0_ffn_wqkv': _L0_ffn_in['wqkv'], 'L0_ffn_q_scale': _L0_ffn_in['q_scale'], 'L0_ffn_k_scale': _L0_ffn_in['k_scale'], 'L0_ffn_wo': _L0_ffn_in['wo'], 'L0_ffn_ln_g': _L0_ffn_in['ln_g'], 'L0_ffn_ln_b': _L0_ffn_in['ln_b'], 'L0_ffn_w1': _L0_ffn_in['w1'], 'L0_ffn_b1': _L0_ffn_in['b1'], 'L0_ffn_w2': _L0_ffn_in['w2'], 'L0_ffn_b2': _L0_ffn_in['b2'], 'L1_attn_mu_x': _L1_attn_in['mu_x'], 'L1_attn_W_x1': _L1_attn_in['W_x1'], 'L1_attn_W_x2': _L1_attn_in['W_x2'], 'L1_attn_x_bias': _L1_attn_in['x_bias'], 'L1_attn_W_r': _L1_attn_in['W_r'], 'L1_attn_W_w1': _L1_attn_in['W_w1'], 'L1_attn_W_w2': _L1_attn_in['W_w2'], 'L1_attn_b_w2': _L1_attn_in['b_w2'], 'L1_attn_W_k': _L1_attn_in['W_k'], 'L1_attn_W_v': _L1_attn_in['W_v'], 'L1_attn_W_g': _L1_attn_in['W_g'], 'L1_attn_u': _L1_attn_in['u'], 'L1_attn_gn_w': _L1_attn_in['gn_w'], 'L1_attn_gn_b': _L1_attn_in['gn_b'], 'L1_attn_W_o': _L1_attn_in['W_o'], 'L1_ffn_w_gate': _L1_ffn_in['w_gate'], 'L1_ffn_w_up': _L1_ffn_in['w_up'], 'L1_ffn_w_down': _L1_ffn_in['w_down']}
    _x0 = _d['L0_attn_x']
    _d['L0_attn_x'] = jax.random.normal(jax.random.fold_in(jax.random.key(seed), 1), (1, 2048, 128), dtype=_x0.dtype)
    del _x0
    return _d

def reference(L0_attn_x, L0_attn_qkv_w, L0_attn_qkv_b, L0_attn_out_w, L0_attn_out_b, L0_ffn_wqkv, L0_ffn_q_scale, L0_ffn_k_scale, L0_ffn_wo, L0_ffn_ln_g, L0_ffn_ln_b, L0_ffn_w1, L0_ffn_b1, L0_ffn_w2, L0_ffn_b2, L1_attn_mu_x, L1_attn_W_x1, L1_attn_W_x2, L1_attn_x_bias, L1_attn_W_r, L1_attn_W_w1, L1_attn_W_w2, L1_attn_b_w2, L1_attn_W_k, L1_attn_W_v, L1_attn_W_g, L1_attn_u, L1_attn_gn_w, L1_attn_gn_b, L1_attn_W_o, L1_ffn_w_gate, L1_ffn_w_up, L1_ffn_w_down):

    def _L0_attn_ref(x, qkv_w, qkv_b, out_w, out_b):
        import jax, jax.numpy as jnp
        import numpy as np
        import math
        DIM = 128
        NUM_HEADS = 16
        HEAD_DIM = 64

        def _rope(q, k, seq_len, head_dim):
            half = head_dim // 2
            pos = jnp.arange(seq_len, dtype=jnp.float32)[:, None]
            freq = 1.0 / 10000.0 ** (jnp.arange(half, dtype=jnp.float32) / half)
            angles = pos * freq[None, :]
            sin = jnp.sin(angles)[None, None]
            cos = jnp.cos(angles)[None, None]

            def rot(t):
                t = t.reshape(*t.shape[:-1], half, 2)
                t0, t1 = (t[..., 0], t[..., 1])
                r0 = t0 * cos - t1 * sin
                r1 = t1 * cos + t0 * sin
                return jnp.stack([r0, r1], axis=-1).reshape(*t0.shape[:-1], head_dim)
            return (rot(q), rot(k))
        B, S, _ = x.shape
        H, D = (NUM_HEADS, HEAD_DIM)
        qkv = x @ qkv_w + qkv_b
        qkv = qkv.reshape(B, S, 3, H, D)
        qkv = jnp.transpose(qkv, (2, 0, 3, 1, 4))
        q, k, v = (qkv[0], qkv[1], qkv[2])
        q, k = _rope(q, k, S, D)
        scale = math.sqrt(D)
        attn = jnp.einsum('bhqd,bhkd->bhqk', q, k) / scale
        attn = jax.nn.softmax(attn, axis=-1)
        out = jnp.einsum('bhqk,bhkd->bhqd', attn, v)
        out = jnp.transpose(out, (0, 2, 1, 3)).reshape(B, S, H * D)
        return out @ out_w + out_b

    def _L0_ffn_ref(x, wqkv, q_scale, k_scale, wo, ln_g, ln_b, w1, b1, w2, b2):
        import jax, jax.numpy as jnp
        import numpy as np
        DIM = 128
        DEPTH = 2
        HEADS = 8
        DIM_HEAD = 64
        WINDOW = 64
        INNER = HEADS * DIM_HEAD
        HID = int(DIM * 4 * 2 / 3)
        B, N = (2, 1024)
        QK_SCALE = 8.0

        def shift_token(t):
            t1, t2 = jnp.split(t, 2, axis=-1)
            t2 = jnp.pad(t2, ((0, 0), (1, 0), (0, 0)))[:, :-1]
            return jnp.concatenate([t1, t2], axis=-1)

        def l2norm(t):
            return t / jnp.clip(jnp.linalg.norm(t, axis=-1, keepdims=True), 1e-12)

        def rotate_half(x):
            x1, x2 = jnp.split(x, 2, axis=-1)
            return jnp.concatenate([-x2, x1], axis=-1)

        def rotary_xpos(q, k):
            n = q.shape[-2]
            half_idx = jnp.arange(0, DIM_HEAD, 2, dtype=jnp.float32)
            inv_freq = 1.0 / 10000.0 ** (half_idx / DIM_HEAD)
            t = jnp.arange(n, dtype=jnp.float32)
            freqs = t[:, None] * inv_freq[None, :]
            freqs = jnp.concatenate([freqs, freqs], axis=-1)
            base = (half_idx + 0.4 * DIM_HEAD) / (1.4 * DIM_HEAD)
            power = (t - n // 2) / float(WINDOW // 2)
            scale = base[None, :] ** power[:, None]
            scale = jnp.concatenate([scale, scale], axis=-1)
            cos, sin = (jnp.cos(freqs), jnp.sin(freqs))
            q = q * cos * scale + rotate_half(q) * sin * scale
            k = k * cos / scale + rotate_half(k) * sin / scale
            return (q, k)

        def local_attention(q, k, v):
            b, h, n, d = q.shape
            w = n // WINDOW
            bq = q.reshape(b, h, w, WINDOW, d) * QK_SCALE
            bk = k.reshape(b, h, w, WINDOW, d)
            bv = v.reshape(b, h, w, WINDOW, d)

            def look_around(t):
                p = jnp.pad(t, ((0, 0), (0, 0), (1, 0), (0, 0), (0, 0)))
                return jnp.concatenate([p[:, :, :w], p[:, :, 1:]], axis=3)
            bk, bv = (look_around(bk), look_around(bv))
            bt = jnp.arange(n).reshape(w, WINDOW)
            btp = jnp.pad(bt, ((1, 0), (0, 0)), constant_values=-1)
            btk = jnp.concatenate([btp[:w], btp[1:]], axis=1)
            sim = jnp.einsum('bhwid,bhwjd->bhwij', bq, bk)
            i = bt[:, :, None]
            j = btk[:, None, :]
            mask = (i < j) | (i > j + WINDOW) | (j == -1)
            sim = jnp.where(mask, -jnp.finfo(sim.dtype).max, sim)
            attn = jax.nn.softmax(sim, axis=-1)
            out = jnp.einsum('bhwij,bhwjd->bhwid', attn, bv)
            return out.reshape(b, h, n, d)

        def _layer(x, wqkv, qs, ksc, wo, lg, lb, w1, b1, w2, b2):
            b, n, _ = x.shape
            h = shift_token(x)
            qkv = h @ wqkv
            q, k, v = jnp.split(qkv, 3, axis=-1)
            to_heads = lambda t: t.reshape(b, n, HEADS, DIM_HEAD).transpose(0, 2, 1, 3)
            q, k, v = (to_heads(q), to_heads(k), to_heads(v))
            q = l2norm(q) * qs
            k = l2norm(k) * ksc
            q, k = rotary_xpos(q, k)
            o = local_attention(q, k, v)
            o = o.transpose(0, 2, 1, 3).reshape(b, n, INNER)
            x = x + o @ wo
            h = shift_token(x)
            mu = h.mean(-1, keepdims=True)
            var = h.var(-1, keepdims=True)
            h = (h - mu) / jnp.sqrt(var + 1e-05) * lg + lb
            h = h @ w1 + b1
            a, g = jnp.split(h, 2, axis=-1)
            h = a * jax.nn.gelu(g, approximate=False)
            x = x + h @ w2 + b2
            return x
        for l in range(DEPTH):
            x = _layer(x, wqkv[l], q_scale[l], k_scale[l], wo[l], ln_g[l], ln_b[l], w1[l], b1[l], w2[l], b2[l])
        return x

    def _L1_attn_ref(x, mu_x, W_x1, W_x2, x_bias, W_r, W_w1, W_w2, b_w2, W_k, W_v, W_g, u, gn_w, gn_b, W_o):
        import jax, jax.numpy as jnp
        import numpy as np
        D_MODEL = 128
        N_HEADS = 16
        KEY_DIM = D_MODEL // 2
        VAL_DIM = D_MODEL
        HEAD_QK = KEY_DIM // N_HEADS
        HEAD_V = VAL_DIM // N_HEADS
        PROJ_LR = 32
        GATE_LR = 64
        EPS = 1e-05
        B, T, D = x.shape
        shifted = jnp.pad(x, ((0, 0), (1, 0), (0, 0)))[:, :T]
        delta = shifted - x
        low = jnp.tanh((x + delta * mu_x) @ W_x1).reshape(B, T, 5, PROJ_LR)
        mus = jnp.einsum('blnr,dnr->blnd', low, W_x2) + x_bias
        xr, xw, xk, xv, xg = [x + delta * mus[:, :, i] for i in range(5)]
        r = (xr @ W_r).reshape(B, T, N_HEADS, HEAD_QK)
        w = (jnp.tanh(xw @ W_w1) @ W_w2 + b_w2).reshape(B, T, N_HEADS, HEAD_QK)
        k = (xk @ W_k).reshape(B, T, N_HEADS, HEAD_QK)
        v = (xv @ W_v).reshape(B, T, N_HEADS, HEAD_V)
        g = xg @ W_g
        w = -jnp.exp(w)

        def step(S, inp):
            r_t, k_t, v_t, w_t = inp
            o_t = jnp.einsum('bhk,bhkv->bhv', r_t, S) + jnp.einsum('bhk,hk,bhk,bhv->bhv', r_t, u, k_t, v_t)
            S = jnp.exp(w_t)[..., None] * S + k_t[..., :, None] * v_t[..., None, :]
            return (S, o_t)
        S0 = jnp.zeros((B, N_HEADS, HEAD_QK, HEAD_V), x.dtype)
        xs = tuple((jnp.moveaxis(t, 1, 0) for t in (r, k, v, w)))
        _, o = jax.lax.scan(step, S0, xs)
        o = jnp.moveaxis(o, 0, 1)
        mean = o.mean(-1, keepdims=True)
        var = o.var(-1, keepdims=True)
        o = ((o - mean) * jax.lax.rsqrt(var + EPS)).reshape(B, T, VAL_DIM)
        o = (o * gn_w + gn_b) * (g * jax.nn.sigmoid(g))
        return o @ W_o

    def _L1_ffn_ref(x, w_gate, w_up, w_down):
        import jax, jax.numpy as jnp
        import numpy as np
        DIM = 128
        HIDDEN = 384
        SCALE = 1.0 / 127.0

        def _dequant(w_int, dtype):
            return w_int.astype(dtype) * jnp.asarray(SCALE, dtype)
        wg = _dequant(w_gate, x.dtype)
        wu = _dequant(w_up, x.dtype)
        wd = _dequant(w_down, x.dtype)
        gate = jnp.einsum('bsd,hd->bsh', x, wg)
        up = jnp.einsum('bsd,hd->bsh', x, wu)
        h = jax.nn.silu(gate) * up
        return jnp.einsum('bsh,dh->bsd', h, wd)
    x = L0_attn_x
    x = _layernorm(x + _L0_attn_ref(x, L0_attn_qkv_w, L0_attn_qkv_b, L0_attn_out_w, L0_attn_out_b), axis=-1)
    x = _layernorm(x + _L0_ffn_ref(x, L0_ffn_wqkv, L0_ffn_q_scale, L0_ffn_k_scale, L0_ffn_wo, L0_ffn_ln_g, L0_ffn_ln_b, L0_ffn_w1, L0_ffn_b1, L0_ffn_w2, L0_ffn_b2), axis=-1)
    x = _layernorm(x + _L1_attn_ref(x, L1_attn_mu_x, L1_attn_W_x1, L1_attn_W_x2, L1_attn_x_bias, L1_attn_W_r, L1_attn_W_w1, L1_attn_W_w2, L1_attn_b_w2, L1_attn_W_k, L1_attn_W_v, L1_attn_W_g, L1_attn_u, L1_attn_gn_w, L1_attn_gn_b, L1_attn_W_o), axis=-1)
    x = _layernorm(x + _L1_ffn_ref(x, L1_ffn_w_gate, L1_ffn_w_up, L1_ffn_w_down), axis=-1)
    return x

_drawn_inputs = setup_inputs


def setup_inputs(seed=0):
    import zlib

    import numpy as np

    out = dict(_drawn_inputs(seed))
    spreads = {'L0_attn_qkv_b': (0.0, 0.1),
     'L0_attn_out_b': (0.0, 0.1),
     'L0_ffn_q_scale': (1.0, 0.6),
     'L0_ffn_k_scale': (1.0, 0.6),
     'L0_ffn_ln_g': (1.0, 0.6),
     'L0_ffn_ln_b': (0.0, 0.8),
     'L0_ffn_b1': (0.0, 0.8),
     'L0_ffn_b2': (0.0, 0.1),
     'L1_attn_gn_w': (1.0, 0.6),
     'L1_attn_gn_b': (0.0, 0.8)}
    factors = {'L0_attn_qkv_w': 8.0,
     'L0_ffn_w1': 4.273,
     'L0_ffn_w2': 4.219,
     'L1_attn_mu_x': 8.0,
     'L1_attn_W_x1': 8.0,
     'L1_attn_W_x2': 8.0,
     'L1_attn_x_bias': 8.0,
     'L1_attn_W_w1': 8.0,
     'L1_attn_W_w2': 8.0,
     'L1_attn_b_w2': 64.0,
     'L1_attn_u': 25.772}
    for name, (base, spread) in spreads.items():
        noise = np.random.default_rng([zlib.crc32(name.encode()), seed]).standard_normal(out[name].shape)
        drawn = base * np.exp(spread * noise) if base else spread * noise
        out[name] = jnp.asarray(drawn.astype(out[name].dtype))
    for name, factor in factors.items():
        out[name] = (out[name] * factor).astype(out[name].dtype)
    return out
```

```python
from contextlib import ExitStack

import numpy as np
import concourse.bass as bass
from concourse import mybir

ALU = mybir.AluOpType
ACT = mybir.ActivationFunctionType
AX = mybir.AxisListType.X
F32 = mybir.dt.float32
F16 = mybir.dt.float16
I32 = mybir.dt.int32

P = 128
D = 128
S = 2048
NT = S // P
CH = 512
NCH = S // CH
TPC = CH // P
LN_EPS = 1e-5


class Scope:
    used = []

    def __init__(self, nc, prefix):
        self.nc, self.prefix, self.stack = nc, prefix, ExitStack()

    def __enter__(self):
        return self

    def __exit__(self, *exc):
        return self.stack.__exit__(*exc)

    def sb(self, name, shape, dt=F32):
        return self.stack.enter_context(self.nc.sbuf_tensor(self.prefix + name, shape, dt))

    def ps(self, name, shape, dt=F32):
        return self.stack.enter_context(self.nc.psum_tensor(self.prefix + name, shape, dt))

    def sem(self, name):
        handle = self.nc.alloc_semaphore(name=self.prefix + name)
        Scope.used.append(handle)
        return handle


def clear_semaphores(nc):
    nc.clear_and_free_semaphores(Scope.used)
    nc.all_engine_barrier()
    Scope.used.clear()


def ge(eng, sem, value, alone=None):
    if isinstance(value, int):
        if value > 0:
            eng.wait_ge(sem, value)
        return
    if alone is not None:
        value = eng.to_reg(value)
        eng.wait_ge(alone, 1)
    eng.wait_ge(sem, value)


def ge_both(eng, sem_a, value_a, sem_b, value_b):
    if not isinstance(value_a, int):
        value_a, value_b = eng.to_reg(value_a), eng.to_reg(value_b)
    ge(eng, sem_a, value_a)
    ge(eng, sem_b, value_b)


class LayerNorm:

    def __init__(self, sc):
        self.stats = sc.sb("ln_stats", [P, NT, 6])
        self.mv = sc.sb("ln_mean_var", [P, NT, 2])
        self.eps = sc.sb("ln_eps", [P, 1])
        self.std = sc.sb("ln_std", [P, NT])
        self.rstd = sc.sb("ln_rstd", [P, NT])


def layernorm_block(nc, ln, name, rows, x_out):
    stats, mv, eps, std, rstd = ln.stats, ln.mv, ln.eps, ln.std, ln.rstd
    with Scope(nc, name) as sc:
        eps_set, stats_done, var_done, std_done, rstd_done, normed = (
            sc.sem(n) for n in ("eps_set", "stats_done", "var_done", "std_done", "rstd_done", "normed"))
        with nc.Block() as block:

            @block.vector
            def _(dve):
                dve.memset(eps[:, :], LN_EPS).then_inc(eps_set, 1)
                for t in range(NT):
                    dve.bn_stats(stats[:, t, :], rows[:, t, :]).then_inc(stats_done, 1)
                for t in range(NT):
                    dve.wait_ge(stats_done, t + 1)
                    dve.bn_aggr(mv[:, t, :], stats[:, t, :]).then_inc(var_done, 1)
                dve.wait_ge(std_done, 1)
                dve.reciprocal(rstd[:, :], std[:, :]).then_inc(rstd_done, 1)
                dve.wait_ge(rstd_done, 1)
                for t in range(NT):
                    dve.tensor_scalar(x_out[:, t, :], rows[:, t, :], mv[:, t, 0:1], rstd[:, t:t + 1],
                                      ALU.subtract, ALU.mult).then_inc(normed, 1)

            @block.scalar
            def _(act):
                act.wait_ge(eps_set, 1)
                act.wait_ge(var_done, NT)
                act.activation(std[:, :], mv[:, :, 1], ACT.Sqrt, bias=eps[:, 0:1]).then_inc(std_done, 1)


def load_block(nc, x_sb, ident, x_dram, ident_dram):
    with Scope(nc, "ld_") as sc:
        loaded = sc.sem("loaded")
        with nc.Block() as block:
            @block.sync
            def _(sp):
                sp.dma_start(x_sb[:, :, :], x_dram.rearrange("(t p) d -> p t d", p=P)).then_inc(loaded, 16)
                sp.dma_start(ident[:, :], ident_dram).then_inc(loaded, 16)
                sp.wait_ge(loaded, 32)


def store_block(nc, x_sb, out_dram):
    with Scope(nc, "st_") as sc:
        stored = sc.sem("stored")
        with nc.Block() as block:
            @block.sync
            def _(sp):
                sp.dma_start(out_dram.rearrange("(t p) d -> p t d", p=P), x_sb[:, :, :]).then_inc(stored, 16)
                sp.wait_ge(stored, 16)


HEADS, HD = 16, 64
KT = NT
QC = NCH
SETS = 3
VW = HD + 1
LAST = HEADS - 1
MAX_SLOTS = (2, 1, 1, 1, 1, 1, 2, 1, 1, 1, 1, 1, 1, 1, 0, 0)
LAG = 5
TAIL = {0: (KT - LAG, KT - LAG + 1), **{i: (KT - LAG + 1 + i,) for i in range(1, LAG - 1)}}
RP, RW = 4, 8
LO_DVE = (3, 6, 9, 11, 14)
LO_POOL = tuple(kt for kt in range(KT) if kt not in LO_DVE)
HI_DVE = (6, 11)
HI_ACT = tuple(kt for kt in range(KT) if kt not in HI_DVE)
EXP_SHIFT = 12 * float(np.log(2.0)) * HD ** 0.5


def phase_mha(nc, x_sb, ident, a, ln):
    with Scope(nc, "a_") as sc:
        attn = sc.sb("attn", [P, NT, HEADS * HD])
        mha_heads(nc, x_sb, ident, a, attn)
        mha_out(nc, x_sb, ident, a, ln, attn)


def run_heads(eng, head, turn):
    for n in (-2, -1):
        head(n, n % SETS)
        for qc in range(QC):
            turn(n, n % SETS, qc)

    def one(n, s):
        head(n, s)
        turn(n, s, 0)
        with eng.Fori(1, QC) as qc:
            turn(n, s, qc)

    one(0, 0)
    with eng.Fori(0, 4) as third:
        for i in range(SETS):
            one(third * SETS + (i + 1), (i + 1) % SETS)
    for n in range(4 * SETS + 1, HEADS):
        one(n, n % SETS)


def before(n, s, qc):
    return (n - 1, (s - 1) % SETS, QC - 1) if isinstance(qc, int) and qc == 0 else (n, s, qc - 1)


def foldone(n, qc):
    return has(n, 0) and not (isinstance(n, int) and n == 0 and isinstance(qc, int) and qc == 0)


def found_max(n, qc):
    if not isinstance(n, int):
        return True
    return 0 <= (n - 1 if isinstance(qc, int) and qc == 0 else n) + 1 <= LAST


def done(which, e, kt):
    if kt < 0:
        e, kt = e - 1, kt + KT
    return len(which) * e + sum(t <= kt for t in which)


def has(n, ahead):
    return not isinstance(n, int) or 0 <= n + ahead <= LAST


def cols(c, w):
    return slice(c * w, c * w + w) if isinstance(c, int) else bass.ds(c * w, w)


def mha_heads(nc, x_sb, ident, a, attn):
    with Scope(nc, "ah_") as sc:
        xh = sc.sb("xT_hi", [P, S], F16)
        xl = sc.sb("xT_lo", [P, S], F16)
        cos = sc.sb("cos", [P, S])
        sin = sc.sb("sin", [P, S])
        bv = sc.sb("bias_v", [P, HEADS, HD])
        w32 = sc.sb("w_head", [P, 3 * HD])
        wh = sc.sb("w_hi", [P, 3 * HD], F16)
        wl = sc.sb("w_lo", [P, 3 * HD], F16)
        bqk = sc.sb("bias_qk", [P, HEADS])
        qh = sc.sb("q_hi_twice", [P, SETS, S], F16)
        ks = sc.sb("k_hi_lo", [P, SETS, S], F16)
        k1 = sc.sb("k_hi_one", [P, SETS, S], F16)
        ql = sc.sb("q_lo_max", [P, SETS, S], F16)
        vh = sc.sb("v_hi", [P, SETS, KT, VW], F16)
        vl = sc.sb("v_lo", [P, SETS, KT, HD], F16)
        v32 = sc.sb("v", [P, TPC, HD])
        qk = sc.sb("qk", [P, CH])
        qks = sc.sb("qk_swapped", [P, CH])
        t1 = sc.sb("rot_cos", [P, CH])
        t2 = sc.sb("rot_sin", [P, CH])
        r = sc.sb("rotated", [P, CH])
        hi = sc.sb("hi", [P, CH], F16)
        lo = sc.sb("lo", [P, CH], F16)
        part = sc.sb("part_max", [P, TPC, 4])
        negm = sc.sb("neg_max", [P, TPC], F16)
        identh = sc.sb("ident_f16", [P, P], F16)
        pb = sc.sb("probs", [P, RP, CH])
        ph = sc.sb("probs_hi", [P, RW, CH], F16)
        pl = sc.sb("probs_lo", [P, RW, CH], F16)
        rcp = sc.sb("rcp", [P, TPC])

        p_s = sc.ps("p_s", [P, 2, CH])
        p_o = sc.ps("p_o", [P, CH])
        p_m = sc.ps("p_m", [P, 2, CH])
        p_a = sc.ps("p_a", [P, CH])
        p_v = sc.ps("p_v", [P, CH])
        p_t = p_a
        v_ones = sc.sem("v_ones")
        (c_in, w_in, x_turned, xh_ready, xl_ready, consts, w_split, proj_ready, qk_ready, swapped, t1_done, t2_done,
         r_ready, hi_done, lo_done, spread, v_ready, v_done, m_ready, maxed, m_done, m_turned, mrow_ready,
         s_ready, exp_done, hi_act, hi_dve, lo_pool, lo_dve, v_biased, vh_done, o_ready, rcp_done, o_free) = (sc.sem(n) for n in (
             "c_in", "w_in", "x_turned", "xh_ready", "xl_ready", "consts", "w_split", "proj_ready", "qk_ready",
             "swapped", "t1_done", "t2_done", "r_ready", "hi_done", "lo_done", "spread", "v_ready", "v_done",
             "m_ready", "maxed", "m_done", "m_turned", "mrow_ready", "s_ready", "exp_done", "hi_act", "hi_dve", "lo_pool",
             "lo_dve", "v_biased", "vh_done", "o_ready", "rcp_done", "o_free"))
        SPREAD = 6 * 16

        with nc.Block() as block:

            @block.sync
            def _(sp):
                sp.dma_start(w32[:, :], a["w_heads"][0]).then_inc(w_in, 16)
                sp.dma_start(cos[:, :], a["cos"]).then_inc(c_in, 16)
                sp.dma_start(sin[:, :], a["sin"]).then_inc(c_in, 16)
                sp.dma_start(bqk[:, :], a["b_qk"]).then_inc(c_in, 16)
                sp.dma_start(bv[:, :, :], a["b_v"]).then_inc(c_in, 16)

                def head(n, s):
                    if has(n, 3):
                        ge(sp, w_split, 2 * (n + 3))
                        sp.dma_start(w32[:, :], a["w_heads"][n + 3]).then_inc(w_in, 16)

                def turn(n, s, qc):
                    if has(n, 2):
                        g, to = 4 * (n + 2) + qc, (s + 2) % SETS
                        ge_both(sp, qk_ready, g + 1, t2_done, g)
                        for q in range(4):
                            o, i = 32 * q, 32 * (q ^ 1)
                            sp.dma_start(qks[o:o + 32, :], qk[i:i + 32, :]).then_inc(swapped, 16)
                        ge(sp, spread, SPREAD * g)
                        ge(sp, hi_done, g + 1)
                        ge(sp, lo_done, g + 1)
                        c = cols(qc, CH)
                        for dst, src in ((qh[0:HD, to, c], hi[0:HD, :]), (qh[HD:P, to, c], hi[0:HD, :]),
                                         (ks[0:HD, to, c], hi[HD:P, :]), (ks[HD:P, to, c], lo[HD:P, :]),
                                         (k1[0:HD, to, c], hi[HD:P, :]), (ql[0:HD, to, c], lo[0:HD, :])):
                            sp.dma_start(dst, src).then_inc(spread, 16)
                run_heads(sp, head, turn)

            @block.gpsimd
            def _(pool):
                pool.memset(vh[:, :, :, HD:VW], 1.0).then_inc(v_ones, 1)
                pool.wait_ge(v_ones, 1)
                pool.memset(k1[HD:HD + 1, :, :], 1.0).then_inc(consts, 1)

                def head(n, s):
                    pass

                def turn(n, s, qc):
                    for kt in range(KT):
                        if has(n, 0) and kt in LO_POOL:
                            ge(pool, hi_act, done(HI_ACT, 4 * n + qc, kt))
                            pool.tensor_tensor(pl[:, kt % RW, :], pb[:, kt % RP, :], ph[:, kt % RW, :],
                                               ALU.subtract).then_inc(lo_pool, 1)
                        if has(n, 2):
                            g = 4 * (n + 2) + qc
                            if kt == 9:
                                ge_both(pool, t1_done, g + 1, t2_done, g + 1)
                                pool.tensor_tensor(r[:, :], t1[:, :], t2[:, :], ALU.add).then_inc(r_ready, 1)
                            if kt == 14:
                                ge_both(pool, hi_done, g + 1, spread, SPREAD * g)
                                pool.tensor_tensor(lo[:, :], r[:, :], hi[:, :], ALU.subtract).then_inc(lo_done, 1)
                            if kt == 12:
                                ge(pool, vh_done, g + 1)
                                pool.tensor_tensor(vl[:, (s + 2) % SETS, cols(qc, TPC), :], v32[:, :, :],
                                                   vh[:, (s + 2) % SETS, cols(qc, TPC), 0:HD],
                                                   ALU.subtract).then_inc(v_done, 1)
                run_heads(pool, head, turn)

            @block.tensor
            def _(pe):
                for c in range(NCH):
                    if c >= 2:
                        pe.wait_ge(xl_ready, c - 1)
                    for t in range(TPC):
                        mm = pe.transpose(p_m[:, c % 2, t * P:(t + 1) * P], x_sb[:, c * TPC + t, :], ident[:, :])
                    mm.then_inc(x_turned, 1)
                pe.wait_ge(xl_ready, NCH)
                pe.wait_ge(consts, 2)

                def head(n, s):
                    pass

                def maxima(n, s, qc, m):
                    g, st = 4 * (n + 1) + qc, (s + 1) % SETS
                    kc, t = divmod(m, TPC)
                    if m == (NCH - 1) * TPC:
                        ge(pe, spread, SPREAD * 4 * (n + 2))
                    if m >= 2 or found_max(n, qc):
                        ge(pe, maxed, 16 * g + m - 1)
                    pe.matmul(p_m[:, m % 2, :], qh[:, st, cols(qc * TPC + t, P)],
                              ks[:, st, kc * CH:(kc + 1) * CH], start=True, stop=True).then_inc(m_ready, 1)

                def scores(n, s, qc, kt):
                    if kt >= 2 or foldone(n, qc):
                        e, by = 4 * n + qc, (kt - 2) % KT
                        if by in HI_DVE:
                            ge(pe, exp_done, done(HI_DVE, e, kt - 2))
                        else:
                            ge(pe, hi_act, done(HI_ACT, e, kt - 2))
                    pe.matmul(p_s[:, kt % 2, :], ks[:, s, kt * P:(kt + 1) * P], qh[:, s, cols(qc, CH)],
                              start=True, stop=False)
                    pe.matmul(p_s[:, kt % 2, :], k1[0:HD + 1, s, kt * P:(kt + 1) * P], ql[0:HD + 1, s, cols(qc, CH)],
                              start=False, stop=True).then_inc(s_ready, 1)

                def weigh(n, s, qc, kt):
                    e = 4 * n + qc
                    if kt == 0:
                        ge(pe, o_free, e + 1)
                    if kt in LO_DVE:
                        ge(pe, lo_dve, done(LO_DVE, e, kt))
                    else:
                        ge(pe, lo_pool, done(LO_POOL, e, kt))
                    for i in range(TPC):
                        o = p_o[:, i * VW:(i + 1) * VW]
                        hi_i = ph[:, kt % RW, i * P:(i + 1) * P]
                        lo_i = pl[:, kt % RW, i * P:(i + 1) * P]
                        pe.matmul(o, hi_i, vh[:, s, kt, :], start=(kt == 0 and i == 0), stop=False,
                                  skip_group_check=True)
                        pe.matmul(o[:, 0:HD], hi_i, vl[:, s, kt, :], start=False, stop=False, skip_group_check=True)
                        mm = pe.matmul(o, lo_i, vh[:, s, kt, :], start=False, stop=(kt == KT - 1),
                                       skip_group_check=True)
                    if kt == KT - 1:
                        mm.then_inc(o_ready, 1)

                def turn(n, s, qc):
                    m = 0
                    if has(n, 1):
                        ge(pe, spread, SPREAD * (4 * (n + 1) + NCH - 1))
                    if has(n, 0):
                        ge(pe, mrow_ready, 4 * n + qc + 1)
                        ge(pe, v_done, 4 * (n + 1))
                    for kt in range(KT):
                        if has(n, 0):
                            scores(n, s, qc, kt)
                        if has(n, 1):
                            for _ in range(MAX_SLOTS[kt]):
                                maxima(n, s, qc, m)
                                m += 1
                        if has(n, 2):
                            g = 4 * (n + 2) + qc
                            if kt == 1:
                                ge(pe, w_split, 2 * (n + 3))
                                ge_both(pe, qk_ready, g, mrow_ready, max(g - 5, 0) if isinstance(g, int) else g - 5)
                                c = cols(qc, CH)
                                pe.matmul(p_a[:, :], wh[:, 0:P], xh[:, c], start=True, stop=False)
                                pe.matmul(p_a[:, :], wl[:, 0:P], xh[:, c], start=False, stop=False)
                                pe.matmul(p_a[:, :], wh[:, 0:P], xl[:, c], start=False,
                                          stop=True).then_inc(proj_ready, 1)
                            if 6 <= kt < 6 + TPC:
                                if kt == 6:
                                    ge(pe, v_biased, g)
                                t = kt - 6
                                c = cols(qc * TPC + t, P)
                                o = p_v[:, t * HD:(t + 1) * HD]
                                pe.matmul(o, xh[:, c], wh[:, P:], start=True, stop=False)
                                pe.matmul(o, xh[:, c], wl[:, P:], start=False, stop=False)
                                mm = pe.matmul(o, xl[:, c], wh[:, P:], start=False, stop=True)
                                if t == TPC - 1:
                                    mm.then_inc(v_ready, 1)
                        if kt == 5 and found_max(n, qc):
                            e = 4 * n + qc + 3
                            ge(pe, m_done, e + 1)
                            if has(n, 2):
                                ge(pe, qk_ready, e + 6)
                            else:
                                ge(pe, mrow_ready, e)
                            for t in range(TPC):
                                mm = pe.matmul(p_t[HD:HD + 1, t * P:(t + 1) * P], negm[:, t:t + 1], identh[:, :],
                                               start=True, stop=True)
                            mm.then_inc(m_turned, 1)
                        if foldone(n, qc):
                            for late in TAIL.get(kt, ()):
                                weigh(*before(n, s, qc), late)
                        if has(n, 0) and kt >= LAG:
                            weigh(n, s, qc, kt - LAG)
                run_heads(pe, head, turn)
                for late in range(KT - LAG, KT):
                    weigh(LAST, LAST % SETS, QC - 1, late)

            @block.scalar
            def _(act):
                for c in range(NCH):
                    act.wait_ge(x_turned, c + 1)
                    act.activation(xh[:, c * CH:(c + 1) * CH], p_m[:, c % 2, :], ACT.Copy).then_inc(xh_ready, 1)
                act.wait_ge(c_in, 64)
                act.wait_ge(consts, 2)

                def head(n, s):
                    pass

                def turn(n, s, qc):
                    for kt in range(KT):
                        if has(n, 0):
                            ge(act, s_ready, 16 * (4 * n + qc) + kt + 1)
                            e, by = 4 * n + qc, (kt - RP) % KT
                            if by in LO_DVE:
                                ge(act, lo_dve, done(LO_DVE, e, kt - RP))
                            else:
                                ge(act, lo_pool, done(LO_POOL, e, kt - RP))
                            exp = act.activation(pb[:, kt % RP, :], p_s[:, kt % 2, :], ACT.Exp, scale=HD ** -0.5)
                            if kt in HI_DVE:
                                exp.then_inc(exp_done, 1)
                            else:
                                act.activation(ph[:, kt % RW, :], p_s[:, kt % 2, :], ACT.Exp,
                                               scale=HD ** -0.5).then_inc(hi_act, 1)
                        if has(n, 2) and kt == 2:
                            g = 4 * (n + 2) + qc
                            ge(act, proj_ready, g + 1)
                            ge(act, t1_done, g)
                            ge(act, swapped, 64 * g, alone=consts)
                            act.activation(qk[:, :], p_a[:, :], ACT.Identity,
                                           bias=bqk[:, cols(n + 2, 1)]).then_inc(qk_ready, 1)
                        if kt == 6 and found_max(n, qc):
                            ps, pq = before(n, s, qc)[1:]
                            ge(act, m_turned, 4 * n + qc + 4)
                            act.activation(ql[HD:HD + 1, (ps + 1) % SETS, cols(pq, CH)], p_t[HD:HD + 1, :],
                                           ACT.Copy, bias=EXP_SHIFT).then_inc(mrow_ready, 1)
                run_heads(act, head, turn)

            @block.vector
            def _(dve):
                for c in range(NCH):
                    cs = slice(c * CH, (c + 1) * CH)
                    dve.wait_ge(xh_ready, c + 1)
                    dve.tensor_tensor(xl[:, cs], p_m[:, c % 2, :], xh[:, cs], ALU.subtract).then_inc(xl_ready, 1)
                dve.tensor_copy(identh[:, :], ident[:, :]).then_inc(consts, 1)
                dve.memset(part[:, :, :], 0.0).then_inc(o_free, 1)
                dve.wait_ge(o_free, 1)
                dve.wait_ge(c_in, 64)
                dve.wait_ge(consts, 2)

                def head(n, s):
                    if has(n, 2):
                        ge(dve, w_in, 16 * (n + 3))
                        ge(dve, v_ready, 4 * (n + 2))
                        dve.tensor_copy(wh[:, :], w32[:, :]).then_inc(w_split, 1)
                        ge(dve, w_split, 2 * (n + 2) + 1)
                        dve.tensor_tensor(wl[:, :], w32[:, :], wh[:, :], ALU.subtract).then_inc(w_split, 1)

                def normalise(n, s, qc):
                    e = 4 * n + qc
                    ge(dve, o_ready, e + 1)
                    o = p_o[:, 0:TPC * VW].rearrange("p (t w) -> p t w", w=VW)
                    dve.reciprocal(rcp[:, :], o[:, :, HD]).then_inc(rcp_done, 1)
                    ge(dve, rcp_done, e + 1)
                    dve.tensor_tensor(attn[:, cols(qc, TPC), cols(n, HD)], o[:, :, 0:HD],
                                      rcp[:, :].unsqueeze(2).to_broadcast([P, TPC, HD]),
                                      ALU.mult).then_inc(o_free, 1)

                def turn(n, s, qc):
                    m = 0
                    for kt in range(KT):
                        if kt == LAG - 1 and foldone(n, qc):
                            normalise(*before(n, s, qc))
                        if has(n, 1):
                            g = 4 * (n + 1) + qc
                            for _ in range(MAX_SLOTS[kt]):
                                if m == 0:
                                    ge(dve, m_done, g)
                                ge(dve, m_ready, 16 * g + m + 1)
                                dve.tensor_reduce(part[:, m % TPC, m // TPC:m // TPC + 1], p_m[:, m % 2, :], AX,
                                                  ALU.max).then_inc(maxed, 1)
                                m += 1
                            if kt == 14:
                                ge(dve, maxed, 16 * (g + 1))
                                ge(dve, m_turned, g)
                                dve.tensor_reduce(negm[:, :], part[:, :, :], AX, ALU.max,
                                                  negate=True).then_inc(m_done, 1)
                        if has(n, 0) and kt - 1 in LO_DVE:
                            j, e = kt - 1, 4 * n + qc
                            if j in HI_DVE:
                                ge(dve, exp_done, done(HI_DVE, e, j))
                                dve.tensor_copy(ph[:, j % RW, :], pb[:, j % RP, :]).then_inc(hi_dve, 1)
                                ge(dve, hi_dve, done(HI_DVE, e, j))
                            else:
                                ge(dve, hi_act, done(HI_ACT, e, j))
                            dve.tensor_tensor(pl[:, j % RW, :], pb[:, j % RP, :], ph[:, j % RW, :],
                                              ALU.subtract).then_inc(lo_dve, 1)
                        if has(n, 2):
                            g, to = 4 * (n + 2) + qc, (s + 2) % SETS
                            c = cols(qc, CH)
                            if kt == 3:
                                ge(dve, qk_ready, g + 1)
                                ge(dve, r_ready, g)
                                dve.tensor_tensor(t1[:, :], qk[:, :], cos[:, c], ALU.mult).then_inc(t1_done, 1)
                            if kt == 8:
                                ge(dve, swapped, 64 * (g + 1))
                                ge(dve, lo_done, g)
                                dve.tensor_tensor(t2[:, :], qks[:, :], sin[:, c], ALU.mult).then_inc(t2_done, 1)
                            if kt == 13:
                                ge_both(dve, r_ready, g + 1, spread, SPREAD * g)
                                dve.tensor_copy(hi[:, :], r[:, :]).then_inc(hi_done, 1)
                            if kt == 10:
                                ge(dve, v_ready, g + 1)
                                ge(dve, v_done, g)
                                src = p_v[:, 0:TPC * HD].rearrange("p (t d) -> p t d", d=HD)
                                dve.tensor_tensor(v32[:, :, :], src, bv[:, cols(n + 2, 1), :].to_broadcast(
                                    [P, TPC, HD]), ALU.add).then_inc(v_biased, 1)
                            if kt == 11:
                                ge(dve, v_biased, g + 1)
                                dve.tensor_copy(vh[:, to, cols(qc, TPC), 0:HD], v32[:, :, :]).then_inc(vh_done, 1)
                run_heads(dve, head, turn)
                normalise(LAST, LAST % SETS, QC - 1)


def mha_out(nc, x_sb, ident, a, ln, attn):
    IC = HEADS * HD // P
    with Scope(nc, "ao_") as sc:
        wo = sc.sb("wo", [P, IC, D])
        bo = sc.sb("bo", [P, 1, D])
        xb = sc.sb("x_plus_bias", [P, NT, D])
        aT = sc.sb("attnT", [P, 2, IC, P])
        rows = sc.sb("rows", [P, NT, D])
        p_t = sc.ps("p_t", [P, 2, 2, CH])
        p_y = sc.ps("p_y", [P, 2, CH])
        w_in, biased, turned, copied_a, copied_b, y_ready, rows_ready = (
            sc.sem(n) for n in ("w_in", "biased", "turned", "copied_a", "copied_b", "y_ready", "rows_ready"))
        with nc.Block() as block:

            @block.sync
            def _(sp):
                sp.dma_start(wo[:, :, :], a["wo_a"].rearrange("(c p) d -> p c d", p=P)).then_inc(w_in, 16)
                sp.dma_start(bo[:, :, :], a["b_o"]).then_inc(w_in, 16)

            @block.tensor
            def _(pe):
                def turn(t):
                    if t >= 2:
                        pe.wait_ge(copied_a, t - 1)
                        pe.wait_ge(copied_b, t - 1)
                    for c in range(IC):
                        mm = pe.transpose(p_t[:, t % 2, c // 4, (c % 4) * P:(c % 4 + 1) * P],
                                          attn[:, t, c * P:(c + 1) * P], ident[:, :])
                    mm.then_inc(turned, 1)

                turn(0)
                pe.wait_ge(w_in, 32)
                for t in range(NT):
                    if t + 1 < NT:
                        turn(t + 1)
                    pe.wait_ge(copied_a, t + 1)
                    pe.wait_ge(copied_b, t + 1)
                    if t >= 2:
                        pe.wait_ge(rows_ready, t - 1)
                    for c in range(IC):
                        mm = pe.matmul(p_y[:, t % 2, 0:D], aT[:, t % 2, c, :], wo[:, c, :], start=(c == 0),
                                       stop=(c == IC - 1))
                    mm.then_inc(y_ready, 1)

            @block.scalar
            def _(act):
                for t in range(NT):
                    act.wait_ge(turned, t + 1)
                    if t >= 2:
                        act.wait_ge(y_ready, t - 1)
                    act.activation(aT[:, t % 2, 0:4, :], p_t[:, t % 2, 0, :].rearrange("p (c t) -> p c t", t=P),
                                   ACT.Copy).then_inc(copied_a, 1)

            @block.vector
            def _(dve):
                dve.wait_ge(w_in, 32)
                dve.tensor_tensor(xb[:, :, :], x_sb[:, :, :], bo[:, :, :].to_broadcast([P, NT, D]),
                                  ALU.add).then_inc(biased, 1)
                dve.wait_ge(biased, 1)
                for t in range(NT):
                    dve.wait_ge(turned, t + 1)
                    if t >= 2:
                        dve.wait_ge(y_ready, t - 1)
                    dve.tensor_copy(aT[:, t % 2, 4:8, :],
                                    p_t[:, t % 2, 1, :].rearrange("p (c t) -> p c t", t=P)).then_inc(copied_b, 1)
                    if t >= 1:
                        dve.wait_ge(y_ready, t)
                        dve.tensor_tensor(rows[:, t - 1, :], p_y[:, (t - 1) % 2, 0:D], xb[:, t - 1, :],
                                          ALU.add).then_inc(rows_ready, 1)
                dve.wait_ge(y_ready, NT)
                dve.tensor_tensor(rows[:, NT - 1, :], p_y[:, (NT - 1) % 2, 0:D], xb[:, NT - 1, :],
                                  ALU.add).then_inc(rows_ready, 1)
        layernorm_block(nc, ln, "aln_", rows, x_sb)


DEPTH = 2
HEADS_B, DH, WINDOW = 8, 64, 64
INNER = HEADS_B * DH
HALF = DH // 2
PAIRS = HEADS_B // 2
KEYS = WINDOW + P
GRP = 4
STAGES = 4
BF16 = mybir.dt.bfloat16


def run_steps(eng, step):
    for j in range(2 * STAGES):
        step(j, j % 4)
    with eng.Fori(0, (NT - 2 * STAGES) // 4) as turn:
        for u in range(4):
            step(turn * 4 + (2 * STAGES + u), u)
    for j in range(NT, NT + STAGES):
        step(j, j % 4)


def live(j, lag):
    return not isinstance(j, int) or 0 <= j - lag < NT


def phase_local(nc, x_sb, ident, a, ln):
    with Scope(nc, "b_") as sc:
        x0 = sc.sb("x_in", [P, NT, D])
        h_tok = sc.sb("h_tok", [P, NT + 1, D])
        with Scope(nc, "bi_") as si:
            kept = si.sem("kept")
            with nc.Block() as block:
                @block.vector
                def _(dve):
                    dve.tensor_copy(x0[:, :, :], x_sb[:, :, :]).then_inc(kept, 1)
                    dve.memset(h_tok[:, NT, :], 0.0)
                    dve.memset(h_tok[0:1, 0, D // 2:], 0.0)
        for l in range(DEPTH):
            shift_block(nc, f"bs{l}_", x_sb, h_tok)
            local_attention(nc, l, x_sb, h_tok, ident, a)
            shift_block(nc, f"bt{l}_", x_sb, h_tok)
            layernorm_block(nc, ln, f"bl{l}_", h_tok, h_tok)
            geglu(nc, l, x_sb, h_tok, ident, a)
            clear_semaphores(nc)
        with Scope(nc, "br_") as si:
            rows = si.sb("rows", [P, NT, D])
            with nc.Block() as block:
                @block.vector
                def _(dve):
                    dve.tensor_tensor(rows[:, :, :], x_sb[:, :, :], x0[:, :, :], ALU.add)
            layernorm_block(nc, ln, "bln_", rows, x_sb)


def shift_block(nc, name, x_sb, h_tok):
    H = D // 2
    with Scope(nc, name) as sc:
        shifted = sc.sem("shifted")
        first_zeroed = sc.sem("first_zeroed")
        with nc.Block() as block:
            @block.sync
            def _(sp):
                sp.dma_start(h_tok[1:P, 0:NT, H:], x_sb[0:P - 1, :, H:]).then_inc(shifted, 16)
                sp.dma_start(h_tok[0:1, 1:NT, H:], x_sb[P - 1:P, 0:NT - 1, H:]).then_inc(shifted, 16)
                sp.wait_ge(shifted, 32)

            @block.vector
            def _(dve):
                dve.tensor_copy(h_tok[:, 0:NT, 0:H], x_sb[:, :, 0:H])
                dve.memset(h_tok[0:1, 0, H:], 0.0).then_inc(first_zeroed, 1)


def local_attention(nc, l, x_sb, h_tok, ident, a):
    with Scope(nc, f"ba{l}_") as sc:
        wqkv = sc.sb("wqkv", [P, 3 * INNER])
        wo = sc.sb("wo", [P, PAIRS, D])
        raw_tab = sc.sb("rot_const", [P, 2, NT, 2, DH])
        tab = sc.sb("rot", [P, 2, NT, 2, DH])
        scl = sc.sb("qk_scale", [P, 2, 2, DH])
        mask_f = sc.sb("mask_f32", [P, 2, 2 * KEYS])
        mask = sc.sb("mask", [P, 2, 2 * KEYS], BF16)
        identb = sc.sb("ident_bf16", [P, P], BF16)
        half_neg = sc.sb("minus_half", [P, 2 * HEADS_B])
        hs = sc.sb("h_tile", [P, 2, P])
        hT = sc.sb("hT", [P, 2, KEYS])
        sq = sc.sb("sq", [P, 2 * INNER])
        ssq = sc.sb("ssq", [P, 2, 2 * HEADS_B])
        ssc = sc.sb("ssq_clamped", [P, 2, 2 * HEADS_B])
        rinv = sc.sb("rnorm", [P, 2, 2 * HEADS_B])
        t1 = sc.sb("rot_cos", [P, 2, 2 * INNER])
        t2 = sc.sb("rot_sin", [P, 2, 2 * INNER])
        t3 = sc.sb("rot_sum", [P, 2 * INNER])
        qk = sc.sb("qk", [P, 2, 2 * INNER])
        qT = sc.sb("qT", [P, 2, PAIRS, P])
        kT = sc.sb("kT", [P, 2, PAIRS, KEYS])
        va = sc.sb("v_a", [P, 4, INNER])
        vb = sc.sb("v_b", [WINDOW, 4, INNER])
        negmax = sc.sb("negmax", [P, 2, HEADS_B])
        pr = sc.sb("probs", [P, 2, HEADS_B, KEYS])
        rsum = sc.sb("rsum", [P, 2, HEADS_B])
        rcp = sc.sb("rcp", [P, 2, HEADS_B])
        pta = sc.sb("probsT_a", [P, HEADS_B, P])
        ptb = sc.sb("probsT_b", [WINDOW, HEADS_B, P])
        at = sc.sb("attn", [P, 2, INNER])
        atT = sc.sb("attnT", [P, PAIRS, P])

        p_v = sc.ps("p_v", [P, CH])
        p_q = sc.ps("p_q", [P, CH])
        p_k = sc.ps("p_k", [P, CH])
        p_s = sc.ps("p_s", [P, 2, CH])
        p_p = sc.ps("p_p", [P, CH])
        p_o = sc.ps("p_o", [P, CH])
        p_x = sc.ps("p_x", [P, CH])
        (c_in, tab_ready, mask_ready, hs_ready, hT_turned, hT_carry, hT_ready, qk_ready, squared, t_done, ssq_done,
         t3_done, clamped, rinv_done, roped, q_turned, k_turned, qT_ready, kT_ready, kT_carry, va_ready, va_done,
         vb_ready, vb_done, s_ready, max_done, exp_done, pt_turned, pt_done, o_ready, rcp_done, at_ready, at_turned,
         atT_ready, y_ready, x_updated) = (sc.sem(n) for n in (
             "c_in", "tab_ready", "mask_ready", "hs_ready", "hT_turned", "hT_carry", "hT_ready", "qk_ready",
             "squared", "t_done", "ssq_done", "t3_done", "clamped", "rinv_done", "roped", "q_turned", "k_turned",
             "qT_ready", "kT_ready", "kT_carry", "va_ready", "va_done", "vb_ready", "vb_done", "s_ready",
             "max_done", "exp_done", "pt_turned", "pt_done", "o_ready", "rcp_done", "at_ready", "at_turned",
             "atT_ready", "y_ready", "x_updated"))
        qk5 = lambda t: t.rearrange("p (s h d) -> p s h d", s=2, d=DH)

        with nc.Block() as block:

            @block.sync
            def _(sp):
                sp.dma_start(raw_tab[:, :, :, :, :], a["rot"]).then_inc(c_in, 16)
                sp.dma_start(scl[:, :, :, :], a["qk_scale"][:, l]).then_inc(c_in, 16)
                sp.dma_start(mask_f[:, :, :], a["mask"]).then_inc(c_in, 16)
                sp.dma_start(wqkv[:, :], a["wqkv"][l]).then_inc(c_in, 16)
                sp.dma_start(wo[:, :, :], a["wo_b"][l].rearrange("(c p) d -> p c d", p=P)).then_inc(c_in, 16)

            @block.gpsimd
            def _(pool):
                def stage(j, u):
                    ge(pool, hT_turned, j - 1, alone=tab_ready)
                    pool.tensor_copy(hs[:, u % 2, :], h_tok[:, j, :]).then_inc(hs_ready, 1)

                def hT_head(j, u):
                    ge(pool, hT_ready, j, alone=tab_ready)
                    ge(pool, vb_ready, j - 1, alone=tab_ready)
                    pool.tensor_copy(hT[:, u % 2, 0:WINDOW], hT[:, (u + 1) % 2, P:KEYS]).then_inc(hT_carry, 1)

                def kT_head(t, u):
                    ge(pool, kT_ready, t, alone=tab_ready)
                    ge(pool, s_ready, 2 * (t - 1), alone=tab_ready)
                    pool.tensor_copy(kT[:, u % 2, :, 0:WINDOW],
                                     kT[:, (u + 1) % 2, :, P:KEYS]).then_inc(kT_carry, 1)

                pool.memset(half_neg[:, :], -0.5).then_inc(tab_ready, 1)
                pool.memset(hT[:, 0, 0:WINDOW], 0.0).then_inc(hT_carry, 1)
                pool.memset(kT[:, 0, :, 0:WINDOW], 0.0).then_inc(kT_carry, 1)
                stage(0, 0)

                def step(j, u):
                    if live(j, 0):
                        stage(j + 1, u + 1)
                    if live(j, 1) and not (isinstance(j, int) and j == 1):
                        kT_head(j - 1, u - 1)
                    if live(j, 0):
                        hT_head(j + 1, u + 1)
                        ge(pool, t_done, 3 * (j + 1))
                        ge(pool, roped, j)
                        pool.tensor_tensor(t3[:, :], t1[:, u % 2, :], t2[:, u % 2, :], ALU.add).then_inc(t3_done, 1)
                        ge(pool, ssq_done, j + 1, alone=tab_ready)
                        pool.tensor_scalar(ssc[:, u % 2, :], ssq[:, u % 2, :], 1e-24, None,
                                           ALU.max).then_inc(clamped, 1)
                        ge(pool, clamped, j + 1)
                        pool.tensor_tensor(rinv[:, u % 2, :], ssc[:, u % 2, :], half_neg[:, :],
                                           ALU.pow).then_inc(rinv_done, 1)
                        ge(pool, rinv_done, j + 1)
                        ge(pool, t3_done, j + 1)
                        ge(pool, k_turned, j - 1)
                        pool.tensor_tensor(qk[:, u % 2, :].rearrange("p (g d) -> p g d", d=DH),
                                           t3[:, :].rearrange("p (g d) -> p g d", d=DH),
                                           rinv[:, u % 2, :].unsqueeze(2).to_broadcast([P, 2 * HEADS_B, DH]),
                                           ALU.mult).then_inc(roped, 1)
                run_steps(pool, step)

            @block.tensor
            def _(pe):
                pe.wait_ge(c_in, 80)
                pe.wait_ge(mask_ready, 2)

                def turn_probs(t, u, g, tail):
                    n = 4 * t + 2 * g + tail
                    ge(pe, exp_done, HEADS_B * (t + 1), alone=mask_ready)
                    ge(pe, pt_done, n, alone=mask_ready)
                    for i in range(GRP):
                        h = GRP * g + i
                        src = pr[:, u % 2, h, P:KEYS] if tail else pr[:, u % 2, h, 0:P]
                        mm = pe.transpose(p_p[0:WINDOW if tail else P, i * P:(i + 1) * P], src, ident[:, :])
                    mm.then_inc(pt_turned, 1)

                def scores(t, u, g):
                    ge(pe, qT_ready, t + 1)
                    ge(pe, kT_ready, t + 1)
                    ge(pe, kT_carry, t + 1)
                    ge(pe, exp_done, HEADS_B * t + GRP * g)
                    for b in range(2):
                        pe.matmul(p_s[:, b, 0:2 * KEYS], identb[:, :],
                                  mask[:, 0 if isinstance(t, int) and t == 0 else 1, :], start=True, stop=False,
                                  skip_group_check=True)
                    for i in range(GRP):
                        h = GRP * g + i
                        rows = slice(DH * (h % 2), DH * (h % 2) + DH)
                        mm = pe.matmul(p_s[:, i % 2, (i // 2) * KEYS:(i // 2 + 1) * KEYS], qT[rows, u % 2, h // 2, :],
                                       kT[rows, u % 2, h // 2, :], start=False, stop=True, skip_group_check=True)
                    mm.then_inc(s_ready, 1)

                def step(j, u):
                    if live(j, 0):
                        ge(pe, hs_ready, j + 1)
                        ge(pe, vb_done, j)
                        pe.transpose(p_v[:, 0:P], hs[:, u % 2, :], ident[:, :]).then_inc(hT_turned, 1)
                    if live(j, 1):
                        t, v = j - 1, u - 1
                        ge(pe, roped, t + 1)
                        for s, (bank, turned) in enumerate(((p_q, q_turned), (p_k, k_turned))):
                            for c in range(PAIRS):
                                col = s * INNER + c * P
                                mm = pe.transpose(bank[:, c * P:(c + 1) * P], qk[:, v % 2, col:col + P], ident[:, :])
                            mm.then_inc(turned, 1)
                    if live(j, 3):
                        turn_probs(j - 3, u - 3, 0, 0)
                    if live(j, 2):
                        scores(j - 2, u - 2, 0)
                    if live(j, 4):
                        t = j - 4
                        ge(pe, at_ready, t + 1)
                        ge(pe, x_updated, t)
                        for c in range(PAIRS):
                            mm = pe.transpose(p_x[:, c * P:(c + 1) * P], at[:, u % 2, c * P:(c + 1) * P], ident[:, :])
                        mm.then_inc(at_turned, 1)
                    if live(j, 3):
                        turn_probs(j - 3, u - 3, 0, 1)
                    if live(j, 0):
                        ge(pe, hT_ready, j + 1)
                        ge(pe, qT_ready, j)
                        ge(pe, kT_ready, j)
                        pe.matmul(p_q[:, :], hT[:, u % 2, WINDOW:KEYS], wqkv[:, 0:INNER], start=True, stop=True)
                        pe.matmul(p_k[:, :], hT[:, u % 2, WINDOW:KEYS], wqkv[:, INNER:2 * INNER], start=True,
                                  stop=True).then_inc(qk_ready, 1)
                    if live(j, 3):
                        turn_probs(j - 3, u - 3, 1, 0)
                    if live(j, 4):
                        t = j - 4
                        ge(pe, atT_ready, t + 1)
                        for c in range(PAIRS):
                            mm = pe.matmul(p_x[:, 0:D], atT[:, c, :], wo[:, c, :], start=(c == 0),
                                           stop=(c == PAIRS - 1))
                        mm.then_inc(y_ready, 1)
                    if live(j, 0):
                        ge(pe, hT_carry, j + 1)
                        pe.matmul(p_v[:, :], hT[:, u % 2, 0:P], wqkv[:, 2 * INNER:], start=True,
                                  stop=True).then_inc(va_ready, 1)
                    if live(j, 3):
                        turn_probs(j - 3, u - 3, 1, 1)
                    if live(j, 2):
                        scores(j - 2, u - 2, 1)
                    if live(j, 0):
                        ge(pe, va_done, j + 1)
                        pe.matmul(p_v[0:WINDOW, :], hT[:, u % 2, P:KEYS], wqkv[:, 2 * INNER:], start=True,
                                  stop=True).then_inc(vb_ready, 1)
                    if live(j, 3):
                        t = j - 3
                        ge(pe, pt_done, 4 * (t + 1))
                        ge(pe, vb_done, t + 1)
                        ge(pe, at_ready, t)
                        for h in range(HEADS_B):
                            cs = slice(h * DH, (h + 1) * DH)
                            pe.matmul(p_o[:, cs], pta[:, h, :], va[:, (u - 3) % 4, cs], start=True, stop=False)
                            mm = pe.matmul(p_o[:, cs], ptb[:, h, :], vb[:, (u - 3) % 4, cs], start=False, stop=True)
                        mm.then_inc(o_ready, 1)
                run_steps(pe, step)

            @block.scalar
            def _(act):
                def exps(t, u, g):
                    ge(act, max_done, 2 * t + g + 1)
                    ge(act, pt_turned, 4 * (t - 1))
                    for i in range(GRP):
                        h = GRP * g + i
                        act.activation(pr[:, u % 2, h, :], p_s[:, i % 2, (i // 2) * KEYS:(i // 2 + 1) * KEYS],
                                       ACT.Exp, bias=negmax[:, u % 2, h:h + 1],
                                       accum_out=rsum[:, u % 2, h:h + 1]).then_inc(exp_done, 1)

                def step(j, u):
                    if live(j, 0):
                        ge(act, hT_turned, j + 1)
                        ge(act, vb_ready, j - 1)
                        ge(act, hT_carry, j)
                        act.activation(hT[:, u % 2, WINDOW:KEYS], p_v[:, 0:P], ACT.Copy).then_inc(hT_ready, 1)
                    if live(j, 1):
                        t, v = j - 1, u - 1
                        ge(act, q_turned, t + 1)
                        ge(act, s_ready, 2 * (t - 1))
                        act.activation(qT[:, v % 2, :, :], p_q[:, :].rearrange("p (c t) -> p c t", c=PAIRS),
                                       ACT.Copy).then_inc(qT_ready, 1)
                        ge(act, k_turned, t + 1)
                        ge(act, kT_carry, t)
                        act.activation(kT[:, v % 2, :, WINDOW:KEYS], p_k[:, :].rearrange("p (c t) -> p c t", c=PAIRS),
                                       ACT.Copy).then_inc(kT_ready, 1)
                    if live(j, 2):
                        exps(j - 2, u - 2, 0)
                    if live(j, 4):
                        t = j - 4
                        ge(act, at_turned, t + 1)
                        ge(act, y_ready, t)
                        act.activation(atT[:, :, :], p_x[:, :].rearrange("p (c t) -> p c t", c=PAIRS),
                                       ACT.Copy).then_inc(atT_ready, 1)
                    if live(j, 0):
                        ge(act, qk_ready, j + 1)
                        ge(act, ssq_done, j)
                        act.activation(sq[:, 0:INNER], p_q[:, :], ACT.Square).then_inc(squared, 1)
                        act.activation(sq[:, INNER:], p_k[:, :], ACT.Square).then_inc(squared, 1)
                        ge(act, va_ready, j + 1)
                        ge(act, o_ready, j - 3)
                        act.activation(va[:, u % 4, :], p_v[:, :], ACT.Copy).then_inc(va_done, 1)
                    if live(j, 2):
                        exps(j - 2, u - 2, 1)
                    if live(j, 0):
                        ge(act, vb_ready, j + 1)
                        act.activation(vb[:, u % 4, :], p_v[0:WINDOW, :], ACT.Copy).then_inc(vb_done, 1)
                run_steps(act, step)

            @block.vector
            def _(dve):
                dve.wait_ge(c_in, 80)
                dve.tensor_copy(identb[:, :], ident[:, :]).then_inc(mask_ready, 1)
                dve.tensor_copy(mask[:, :, :], mask_f[:, :, :]).then_inc(mask_ready, 1)
                for s in range(2):
                    for r in range(2):
                        dve.tensor_tensor(tab[:, s, :, r, :], raw_tab[:, s, :, r, :],
                                          scl[:, s, r:r + 1, :].to_broadcast([P, NT, DH]),
                                          ALU.mult).then_inc(tab_ready, 1)
                dve.wait_ge(tab_ready, 5)

                def copy_probs(t, u, g, tail):
                    n = 4 * t + 2 * g + tail
                    ge(dve, pt_turned, n + 1)
                    ge(dve, o_ready, t)
                    rows = WINDOW if tail else P
                    dst = ptb if tail else pta
                    dve.tensor_copy(dst[:, GRP * g:GRP * g + GRP, :],
                                    p_p[0:rows, :].rearrange("p (h t) -> p h t", h=GRP)).then_inc(pt_done, 1)

                def maxes(t, u, g):
                    ge(dve, s_ready, 2 * t + g + 1)
                    ge(dve, exp_done, HEADS_B * (t - 1))
                    src = p_s[:, :, 0:2 * KEYS].rearrange("p b (i k) -> p b i k", i=2)
                    dve.tensor_reduce(negmax[:, u % 2, GRP * g:GRP * g + GRP].rearrange("p (b i) -> p b i", i=2),
                                      src, AX, ALU.max, negate=True).then_inc(max_done, 1)

                def rot(j, u, part):
                    for s, bank in ((0, p_q), (1, p_k)):
                        x3 = bank[:, :].rearrange("p (h d) -> p h d", d=DH)
                        tb = tab[:, 0 if part == 0 else 1, j, s, :]
                        if part == 0:
                            o, i, w = slice(0, DH), slice(0, DH), DH
                        else:
                            o = slice(0, HALF) if part == 1 else slice(HALF, DH)
                            i = slice(HALF, DH) if part == 1 else slice(0, HALF)
                            w = HALF
                        dst = (t1 if part == 0 else t2)[:, u % 2, s * INNER:(s + 1) * INNER].rearrange(
                            "p (h d) -> p h d", d=DH)
                        ins = dve.tensor_tensor(dst[:, :, o], x3[:, :, i],
                                                tb[:, o].unsqueeze(1).to_broadcast([P, HEADS_B, w]), ALU.mult)
                    ins.then_inc(t_done, 1)

                def step(j, u):
                    if live(j, 4):
                        t = j - 4
                        ge(dve, o_ready, t + 1)
                        dve.reciprocal(rcp[:, u % 2, :], rsum[:, u % 2, :]).then_inc(rcp_done, 1)
                        ge(dve, rcp_done, t + 1)
                        ge(dve, at_turned, t)
                        dve.tensor_tensor(at[:, u % 2, :].rearrange("p (h d) -> p h d", d=DH),
                                          p_o[:, :].rearrange("p (h d) -> p h d", d=DH),
                                          rcp[:, u % 2, :].unsqueeze(2).to_broadcast([P, HEADS_B, DH]),
                                          ALU.mult).then_inc(at_ready, 1)
                    if live(j, 3):
                        copy_probs(j - 3, u - 3, 0, 0)
                    if live(j, 2):
                        maxes(j - 2, u - 2, 0)
                    if live(j, 3):
                        copy_probs(j - 3, u - 3, 0, 1)
                        copy_probs(j - 3, u - 3, 1, 0)
                    if live(j, 0):
                        ge(dve, squared, 2 * (j + 1))
                        ge(dve, t3_done, j - 1)
                        rot(j, u, 0)
                    if live(j, 3):
                        copy_probs(j - 3, u - 3, 1, 1)
                    if live(j, 0):
                        rot(j, u, 1)
                        rot(j, u, 2)
                    if live(j, 2):
                        maxes(j - 2, u - 2, 1)
                    if live(j, 4):
                        t = j - 4
                        ge(dve, y_ready, t + 1)
                        dve.tensor_tensor(x_sb[:, t, :], p_x[:, 0:D], x_sb[:, t, :], ALU.add).then_inc(x_updated, 1)
                    if live(j, 0):
                        ge(dve, clamped, j - 1)
                        dve.tensor_reduce(ssq[:, u % 2, :], sq[:, :].rearrange("p (g d) -> p g d", d=DH), AX,
                                          ALU.add).then_inc(ssq_done, 1)
                run_steps(dve, step)


def geglu(nc, l, x_sb, h_tok, ident, a):
    HID = a["w2"].shape[1]
    chunks = [(k, min(P, HID - k)) for k in range(0, HID, P)]
    HC = len(chunks)
    STEPS = NCH * HC
    with Scope(nc, f"bg{l}_") as sc:
        w1 = sc.sb("w1", [P, 2 * HID])
        w2 = sc.sb("w2", [P, HC, D])
        b1 = sc.sb("b1", [P, 2, HC])
        b2 = sc.sb("b2", [1, D])
        ones = sc.sb("ones", [1, P])
        gb = sc.sb("ln_gb", [P, 2])
        hT = sc.sb("hT", [P, S])
        ge_act = sc.sb("gelu", [P, 2, CH])
        uT = sc.sb("uT", [P, 2, HC, CH])
        p_a = sc.ps("p_a", [P, 2, CH])
        p_g = sc.ps("p_g", [P, 2, CH])
        p_y = sc.ps("p_y", [P, 2, CH])
        p_x = sc.ps("p_x", [P, 2, CH])
        w_in, ones_set, turned, hT_ready, ag_ready, gelu_done, hidden, y_ready, x_updated = (
            sc.sem(n) for n in ("w_in", "ones_set", "turned", "hT_ready", "ag_ready", "gelu_done", "hidden",
                                "y_ready", "x_updated"))
        with nc.Block() as block:

            @block.sync
            def _(sp):
                sp.dma_start(gb[:, :], a["ln_gb"][l]).then_inc(w_in, 16)
                sp.dma_start(w1[:, :], a["w1"][l]).then_inc(w_in, 16)
                sp.dma_start(b1[:, :, :], a["b1"][l]).then_inc(w_in, 16)
                sp.dma_start(b2[:, :], a["b2"][l:l + 1, :]).then_inc(w_in, 16)
                for k, (at, n) in enumerate(chunks):
                    sp.dma_start(w2[0:n, k, :], a["w2"][l, at:at + n, :]).then_inc(w_in, 16)

            @block.tensor
            def _(pe):
                for c in range(NCH):
                    if c >= 2:
                        pe.wait_ge(hT_ready, c - 1)
                    for t in range(TPC):
                        mm = pe.transpose(p_x[:, c % 2, t * P:(t + 1) * P], h_tok[:, c * TPC + t, :], ident[:, :])
                    mm.then_inc(turned, 1)

                def down(c):
                    pe.wait_ge(hidden, HC * (c + 1))
                    if c >= 2:
                        pe.wait_ge(x_updated, c - 1)
                    for t in range(TPC):
                        for k, (at, n) in enumerate(chunks):
                            pe.matmul(p_y[:, c % 2, t * P:(t + 1) * P], uT[0:n, c % 2, k, t * P:(t + 1) * P],
                                      w2[0:n, k, :], start=(k == 0), stop=False)
                        mm = pe.matmul(p_y[:, c % 2, t * P:(t + 1) * P], ones[:, :], b2[:, :], start=False, stop=True)
                    mm.then_inc(y_ready, 1)

                pe.wait_ge(w_in, 16 * (4 + HC))
                pe.wait_ge(ones_set, 1)
                for c in range(NCH):
                    pe.wait_ge(hT_ready, c + 1)
                    for k, (at, n) in enumerate(chunks):
                        m = c * HC + k
                        if m >= 2:
                            pe.wait_ge(hidden, m - 1)
                        pe.matmul(p_g[0:n, m % 2, :], w1[:, HID + at:HID + at + n], hT[:, c * CH:(c + 1) * CH],
                                  start=True, stop=True)
                        pe.matmul(p_a[0:n, m % 2, :], w1[:, at:at + n], hT[:, c * CH:(c + 1) * CH],
                                  start=True, stop=True).then_inc(ag_ready, 1)
                        if c >= 1 and k == 1:
                            down(c - 1)
                down(NCH - 1)

            @block.scalar
            def _(act):
                act.wait_ge(w_in, 16 * (4 + HC))
                for m in range(STEPS):
                    k, (at, n) = m % HC, chunks[m % HC]
                    act.wait_ge(ag_ready, m + 1)
                    if m >= 2:
                        act.wait_ge(hidden, m - 1)
                    act.activation(ge_act[0:n, m % 2, :], p_g[0:n, m % 2, :], ACT.Gelu,
                                   bias=b1[0:n, 1, k:k + 1]).then_inc(gelu_done, 1)

            @block.vector
            def _(dve):
                dve.memset(ones[:, :], 1.0).then_inc(ones_set, 1)
                dve.wait_ge(w_in, 16 * (4 + HC))
                for c in range(NCH):
                    dve.wait_ge(turned, c + 1)
                    dve.tensor_scalar(hT[:, c * CH:(c + 1) * CH], p_x[:, c % 2, :], gb[:, 0:1], gb[:, 1:2],
                                      ALU.mult, ALU.add).then_inc(hT_ready, 1)

                def residual(c):
                    dve.wait_ge(y_ready, c + 1)
                    xs = x_sb[:, c * TPC:(c + 1) * TPC, :]
                    dve.tensor_tensor(xs, p_y[:, c % 2, :].rearrange("p (t d) -> p t d", d=D), xs,
                                      ALU.add).then_inc(x_updated, 1)

                for m in range(STEPS):
                    c, k = divmod(m, HC)
                    n = chunks[k][1]
                    dve.wait_ge(gelu_done, m + 1)
                    if c >= 2:
                        dve.wait_ge(y_ready, c - 1)
                    dve.scalar_tensor_tensor(uT[0:n, c % 2, k, :], p_a[0:n, m % 2, :], b1[0:n, 0, k:k + 1],
                                             ge_act[0:n, m % 2, :], ALU.add, ALU.mult).then_inc(hidden, 1)
                    if c >= 1 and k == 2:
                        residual(c - 1)
                residual(NCH - 1)


MIXES = 5
LR = 32
HEADS_C, QK_C, V_C = 16, 4, 8
HPC = P // (QK_C * V_C)
HCH = HEADS_C // HPC


def phase_rwkv(nc, x_sb, ident, a, ln):
    with Scope(nc, "c_") as sc:
        tw = sc.sb("tanh_w", [a["ww1"].shape[1], S])
        xi = sc.sb("x_mixed", [P, MIXES, S])
        g_sb = sc.sb("g", [P, S])
        g_th = sc.sb("g_tanh", [P, S])
        o_sb = sc.sb("o", [P, S])
        rwkv_mix(nc, x_sb, ident, a, xi, tw, g_sb, g_th)
        rwkv_scan(nc, a, xi, tw, o_sb)
        rwkv_out(nc, x_sb, ident, a, ln, o_sb, g_sb, g_th)


def rwkv_mix(nc, x_sb, ident, a, xi, tw, g_sb, g_th):
    GATE = a["ww1"].shape[1]
    with Scope(nc, "cm_") as sc:
        xTp = sc.sb("xT_padded", [P, S + 1])
        delta = sc.sb("delta", [P, S])
        z = sc.sb("z", [P, 2, CH])
        low_a = sc.sb("low_a", [P, 2, CH])
        low_b = sc.sb("low_b", [LR, 2, CH])
        tmp = sc.sb("tmp", [P, 2, CH])
        wx1 = sc.sb("wx1", [P, MIXES * LR])
        wx2a = sc.sb("wx2a", [P, P])
        wx2b = sc.sb("wx2b", [LR, P])
        ww1 = sc.sb("ww1", [P, GATE])
        wg = sc.sb("wg", [P, D])
        cols = sc.sb("cols", [P, 1 + MIXES])
        p_x = sc.ps("p_x", [P, 2, CH])
        p_la = sc.ps("p_la", [P, CH])
        p_lb = sc.ps("p_lb", [P, CH])
        p_mu = sc.ps("p_mu", [P, 2, CH])
        p_tw = sc.ps("p_tw", [P, CH])
        p_g = sc.ps("p_g", [P, CH])
        (w_in, x_transposed, pad_set, xT_ready, delta_ready, z_ready, low_ready, tanh_low, mu_ready, tmp_ready,
         mixed, tw_ready, tw_done, g_ready, g_done) = (sc.sem(n) for n in (
             "w_in", "x_transposed", "pad_set", "xT_ready", "delta_ready", "z_ready", "low_ready", "tanh_low",
             "mu_ready", "tmp_ready", "mixed", "tw_ready", "tw_done", "g_ready", "g_done"))
        with nc.Block() as block:

            @block.sync
            def _(sp):
                sp.dma_start(cols[:, :], a["mix_cols"]).then_inc(w_in, 16)
                sp.dma_start(wx1[:, :], a["wx1"]).then_inc(w_in, 16)
                sp.dma_start(wx2a[:, :], a["wx2_t"][0:P, :]).then_inc(w_in, 16)
                sp.dma_start(wx2b[:, :], a["wx2_t"][P:P + LR, :]).then_inc(w_in, 16)
                sp.dma_start(ww1[:, :], a["ww1"]).then_inc(w_in, 16)
                sp.dma_start(wg[:, :], a["wg"]).then_inc(w_in, 16)

            @block.tensor
            def _(pe):
                for c in range(NCH):
                    if c >= 2:
                        pe.wait_ge(xT_ready, c - 1)
                    for t in range(TPC):
                        mm = pe.transpose(p_x[:, c % 2, t * P:(t + 1) * P], x_sb[:, c * TPC + t, :], ident[:, :])
                    mm.then_inc(x_transposed, 1)
                pe.wait_ge(w_in, 96)
                for c in range(NCH):
                    pe.wait_ge(z_ready, c + 1)
                    if c >= 1:
                        pe.wait_ge(tanh_low, 2 * c)
                    pe.matmul(p_la[:, :], wx1[:, 0:P], z[:, c % 2, :], start=True, stop=True).then_inc(low_ready, 1)
                    pe.matmul(p_lb[0:LR, :], wx1[:, P:P + LR], z[:, c % 2, :], start=True,
                              stop=True).then_inc(low_ready, 1)
                    pe.wait_ge(tanh_low, 2 * c + 2)
                    for i in range(MIXES):
                        n = MIXES * c + i
                        if n >= 2:
                            pe.wait_ge(tmp_ready, n - 1)
                        if i < 4:
                            lhs, rhs = wx2a[LR * i:LR * i + LR, :], low_a[LR * i:LR * i + LR, c % 2, :]
                        else:
                            lhs, rhs = wx2b[:, :], low_b[:, c % 2, :]
                        pe.matmul(p_mu[:, n % 2, :], lhs, rhs, start=True, stop=True).then_inc(mu_ready, 1)
                    cs = slice(c * CH, (c + 1) * CH)
                    pe.wait_ge(mixed, MIXES * c + 2)
                    if c >= 1:
                        pe.wait_ge(tw_done, c)
                        pe.wait_ge(g_done, 2 * c)
                    pe.matmul(p_tw[0:GATE, :], ww1[:, :], xi[:, 1, cs], start=True, stop=True).then_inc(tw_ready, 1)
                    pe.wait_ge(mixed, MIXES * c + 5)
                    for t in range(TPC):
                        tok = c * CH + t * P
                        mm = pe.matmul(p_g[:, t * P:(t + 1) * P], xi[:, 4, tok:tok + P], wg[:, :],
                                       start=True, stop=True)
                    mm.then_inc(g_ready, 1)

            @block.scalar
            def _(act):
                for c in range(NCH):
                    act.wait_ge(x_transposed, c + 1)
                    act.activation(xTp[:, 1 + c * CH:1 + (c + 1) * CH], p_x[:, c % 2, :],
                                   ACT.Copy).then_inc(xT_ready, 1)
                for c in range(NCH):
                    if c >= 2:
                        act.wait_ge(mu_ready, MIXES * (c - 1))
                    act.wait_ge(low_ready, 2 * c + 1)
                    act.activation(low_a[:, c % 2, :], p_la[:, :], ACT.Tanh).then_inc(tanh_low, 1)
                    act.wait_ge(low_ready, 2 * c + 2)
                    act.activation(low_b[:, c % 2, :], p_lb[0:LR, :], ACT.Tanh).then_inc(tanh_low, 1)
                    cs = slice(c * CH, (c + 1) * CH)
                    act.wait_ge(tw_ready, c + 1)
                    act.activation(tw[:, cs], p_tw[0:GATE, :], ACT.Tanh).then_inc(tw_done, 1)
                    act.wait_ge(g_ready, c + 1)
                    act.activation(g_th[:, cs], p_g[:, :], ACT.Tanh, scale=0.5).then_inc(g_done, 1)
                    act.activation(g_sb[:, cs], p_g[:, :], ACT.Copy).then_inc(g_done, 1)

            @block.vector
            def _(dve):
                dve.memset(xTp[:, 0:1], 0.0).then_inc(pad_set, 1)
                dve.wait_ge(pad_set, 1)
                dve.wait_ge(w_in, 96)

                def delta_z(c):
                    dve.wait_ge(xT_ready, c + 1)
                    dve.tensor_tensor(delta[:, c * CH:(c + 1) * CH], xTp[:, c * CH:(c + 1) * CH],
                                      xTp[:, 1 + c * CH:1 + (c + 1) * CH], ALU.subtract).then_inc(delta_ready, 1)
                    dve.wait_ge(delta_ready, c + 1)
                    if c >= 2:
                        dve.wait_ge(low_ready, 2 * (c - 1))
                    dve.scalar_tensor_tensor(z[:, c % 2, :], delta[:, c * CH:(c + 1) * CH], cols[:, 0:1],
                                             xTp[:, 1 + c * CH:1 + (c + 1) * CH], ALU.mult,
                                             ALU.add).then_inc(z_ready, 1)

                delta_z(0)
                for c in range(NCH):
                    if c + 1 < NCH:
                        delta_z(c + 1)
                    for i in range(MIXES):
                        n = MIXES * c + i
                        dve.wait_ge(mu_ready, n + 1)
                        if n >= 2:
                            dve.wait_ge(mixed, n - 1)
                        dve.scalar_tensor_tensor(tmp[:, n % 2, :], p_mu[:, n % 2, :], cols[:, 1 + i:2 + i],
                                                 delta[:, c * CH:(c + 1) * CH], ALU.add,
                                                 ALU.mult).then_inc(tmp_ready, 1)

            @block.gpsimd
            def _(pool):
                pool.wait_ge(xT_ready, NCH)
                for n in range(NCH * MIXES):
                    c, i = divmod(n, MIXES)
                    pool.wait_ge(tmp_ready, n + 1)
                    pool.tensor_tensor(xi[:, i, c * CH:(c + 1) * CH], tmp[:, n % 2, :],
                                       xTp[:, 1 + c * CH:1 + (c + 1) * CH], ALU.add).then_inc(mixed, 1)


def rwkv_scan(nc, a, xi, tw, o_sb):
    GATE = a["ww1"].shape[1]
    R_, K_, V_ = 0, 2, 3
    ROWS = HEADS_C * QK_C * V_C
    OC = HPC * V_C
    STEPS = NCH * HCH
    with Scope(nc, "cs_") as sc:
        w = sc.sb("w_rkv", [P, 3, ROWS])
        ww2 = sc.sb("ww2", [GATE, ROWS])
        cols = sc.sb("cols", [P, 2, HCH])
        sel = sc.sb("sel", [P, OC])
        ew = sc.sb("exp_w", [P, 2, CH])
        dec = sc.sb("decay", [P, 2, CH])
        v_sb = sc.sb("v", [P, 2, CH])
        kv = sc.sb("kv", [P, 2, CH])
        st = sc.sb("state", [P, HCH, 2, 1 + CH])
        m = sc.sb("m", [P, 2, CH])
        pr = sc.sb("pr", [P, 2, CH])
        p_w = sc.ps("p_w", [P, CH])
        p_k = sc.ps("p_k", [P, CH])
        p_v = sc.ps("p_v", [P, CH])
        p_r = sc.ps("p_r", [P, CH])
        p_o = sc.ps("p_o", [P, 2, CH])
        (w_in, w_ready, k_ready, v_ready, r_ready, exp_done, dec_done, v_done, kv_done, scanned, m_done, pr_done,
         zeroed, carried, o_ready, o_done) = (sc.sem(n) for n in (
             "w_in", "w_ready", "k_ready", "v_ready", "r_ready", "exp_done", "dec_done", "v_done", "kv_done",
             "scanned", "m_done", "pr_done", "zeroed", "carried", "o_ready", "o_done"))
        with nc.Block() as block:

            @block.sync
            def _(sp):
                sp.dma_start(ww2[:, :], a["ww2_rep"]).then_inc(w_in, 16)
                sp.dma_start(w[:, :, :], a["w_rkv_rep"]).then_inc(w_in, 16)
                sp.dma_start(cols[:, :, :], a["scan_cols"]).then_inc(w_in, 16)
                sp.dma_start(sel[:, :], a["sel"]).then_inc(w_in, 16)

            @block.tensor
            def _(pe):
                pe.wait_ge(w_in, 64)

                def out(n):
                    c, h = divmod(n, HCH)
                    pe.wait_ge(pr_done, n + 1)
                    if h == 0 and c >= 2:
                        pe.wait_ge(o_done, c - 1)
                    for t in range(TPC):
                        mm = pe.matmul(p_o[:, c % 2, t * P + h * OC:t * P + (h + 1) * OC],
                                       pr[:, n % 2, t * P:(t + 1) * P], sel[:, :], start=True, stop=True)
                    mm.then_inc(o_ready, 1)

                for n in range(STEPS):
                    c, h = divmod(n, HCH)
                    cs, rs = slice(c * CH, (c + 1) * CH), slice(h * P, (h + 1) * P)
                    if n >= 1:
                        pe.wait_ge(exp_done, n)
                    pe.matmul(p_w[:, :], ww2[:, rs], tw[:, cs], start=True, stop=True).then_inc(w_ready, 1)
                    if n >= 1:
                        pe.wait_ge(v_done, n)
                    pe.matmul(p_v[:, :], w[:, 2, rs], xi[:, V_, cs], start=True, stop=True).then_inc(v_ready, 1)
                    if n >= 1:
                        pe.wait_ge(kv_done, n)
                    pe.matmul(p_k[:, :], w[:, 1, rs], xi[:, K_, cs], start=True, stop=True).then_inc(k_ready, 1)
                    if n >= 1:
                        pe.wait_ge(pr_done, n)
                    pe.matmul(p_r[:, :], w[:, 0, rs], xi[:, R_, cs], start=True, stop=True).then_inc(r_ready, 1)
                    if n >= 1:
                        out(n - 1)
                out(STEPS - 1)

            @block.scalar
            def _(act):
                act.wait_ge(w_in, 64)
                for n in range(STEPS):
                    h = n % HCH
                    act.wait_ge(w_ready, n + 1)
                    act.activation(ew[:, n % 2, :], p_w[:, :], ACT.Exp, bias=cols[:, 0, h:h + 1]).then_inc(exp_done, 1)
                    act.wait_ge(exp_done, n + 1)
                    if n >= 2:
                        act.wait_ge(scanned, n - 1)
                    act.activation(dec[:, n % 2, :], ew[:, n % 2, :], ACT.Exp, scale=-1.0).then_inc(dec_done, 1)
                    act.wait_ge(v_ready, n + 1)
                    if n >= 2:
                        act.wait_ge(kv_done, n - 1)
                    act.activation(v_sb[:, n % 2, :], p_v[:, :], ACT.Copy).then_inc(v_done, 1)
                    if h == HCH - 1:
                        c = n // HCH
                        if c >= 1:
                            act.wait_ge(o_ready, HCH * c)
                            act.activation(o_sb[:, (c - 1) * CH:c * CH], p_o[:, (c - 1) % 2, :],
                                           ACT.Copy).then_inc(o_done, 1)
                act.wait_ge(o_ready, STEPS)
                act.activation(o_sb[:, (NCH - 1) * CH:], p_o[:, (NCH - 1) % 2, :], ACT.Copy).then_inc(o_done, 1)

            @block.vector
            def _(dve):
                dve.wait_ge(w_in, 64)
                dve.memset(st[:, :, 0, 0:1], 0.0).then_inc(zeroed, 1)
                dve.wait_ge(zeroed, 1)
                for n in range(STEPS):
                    c, h = divmod(n, HCH)
                    dve.wait_ge(v_done, n + 1)
                    dve.wait_ge(k_ready, n + 1)
                    dve.tensor_tensor(kv[:, n % 2, :], p_k[:, :], v_sb[:, n % 2, :], ALU.mult).then_inc(kv_done, 1)
                    dve.wait_ge(kv_done, n + 1)
                    dve.wait_ge(dec_done, n + 1)
                    if c >= 1:
                        dve.wait_ge(carried, n - HCH + 1)
                    dve.tensor_tensor_scan(st[:, h, c % 2, 1:], dec[:, n % 2, :], kv[:, n % 2, :],
                                           st[:, h, c % 2, 0:1], ALU.mult, ALU.add).then_inc(scanned, 1)
                    dve.wait_ge(scanned, n + 1)
                    dve.tensor_copy(st[:, h, (c + 1) % 2, 0:1], st[:, h, c % 2, CH:CH + 1]).then_inc(carried, 1)
                    dve.scalar_tensor_tensor(m[:, n % 2, :], kv[:, n % 2, :], cols[:, 1, h:h + 1],
                                             st[:, h, c % 2, 0:CH], ALU.mult, ALU.add).then_inc(m_done, 1)
                    dve.wait_ge(m_done, n + 1)
                    dve.wait_ge(r_ready, n + 1)
                    if n >= 2:
                        dve.wait_ge(o_ready, n - 1)
                    dve.tensor_tensor(pr[:, n % 2, :], m[:, n % 2, :], p_r[:, :], ALU.mult).then_inc(pr_done, 1)


def rwkv_out(nc, x_sb, ident, a, ln, o_sb, g_sb, g_th):
    NG = NT * HEADS_C
    with Scope(nc, "co_") as sc:
        wo = sc.sb("wo", [P, D])
        gn = sc.sb("gn", [P, 2, D])
        eps = sc.sb("eps", [P, 1])
        tot = sc.sb("tot", [P, NG])
        mean = sc.sb("mean", [P, NG])
        oc = sc.sb("centred", [P, S])
        sq = sc.sb("sq", [P, S])
        ssq = sc.sb("ssq", [P, NG])
        std = sc.sb("std", [P, NG])
        rstd = sc.sb("rstd", [P, NG])
        gate = sc.sb("gate", [P, S])
        oT = sc.sb("oT", [P, S])
        rows = sc.sb("rows", [P, NT, D])
        p_t = sc.ps("p_t", [P, 2, CH])
        p_y = sc.ps("p_y", [P, 2, CH])
        (w_in, step, squared, ssq_done, std_done, gated, transposed, oT_ready, y_ready, rows_ready) = (
            sc.sem(n) for n in ("w_in", "dve_step", "squared", "ssq_done", "std_done", "gated", "transposed",
                                "oT_ready", "y_ready", "rows_ready"))
        heads = lambda t: t[:, :].rearrange("p (g v) -> p g v", v=V_C)
        tiles = lambda t: t[:, :].rearrange("p (t d) -> p t d", d=D)
        with nc.Block() as block:

            @block.sync
            def _(sp):
                sp.dma_start(wo[:, :], a["wo_c"]).then_inc(w_in, 16)
                sp.dma_start(gn[:, :, :], a["gn"]).then_inc(w_in, 16)

            @block.vector
            def _(dve):
                dve.memset(eps[:, :], LN_EPS).then_inc(step, 1)
                dve.tensor_reduce(tot[:, :], heads(o_sb), AX, ALU.add).then_inc(step, 1)
                dve.wait_ge(step, 2)
                dve.tensor_scalar(mean[:, :], tot[:, :], 1.0 / V_C, None, ALU.mult).then_inc(step, 1)
                dve.wait_ge(step, 3)
                dve.tensor_tensor(heads(oc), heads(o_sb), mean[:, :].unsqueeze(2).to_broadcast([P, NG, V_C]),
                                  ALU.subtract).then_inc(step, 1)
                dve.scalar_tensor_tensor(gate[:, :], g_th[:, :], 1.0, g_sb[:, :], ALU.add,
                                         ALU.mult).then_inc(step, 1)
                dve.wait_ge(squared, 1)
                dve.tensor_reduce(ssq[:, :], heads(sq), AX, ALU.add).then_inc(ssq_done, 1)
                dve.wait_ge(std_done, 1)
                dve.reciprocal(rstd[:, :], std[:, :]).then_inc(step, 1)
                dve.wait_ge(step, 6)
                dve.tensor_tensor(heads(sq), heads(oc), rstd[:, :].unsqueeze(2).to_broadcast([P, NG, V_C]),
                                  ALU.mult).then_inc(step, 1)
                dve.wait_ge(w_in, 32)
                dve.wait_ge(step, 7)
                dve.tensor_tensor(tiles(oc), tiles(sq), gn[:, 0:1, :].to_broadcast([P, NT, D]),
                                  ALU.mult).then_inc(step, 1)
                dve.wait_ge(step, 8)
                dve.tensor_tensor(tiles(sq), tiles(oc), gn[:, 1:2, :].to_broadcast([P, NT, D]),
                                  ALU.add).then_inc(step, 1)
                dve.wait_ge(step, 9)
                for c in range(NCH):
                    cs = slice(c * CH, (c + 1) * CH)
                    dve.scalar_tensor_tensor(oc[:, cs], sq[:, cs], 0.5, gate[:, cs], ALU.mult,
                                             ALU.mult).then_inc(gated, 1)
                for c in range(NCH):
                    dve.wait_ge(y_ready, c + 1)
                    dve.tensor_tensor(rows[:, c * TPC:(c + 1) * TPC, :],
                                      p_y[:, c % 2, :].rearrange("p (t d) -> p t d", d=D),
                                      x_sb[:, c * TPC:(c + 1) * TPC, :], ALU.add).then_inc(rows_ready, 1)

            @block.scalar
            def _(act):
                act.wait_ge(step, 4)
                act.activation(sq[:, :], oc[:, :], ACT.Square).then_inc(squared, 1)
                act.wait_ge(ssq_done, 1)
                act.activation(std[:, :], ssq[:, :], ACT.Sqrt, scale=1.0 / V_C, bias=eps[:, 0:1]).then_inc(std_done, 1)
                for c in range(NCH):
                    act.wait_ge(transposed, c + 1)
                    act.activation(oT[:, c * CH:(c + 1) * CH], p_t[:, c % 2, :], ACT.Copy).then_inc(oT_ready, 1)

            @block.tensor
            def _(pe):
                for c in range(NCH):
                    pe.wait_ge(gated, c + 1)
                    if c >= 2:
                        pe.wait_ge(oT_ready, c - 1)
                    for t in range(TPC):
                        mm = pe.transpose(p_t[:, c % 2, t * P:(t + 1) * P],
                                          oc[:, c * CH + t * P:c * CH + (t + 1) * P], ident[:, :])
                    mm.then_inc(transposed, 1)
                pe.wait_ge(w_in, 32)
                for c in range(NCH):
                    pe.wait_ge(oT_ready, c + 1)
                    if c >= 2:
                        pe.wait_ge(rows_ready, c - 1)
                    for t in range(TPC):
                        mm = pe.matmul(p_y[:, c % 2, t * P:(t + 1) * P], oT[:, c * CH + t * P:c * CH + (t + 1) * P],
                                       wo[:, :], start=True, stop=True)
                    mm.then_inc(y_ready, 1)
        layernorm_block(nc, ln, "cln_", rows, x_sb)


def phase_int_ffn(nc, x_sb, ident, a, ln):
    HID = a["wg_t"].shape[1]
    HC = HID // P
    STEPS = NCH * HC
    SCALE = float(np.float32(1.0 / 127.0))
    with Scope(nc, "d_") as sc:
        wi = sc.sb("w_int", [P, 3, HID], I32)
        wf = sc.sb("w_f32", [P, 3, HID])
        xT = sc.sb("xT", [P, S])
        th = sc.sb("tanh", [P, 2, CH])
        t1 = sc.sb("gate_act", [P, 2, CH])
        hT = sc.sb("hT", [P, 2, HC, CH])
        rows = sc.sb("rows", [P, NT, D])
        p_gate = sc.ps("p_gate", [P, 2, CH])
        p_up = sc.ps("p_up", [P, 2, CH])
        p_y = sc.ps("p_y", [P, 2, CH])
        p_x = sc.ps("p_x", [P, 2, CH])
        names = ("w_in", "w_ready", "x_transposed", "xT_ready", "gate_up", "tanh_done", "act_done", "hidden",
                 "y_ready", "rows_ready")
        w_in, w_ready, x_transposed, xT_ready, gate_up, tanh_done, act_done, hidden, y_ready, rows_ready = (
            sc.sem(n) for n in names)
        with nc.Block() as block:

            @block.sync
            def _(sp):
                sp.dma_start(wi[:, 0, :], a["wg_t"]).then_inc(w_in, 16)
                sp.dma_start(wi[:, 1, :], a["wu_t"]).then_inc(w_in, 16)
                sp.dma_start(wi[:, 2, :].rearrange("p (c d) -> p c d", c=HC),
                             a["wd_t"].rearrange("(c p) d -> p c d", p=P)).then_inc(w_in, 16)

            @block.tensor
            def _(pe):
                for c in range(NCH):
                    if c >= 2:
                        pe.wait_ge(xT_ready, c - 1)
                    for t in range(TPC):
                        mm = pe.transpose(p_x[:, c % 2, t * P:(t + 1) * P], x_sb[:, c * TPC + t, :], ident[:, :])
                    mm.then_inc(x_transposed, 1)

                def down(c):
                    pe.wait_ge(hidden, HC * (c + 1))
                    if c >= 2:
                        pe.wait_ge(rows_ready, c - 1)
                    for t in range(TPC):
                        for k in range(HC):
                            mm = pe.matmul(p_y[:, c % 2, t * P:(t + 1) * P], hT[:, c % 2, k, t * P:(t + 1) * P],
                                           wf[:, 2, k * P:(k + 1) * P], start=(k == 0), stop=(k == HC - 1))
                    mm.then_inc(y_ready, 1)

                pe.wait_ge(w_ready, 3)
                for c in range(NCH):
                    pe.wait_ge(xT_ready, c + 1)
                    for k in range(HC):
                        n = c * HC + k
                        if n >= 2:
                            pe.wait_ge(hidden, n - 1)
                        pe.matmul(p_gate[:, n % 2, :], wf[:, 0, k * P:(k + 1) * P], xT[:, c * CH:(c + 1) * CH],
                                  start=True, stop=True)
                        pe.matmul(p_up[:, n % 2, :], wf[:, 1, k * P:(k + 1) * P], xT[:, c * CH:(c + 1) * CH],
                                  start=True, stop=True).then_inc(gate_up, 1)
                        if c >= 1 and k == 1:
                            down(c - 1)
                down(NCH - 1)

            @block.scalar
            def _(act):
                for c in range(NCH):
                    act.wait_ge(x_transposed, c + 1)
                    act.activation(xT[:, c * CH:(c + 1) * CH], p_x[:, c % 2, :], ACT.Copy).then_inc(xT_ready, 1)
                for n in range(STEPS):
                    act.wait_ge(gate_up, n + 1)
                    if n >= 2:
                        act.wait_ge(act_done, n - 1)
                    act.activation(th[:, n % 2, :], p_gate[:, n % 2, :], ACT.Tanh, scale=0.5).then_inc(tanh_done, 1)

            @block.vector
            def _(dve):
                dve.wait_ge(w_in, 48)
                for k in range(3):
                    dve.tensor_scalar(wf[:, k, :], wi[:, k, :], SCALE, None, ALU.mult).then_inc(w_ready, 1)

                def residual(c):
                    dve.wait_ge(y_ready, c + 1)
                    dve.tensor_tensor(rows[:, c * TPC:(c + 1) * TPC, :],
                                      p_y[:, c % 2, :].rearrange("p (t d) -> p t d", d=D),
                                      x_sb[:, c * TPC:(c + 1) * TPC, :], ALU.add).then_inc(rows_ready, 1)

                for n in range(STEPS):
                    c, k = divmod(n, HC)
                    dve.wait_ge(tanh_done, n + 1)
                    dve.scalar_tensor_tensor(t1[:, n % 2, :], th[:, n % 2, :], 1.0, p_gate[:, n % 2, :],
                                             ALU.add, ALU.mult).then_inc(act_done, 1)
                    dve.wait_ge(act_done, n + 1)
                    if c >= 2:
                        dve.wait_ge(y_ready, c - 1)
                    dve.scalar_tensor_tensor(hT[:, c % 2, k, :], t1[:, n % 2, :], 0.5, p_up[:, n % 2, :],
                                             ALU.mult, ALU.mult).then_inc(hidden, 1)
                    if c >= 1 and k == 2:
                        residual(c - 1)
                residual(NCH - 1)
        layernorm_block(nc, ln, "dln_", rows, x_sb)


def build(nc, a, out):
    Scope.used.clear()
    with Scope(nc, "g_") as sc:
        x_sb = sc.sb("x", [P, NT, D])
        ident = sc.sb("ident", [P, P])
        ln = LayerNorm(sc)
        load_block(nc, x_sb, ident, a["x"], a["ident"])
        phase_mha(nc, x_sb, ident, a, ln)
        clear_semaphores(nc)
        phase_local(nc, x_sb, ident, a, ln)
        phase_rwkv(nc, x_sb, ident, a, ln)
        phase_int_ffn(nc, x_sb, ident, a, ln)
        store_block(nc, x_sb, out)
    clear_semaphores(nc)


def _local_rotation_tables():
    f = np.float32
    half_idx = np.arange(0, DH, 2, dtype=f)
    inv_freq = f(1.0) / np.power(f(10000.0), half_idx / f(DH))
    t = np.arange(S, dtype=f)
    ang = np.tile(t[:, None] * inv_freq[None, :], 2)
    base = (half_idx + f(0.4 * DH)) / f(1.4 * DH)
    scale = np.tile(np.power(base[None, :].astype(np.float64), ((t - S // 2) / f(WINDOW // 2))[:, None]), 2)
    sign = np.where(np.arange(DH) < HALF, -1.0, 1.0)
    cos, sin = np.cos(ang.astype(np.float64)), np.sin(ang.astype(np.float64)) * sign
    both = np.stack([np.stack([w * 8.0 * scale, w / scale], 1) for w in (cos, sin)])
    return np.ascontiguousarray(both.reshape(2, NT, P, 2, DH).transpose(2, 0, 1, 3, 4).astype(f))


def _band_mask():
    q = np.arange(P)[:, None]
    k = np.arange(KEYS)[None, :] - WINDOW
    ok = (k <= q) & (k >= q - WINDOW)
    both = np.stack([ok & (k >= 0), ok])
    m = np.where(both, 0.0, -1e30).astype(np.float32)
    return np.ascontiguousarray(np.concatenate([m, m], -1).transpose(1, 0, 2))


def _rotation_tables():
    f = np.float32
    half = HD // 2
    freq = f(1.0) / np.power(f(10000.0), np.arange(half, dtype=f) / f(half))
    ang = (freq[:, None] * np.arange(S, dtype=f)[None, :]).astype(np.float64)
    cos, sin = np.cos(ang).astype(f), np.sin(ang).astype(f)
    return np.ascontiguousarray(np.tile(cos, (4, 1))), np.ascontiguousarray(np.concatenate([-sin, sin, -sin, sin]))


def _layouts(i):
    f = np.float32
    c = np.ascontiguousarray
    a = {"x": c(i["L0_attn_x"][0]), "ident": np.eye(P, dtype=f)}
    w = i["L0_attn_qkv_w"].reshape(D, 3, HEADS, HD)
    order = np.concatenate([np.arange(0, HD, 2), np.arange(1, HD, 2)])
    a["w_heads"] = c(np.concatenate([w[:, 0][..., order], w[:, 1][..., order], w[:, 2]], -1).transpose(1, 0, 2))
    b = i["L0_attn_qkv_b"].reshape(3, HEADS, HD)
    a["b_qk"] = c(np.concatenate([b[0][:, order], b[1][:, order]], -1).T)
    a["b_v"] = c(np.broadcast_to(b[2], (P, HEADS, HD)))
    a["cos"], a["sin"] = _rotation_tables()
    a["wo_a"] = i["L0_attn_out_w"]
    a["b_o"] = c(np.broadcast_to(i["L0_attn_out_b"], (P, 1, D)))
    a["rot"] = _local_rotation_tables()
    qk_scale = np.stack([i["L0_ffn_q_scale"], i["L0_ffn_k_scale"]], 1)
    a["qk_scale"] = c(np.broadcast_to(np.stack([qk_scale, np.roll(qk_scale, 32, -1)], 1), (P, 2, 2, 2, 64)))
    a["mask"] = _band_mask()
    a["wqkv"] = i["L0_ffn_wqkv"]
    a["wo_b"] = i["L0_ffn_wo"]
    a["ln_gb"] = c(np.stack([i["L0_ffn_ln_g"], i["L0_ffn_ln_b"]], -1))
    a["w1"] = i["L0_ffn_w1"]
    hid = i["L0_ffn_w2"].shape[1]
    b1 = np.zeros((2, 2, 3 * P), f)
    b1[:, :, :hid] = i["L0_ffn_b1"].reshape(2, 2, hid)
    a["b1"] = c(b1.reshape(2, 2, 3, P).transpose(0, 3, 1, 2))
    a["w2"] = i["L0_ffn_w2"]
    a["b2"] = i["L0_ffn_b2"]
    heads, qk, vd = 16, 4, 8
    over_v = lambda w: np.repeat(w, vd, axis=-1)
    over_qk = lambda w: np.repeat(w.reshape(w.shape[:-1] + (heads, 1, vd)), qk, axis=-2).reshape(w.shape[:-1] + (-1,))
    rows = lambda v: c(v.reshape(4, P).T)
    a["mix_cols"] = c(np.stack([i["L1_attn_mu_x"], *i["L1_attn_x_bias"]], 1))
    a["wx1"] = i["L1_attn_W_x1"]
    a["wx2_t"] = c(i["L1_attn_W_x2"].transpose(1, 2, 0).reshape(-1, D))
    a["ww1"] = i["L1_attn_W_w1"]
    a["wg"] = i["L1_attn_W_g"]
    a["ww2_rep"] = c(over_v(i["L1_attn_W_w2"]))
    a["w_rkv_rep"] = c(np.stack([over_v(i["L1_attn_W_r"]), over_v(i["L1_attn_W_k"]), over_qk(i["L1_attn_W_v"])], 1))
    a["scan_cols"] = c(np.stack([rows(over_v(i["L1_attn_b_w2"])), rows(over_v(i["L1_attn_u"].reshape(-1)))], 1))
    a["sel"] = c(np.eye(32, dtype=f).reshape(4, 1, 8, 32).repeat(4, 1).reshape(P, 32))
    a["wo_c"] = i["L1_attn_W_o"]
    a["gn"] = c(np.broadcast_to(np.stack([i["L1_attn_gn_w"], i["L1_attn_gn_b"]]), (P, 2, D)))
    a["wg_t"] = c(i["L1_ffn_w_gate"].T)
    a["wu_t"] = c(i["L1_ffn_w_up"].T)
    a["wd_t"] = c(i["L1_ffn_w_down"].T)
    return a


def kernel(**inputs):
    import concourse.bacc as bacc
    from concourse.bass_utils import run_bass_kernel_spmd

    arrays = _layouts({k: np.asarray(v) for k, v in inputs.items()})
    nc = bacc.Bacc("TRN2", target_bir_lowering=False, num_devices=1)
    aps = {n: nc.dram_tensor(f"in_{n}", v.shape, mybir.dt.from_np(v.dtype), kind="ExternalInput").ap()
           for n, v in arrays.items()}
    out = nc.dram_tensor("out", (S, D), F32, kind="ExternalOutput").ap()
    build(nc, aps, out)
    r = run_bass_kernel_spmd(nc, [{f"in_{n}": v for n, v in arrays.items()}], core_ids=[0])
    return r.results[0]["out"].reshape(1, S, D)
```

```python
from contextlib import ExitStack

import numpy as np
import concourse.bass as bass
from concourse import mybir

ALU = mybir.AluOpType
ACT = mybir.ActivationFunctionType
AX = mybir.AxisListType.X
F32 = mybir.dt.float32
F16 = mybir.dt.float16
I32 = mybir.dt.int32

P = 128
D = 128
S = 2048
NT = S // P
CH = 512
NCH = S // CH
TPC = CH // P
LN_EPS = 1e-5


class Scope:
    used, long = [], []

    def __init__(self, nc, prefix, side=None):
        self.nc, self.prefix, self.side, self.stack = nc, prefix, side, ExitStack()

    def __enter__(self):
        return self

    def __exit__(self, *exc):
        return self.stack.__exit__(*exc)

    def sb(self, name, shape, dt=F32):
        return self.stack.enter_context(self.nc.sbuf_tensor(self.prefix + name, shape, dt, side=self.side))

    def ps(self, name, shape, dt=F32):
        return self.stack.enter_context(self.nc.psum_tensor(self.prefix + name, shape, dt))

    def sem(self, name):
        handle = self.nc.alloc_semaphore(name=self.prefix + name)
        Scope.used.append(handle)
        return handle

    def long_sem(self, name):
        handle = self.nc.alloc_semaphore(name=self.prefix + name)
        Scope.long.append(handle)
        return handle


def clear_semaphores(nc, all_of_them=False):
    if all_of_them:
        Scope.used += Scope.long
    nc.clear_and_free_semaphores(Scope.used)
    nc.all_engine_barrier()
    Scope.used.clear()


def ge(eng, sem, value, alone=None):
    if isinstance(value, int):
        if value > 0:
            eng.wait_ge(sem, value)
        return
    if alone is not None:
        value = eng.to_reg(value)
        eng.wait_ge(alone, 1)
    eng.wait_ge(sem, value)


def ge_both(eng, sem_a, value_a, sem_b, value_b):
    if not isinstance(value_a, int):
        value_a, value_b = eng.to_reg(value_a), eng.to_reg(value_b)
    ge(eng, sem_a, value_a)
    ge(eng, sem_b, value_b)


class LayerNorm:

    def __init__(self, sc):
        self.stats = sc.sb("ln_stats", [P, NT, 6])
        self.mv = sc.sb("ln_mean_var", [P, NT, 2])
        self.eps = sc.sb("ln_eps", [P, 1])
        self.std = sc.sb("ln_std", [P, NT])
        self.rstd = sc.sb("ln_rstd", [P, NT])
        self.shift = sc.sb("ln_shift", [P, NT])


def layernorm_block(nc, ln, name, rows, x_out):
    stats, mv, eps, std, rstd, shift = ln.stats, ln.mv, ln.eps, ln.std, ln.rstd, ln.shift
    ON_ACT, ON_POOL = 5, 3
    with Scope(nc, name) as sc:
        (eps_set, table_in, stats_done, var_done, std_done, rstd_done, shift_done, normed, normed_pool,
         normed_act) = (sc.sem(n) for n in ("eps_set", "table_in", "stats_done", "var_done", "std_done", "rstd_done",
                                            "shift_done", "normed", "normed_pool", "normed_act"))
        with nc.Block() as block:

            @block.vector
            def _(dve):
                dve.memset(eps[:, :], LN_EPS).then_inc(eps_set, 1)
                for t in range(NT):
                    dve.bn_stats(stats[:, t, :], rows[:, t, :]).then_inc(stats_done, 1)
                for t in range(NT):
                    dve.wait_ge(stats_done, t + 1)
                    dve.bn_aggr(mv[:, t, :], stats[:, t, :]).then_inc(var_done, 1)
                dve.wait_ge(std_done, 1)
                dve.reciprocal(rstd[:, :], std[:, :]).then_inc(rstd_done, 1)
                dve.wait_ge(rstd_done, 1)
                dve.scalar_tensor_tensor(shift[:, :], mv[:, :, 0], -1.0, rstd[:, :], ALU.mult,
                                         ALU.mult).then_inc(shift_done, 1)
                for t in range(ON_ACT + ON_POOL, NT):
                    dve.tensor_scalar(x_out[:, t, :], rows[:, t, :], mv[:, t, 0:1], rstd[:, t:t + 1],
                                      ALU.subtract, ALU.mult).then_inc(normed, 1)

            @block.gpsimd
            def _(pool):
                pool.wait_ge(rstd_done, 1)
                for t in range(ON_ACT, ON_ACT + ON_POOL):
                    pool.tensor_scalar(x_out[:, t, :], rows[:, t, :], mv[:, t, 0:1], rstd[:, t:t + 1],
                                       ALU.subtract, ALU.mult).then_inc(normed_pool, 1)

            @block.scalar
            def _(act):
                act.wait_ge(eps_set, 1)
                act.activation(std[:, 0:1], eps[:, :], ACT.Sqrt).then_inc(table_in, 1)
                act.wait_ge(table_in, 1)
                act.wait_ge(var_done, NT)
                act.activation(std[:, :], mv[:, :, 1], ACT.Sqrt, bias=eps[:, 0:1]).then_inc(std_done, 1)
                act.wait_ge(shift_done, 1)
                for t in range(ON_ACT):
                    act.activation(x_out[:, t, :], rows[:, t, :], ACT.Identity, scale=rstd[:, t:t + 1],
                                   bias=shift[:, t:t + 1]).then_inc(normed_act, 1)


def load_block(nc, x_sb, ident, x_dram, ident_dram):
    with Scope(nc, "ld_") as sc:
        loaded = sc.sem("loaded")
        with nc.Block() as block:
            @block.sync
            def _(sp):
                sp.dma_start(x_sb[:, :, :], x_dram.rearrange("(t p) d -> p t d", p=P)).then_inc(loaded, 16)
                sp.dma_start(ident[:, :], ident_dram).then_inc(loaded, 16)
                sp.wait_ge(loaded, 32)


def store_block(nc, x_sb, out_dram):
    with Scope(nc, "st_") as sc:
        stored = sc.sem("stored")
        with nc.Block() as block:
            @block.sync
            def _(sp):
                sp.dma_start(out_dram.rearrange("(t p) d -> p t d", p=P), x_sb[:, :, :]).then_inc(stored, 16)
                sp.wait_ge(stored, 16)


HEADS, HD = 16, 64
KT = NT
QC = NCH
SETS = 3
VW = HD + 1
LAST = HEADS - 1
MAX_SLOTS = (2, 1, 2, 1, 1, 1, 1, 1, 1, 1, 1, 1, 1, 1, 0, 0)
LAG = 5
TAIL = {0: (KT - LAG, KT - LAG + 1), **{i: (KT - LAG + 1 + i,) for i in range(1, LAG - 1)}}
RP, RW = 4, 8
LO_DVE = (3, 6, 10, 14)
LO_POOL = tuple(kt for kt in range(KT) if kt not in LO_DVE)
HI_DVE = (6, 10)
HI_ACT = tuple(kt for kt in range(KT) if kt not in HI_DVE)
BANK = tuple(kt % 3 for kt in range(KT - 1)) + ((KT - 3) % 3,)
HELD = tuple(max(k for k in range(-KT, kt) if BANK[k % KT] == BANK[kt]) for kt in range(KT))
EXP_SHIFT = 12 * float(np.log(2.0)) * HD ** 0.5


def phase_mha(nc, x_sb, ident, a, ln, local_scope, late_scope):
    with Scope(nc, "a_") as sc:
        attn = sc.sb("attn", [P, NT, HEADS * HD])
        mha_heads(nc, x_sb, ident, a, attn)
        late = LateWeights(late_scope, a)
        local = LocalWeights(local_scope, a)
        mha_out(nc, x_sb, ident, a, ln, attn, local, late)
    return local, late


def run_heads(eng, head, turn):
    for n in (-2, -1):
        head(n, n % SETS)
        for qc in range(QC):
            turn(n, n % SETS, qc)

    def one(n, s):
        head(n, s)
        turn(n, s, 0)
        with eng.Fori(1, QC) as qc:
            turn(n, s, qc)

    one(0, 0)
    with eng.Fori(0, 4) as third:
        for i in range(SETS):
            one(third * SETS + (i + 1), (i + 1) % SETS)
    for n in range(4 * SETS + 1, HEADS):
        one(n, n % SETS)


def before(n, s, qc):
    return (n - 1, (s - 1) % SETS, QC - 1) if isinstance(qc, int) and qc == 0 else (n, s, qc - 1)


def follows(n, qc):
    return has(n, 0) and not (isinstance(n, int) and n == 0 and isinstance(qc, int) and qc == 0)


def found_max(n, qc):
    if not isinstance(n, int):
        return True
    return 0 <= (n - 1 if isinstance(qc, int) and qc == 0 else n) + 1 <= LAST


def done(which, e, kt):
    if kt < 0:
        e, kt = e - 1, kt + KT
    return len(which) * e + sum(t <= kt for t in which)


def has(n, ahead):
    return not isinstance(n, int) or 0 <= n + ahead <= LAST


def cols(c, w):
    return slice(c * w, c * w + w) if isinstance(c, int) else bass.ds(c * w, w)


def mha_heads(nc, x_sb, ident, a, attn):
    with Scope(nc, "ah_") as sc:
        xh = sc.sb("xT_hi", [P, S], F16)
        xl = sc.sb("xT_lo", [P, S], F16)
        cos = sc.sb("cos", [P, S])
        sin = sc.sb("sin", [P, S])
        bv = sc.sb("bias_v", [P, HEADS, HD])
        w32 = sc.sb("w_head", [P, 3 * HD])
        wh = sc.sb("w_hi", [P, 3 * HD], F16)
        wl = sc.sb("w_lo", [P, 3 * HD], F16)
        bqk = sc.sb("bias_qk", [P, HEADS])
        qh = sc.sb("q_hi_twice", [P, SETS, S], F16)
        ks = sc.sb("k_hi_lo", [P, SETS, S], F16)
        k1 = sc.sb("k_hi_one", [P, SETS, S], F16)
        ql = sc.sb("q_lo_max", [P, SETS, S], F16)
        vh = sc.sb("v_hi", [P, SETS, KT, VW], F16)
        vl = sc.sb("v_lo", [P, SETS, KT, HD], F16)
        v32 = sc.sb("v", [P, TPC, HD])
        qk = sc.sb("qk", [P, CH])
        qks = sc.sb("qk_swapped", [P, CH])
        t1 = sc.sb("rot_cos", [P, CH])
        t2 = sc.sb("rot_sin", [P, CH])
        r = sc.sb("rotated", [P, CH])
        hi = sc.sb("hi", [P, CH], F16)
        lo = sc.sb("lo", [P, CH], F16)
        part = sc.sb("part_max", [P, TPC, 4])
        negm = sc.sb("neg_max", [P, TPC], F16)
        identh = sc.sb("ident_f16", [P, P], F16)
        pb = sc.sb("probs", [P, RP, CH])
        ph = sc.sb("probs_hi", [P, RW, CH], F16)
        pl = sc.sb("probs_lo", [P, RW, CH], F16)
        rcp = sc.sb("rcp", [P, TPC])

        p_s = sc.ps("p_s", [P, 3, CH])
        p_o = sc.ps("p_o", [P, CH])
        p_m = sc.ps("p_m", [P, 2, CH])
        p_a = sc.ps("p_a", [P, CH])
        p_v = sc.ps("p_v", [P, CH])
        p_t = p_a
        v_ones = sc.sem("v_ones")
        (c_in, w_in, x_turned, xh_ready, xl_ready, consts, w_split, proj_ready, qk_ready, swapped, t1_done, t2_done,
         r_ready, hi_done, lo_done, spread, v_ready, v_done, m_ready, maxed, m_done, m_turned, mrow_ready, s_ready,
         exp_done, hi_act, hi_dve, lo_pool, lo_dve, v_biased, vh_done, o_ready, rcp_done,
         o_free) = (sc.sem(n) for n in (
             "c_in", "w_in", "x_turned", "xh_ready", "xl_ready", "consts", "w_split", "proj_ready", "qk_ready",
             "swapped", "t1_done", "t2_done", "r_ready", "hi_done", "lo_done", "spread", "v_ready", "v_done",
             "m_ready", "maxed", "m_done", "m_turned", "mrow_ready", "s_ready", "exp_done", "hi_act", "hi_dve",
             "lo_pool", "lo_dve", "v_biased", "vh_done", "o_ready", "rcp_done", "o_free"))
        SPREAD = 6 * 16

        with nc.Block() as block:

            @block.sync
            def _(sp):
                sp.dma_start(w32[:, :], a["w_heads"][0]).then_inc(w_in, 16)
                sp.dma_start(cos[:, :], a["cos"]).then_inc(c_in, 16)
                sp.dma_start(sin[:, :], a["sin"]).then_inc(c_in, 16)
                sp.dma_start(bqk[:, :], a["b_qk"]).then_inc(c_in, 16)
                sp.dma_start(bv[:, :, :], a["b_v"]).then_inc(c_in, 16)

                def head(n, s):
                    if has(n, 3):
                        ge(sp, w_split, 2 * (n + 3))
                        sp.dma_start(w32[:, :], a["w_heads"][n + 3]).then_inc(w_in, 16)

                def swap(g):
                    ge_both(sp, qk_ready, g + 1, t2_done, g)
                    for q in range(4):
                        o, i = 32 * q, 32 * (q ^ 1)
                        sp.dma_start(qks[o:o + 32, :], qk[i:i + 32, :]).then_inc(swapped, 16)

                def turn(n, s, qc):
                    if has(n, 2):
                        g, to = 4 * (n + 2) + qc, (s + 2) % SETS
                        first_steady = 4 * 2
                        if not isinstance(g, int) or g == 0 or g >= first_steady:
                            swap(g)
                        if isinstance(g, int) and g + 1 < first_steady:
                            swap(g + 1)
                        ge(sp, spread, SPREAD * g)
                        ge(sp, hi_done, g + 1)
                        ge(sp, lo_done, g + 1)
                        c = cols(qc, CH)
                        for dst, src in ((qh[0:HD, to, c], hi[0:HD, :]), (qh[HD:P, to, c], hi[0:HD, :]),
                                         (ks[0:HD, to, c], hi[HD:P, :]), (ks[HD:P, to, c], lo[HD:P, :]),
                                         (k1[0:HD, to, c], hi[HD:P, :]), (ql[0:HD, to, c], lo[0:HD, :])):
                            sp.dma_start(dst, src).then_inc(spread, 16)
                run_heads(sp, head, turn)

            @block.gpsimd
            def _(pool):
                pool.memset(vh[:, :, :, HD:VW], 1.0).then_inc(v_ones, 1)
                pool.wait_ge(v_ones, 1)
                pool.memset(k1[HD:HD + 1, :, :], 1.0).then_inc(consts, 1)

                def head(n, s):
                    pass

                def turn(n, s, qc):
                    for kt in range(KT):
                        if has(n, 0) and kt in LO_POOL:
                            ge(pool, hi_act, done(HI_ACT, 4 * n + qc, kt))
                            pool.tensor_tensor(pl[:, kt % RW, :], pb[:, kt % RP, :], ph[:, kt % RW, :],
                                               ALU.subtract).then_inc(lo_pool, 1)
                        if has(n, 2):
                            g = 4 * (n + 2) + qc
                            if kt == 9:
                                ge_both(pool, t1_done, g + 1, t2_done, g + 1)
                                pool.tensor_tensor(r[:, :], t1[:, :], t2[:, :], ALU.add).then_inc(r_ready, 1)
                            if kt == 14:
                                ge_both(pool, hi_done, g + 1, spread, SPREAD * g)
                                pool.tensor_tensor(lo[:, :], r[:, :], hi[:, :], ALU.subtract).then_inc(lo_done, 1)
                            if kt == 12:
                                ge(pool, vh_done, g + 1)
                                pool.tensor_tensor(vl[:, (s + 2) % SETS, cols(qc, TPC), :], v32[:, :, :],
                                                   vh[:, (s + 2) % SETS, cols(qc, TPC), 0:HD],
                                                   ALU.subtract).then_inc(v_done, 1)
                run_heads(pool, head, turn)

            @block.tensor
            def _(pe):
                for c in range(NCH):
                    if c >= 2:
                        pe.wait_ge(xl_ready, c - 1)
                    for t in range(TPC):
                        mm = pe.transpose(p_m[:, c % 2, t * P:(t + 1) * P], x_sb[:, c * TPC + t, :], ident[:, :])
                    mm.then_inc(x_turned, 1)
                pe.wait_ge(xl_ready, NCH)
                pe.wait_ge(consts, 2)

                def head(n, s):
                    pass

                def maxima(n, s, qc, m):
                    g, st = 4 * (n + 1) + qc, (s + 1) % SETS
                    kc, t = divmod(m, TPC)
                    if m == (NCH - 1) * TPC:
                        ge(pe, spread, SPREAD * 4 * (n + 2))
                    if m >= 2 or found_max(n, qc):
                        ge(pe, maxed, 16 * g + m - 1)
                    pe.matmul(p_m[:, m % 2, :], qh[:, st, cols(qc * TPC + t, P)],
                              ks[:, st, kc * CH:(kc + 1) * CH], start=True, stop=True).then_inc(m_ready, 1)

                def scores(n, s, qc, kt):
                    held = HELD[kt]
                    if held >= 0 or follows(n, qc):
                        if held % KT in HI_DVE:
                            ge(pe, exp_done, done(HI_DVE, 4 * n + qc, held))
                        else:
                            ge(pe, hi_act, done(HI_ACT, 4 * n + qc, held))
                    pe.matmul(p_s[:, BANK[kt], :], ks[:, s, kt * P:(kt + 1) * P], qh[:, s, cols(qc, CH)],
                              start=True, stop=False)
                    pe.matmul(p_s[:, BANK[kt], :], k1[0:HD + 1, s, kt * P:(kt + 1) * P],
                              ql[0:HD + 1, s, cols(qc, CH)], start=False, stop=True).then_inc(s_ready, 1)

                def weigh(n, s, qc, kt):
                    e = 4 * n + qc
                    if kt == 0:
                        ge(pe, o_free, e + 1)
                    if kt in LO_DVE:
                        ge(pe, lo_dve, done(LO_DVE, e, kt))
                    else:
                        ge(pe, lo_pool, done(LO_POOL, e, kt))
                    for i in range(TPC):
                        o = p_o[:, i * VW:(i + 1) * VW]
                        hi_i = ph[:, kt % RW, i * P:(i + 1) * P]
                        lo_i = pl[:, kt % RW, i * P:(i + 1) * P]
                        pe.matmul(o, hi_i, vh[:, s, kt, :], start=(kt == 0 and i == 0), stop=False,
                                  skip_group_check=True)
                        pe.matmul(o[:, 0:HD], hi_i, vl[:, s, kt, :], start=False, stop=False, skip_group_check=True)
                        mm = pe.matmul(o, lo_i, vh[:, s, kt, :], start=False, stop=(kt == KT - 1),
                                       skip_group_check=True)
                    if kt == KT - 1:
                        mm.then_inc(o_ready, 1)

                def turn(n, s, qc):
                    m = 0
                    if has(n, 1):
                        ge(pe, spread, SPREAD * (4 * (n + 1) + NCH - 1))
                    if has(n, 0):
                        ge(pe, mrow_ready, 4 * n + qc + 1)
                        ge(pe, v_done, 4 * (n + 1))
                    for kt in range(KT):
                        if has(n, 0):
                            scores(n, s, qc, kt)
                        if has(n, 1):
                            for _ in range(MAX_SLOTS[kt]):
                                maxima(n, s, qc, m)
                                m += 1
                        if has(n, 2):
                            g = 4 * (n + 2) + qc
                            if kt == 1:
                                ge(pe, w_split, 2 * (n + 3))
                                ge_both(pe, qk_ready, g, mrow_ready, max(g - 5, 0) if isinstance(g, int) else g - 5)
                                c = cols(qc, CH)
                                pe.matmul(p_a[:, :], wh[:, 0:P], xh[:, c], start=True, stop=False)
                                pe.matmul(p_a[:, :], wl[:, 0:P], xh[:, c], start=False, stop=False)
                                pe.matmul(p_a[:, :], wh[:, 0:P], xl[:, c], start=False,
                                          stop=True).then_inc(proj_ready, 1)
                            if 6 <= kt < 6 + TPC:
                                if kt == 6:
                                    ge(pe, v_biased, g)
                                t = kt - 6
                                c = cols(qc * TPC + t, P)
                                o = p_v[:, t * HD:(t + 1) * HD]
                                pe.matmul(o, xh[:, c], wh[:, P:], start=True, stop=False)
                                pe.matmul(o, xh[:, c], wl[:, P:], start=False, stop=False)
                                mm = pe.matmul(o, xl[:, c], wh[:, P:], start=False, stop=True)
                                if t == TPC - 1:
                                    mm.then_inc(v_ready, 1)
                        if kt == 5 and found_max(n, qc):
                            e = 4 * n + qc + 3
                            ge(pe, m_done, e + 1)
                            if has(n, 2):
                                ge(pe, qk_ready, e + 6)
                            else:
                                ge(pe, mrow_ready, e)
                            for t in range(TPC):
                                mm = pe.matmul(p_t[HD:HD + 1, t * P:(t + 1) * P], negm[:, t:t + 1], identh[:, :],
                                               start=True, stop=True)
                            mm.then_inc(m_turned, 1)
                        if follows(n, qc):
                            for late in TAIL.get(kt, ()):
                                weigh(*before(n, s, qc), late)
                        if has(n, 0) and kt >= LAG:
                            weigh(n, s, qc, kt - LAG)
                run_heads(pe, head, turn)
                for late in range(KT - LAG, KT):
                    weigh(LAST, LAST % SETS, QC - 1, late)

            @block.scalar
            def _(act):
                for c in range(NCH):
                    act.wait_ge(x_turned, c + 1)
                    act.activation(xh[:, c * CH:(c + 1) * CH], p_m[:, c % 2, :], ACT.Copy).then_inc(xh_ready, 1)
                act.wait_ge(c_in, 64)
                act.wait_ge(consts, 2)

                def head(n, s):
                    pass

                def turn(n, s, qc):
                    for kt in range(KT):
                        if has(n, 0):
                            ge(act, s_ready, 16 * (4 * n + qc) + kt + 1)
                            e, by = 4 * n + qc, (kt - RP) % KT
                            if by in LO_DVE:
                                ge(act, lo_dve, done(LO_DVE, e, kt - RP))
                            else:
                                ge(act, lo_pool, done(LO_POOL, e, kt - RP))
                            exp = act.activation(pb[:, kt % RP, :], p_s[:, BANK[kt], :], ACT.Exp, scale=HD ** -0.5)
                            if kt in HI_DVE:
                                exp.then_inc(exp_done, 1)
                            else:
                                act.activation(ph[:, kt % RW, :], p_s[:, BANK[kt], :], ACT.Exp,
                                               scale=HD ** -0.5).then_inc(hi_act, 1)
                        if has(n, 2) and kt == 2:
                            g = 4 * (n + 2) + qc
                            ge(act, proj_ready, g + 1)
                            ge(act, t1_done, g)
                            ge(act, swapped, 64 * g, alone=consts)
                            act.activation(qk[:, :], p_a[:, :], ACT.Identity,
                                           bias=bqk[:, cols(n + 2, 1)]).then_inc(qk_ready, 1)
                        if kt == 6 and found_max(n, qc):
                            ps, pq = before(n, s, qc)[1:]
                            ge(act, m_turned, 4 * n + qc + 4)
                            act.activation(ql[HD:HD + 1, (ps + 1) % SETS, cols(pq, CH)], p_t[HD:HD + 1, :],
                                           ACT.Copy, bias=EXP_SHIFT).then_inc(mrow_ready, 1)
                run_heads(act, head, turn)

            @block.vector
            def _(dve):
                for c in range(NCH):
                    cs = slice(c * CH, (c + 1) * CH)
                    dve.wait_ge(xh_ready, c + 1)
                    dve.tensor_tensor(xl[:, cs], p_m[:, c % 2, :], xh[:, cs], ALU.subtract).then_inc(xl_ready, 1)
                dve.tensor_copy(identh[:, :], ident[:, :]).then_inc(consts, 1)
                dve.memset(part[:, :, :], 0.0).then_inc(o_free, 1)
                dve.wait_ge(o_free, 1)
                dve.wait_ge(c_in, 64)
                dve.wait_ge(consts, 2)

                def head(n, s):
                    if has(n, 2):
                        ge(dve, w_in, 16 * (n + 3))
                        ge(dve, v_ready, 4 * (n + 2))
                        dve.tensor_copy(wh[:, :], w32[:, :]).then_inc(w_split, 1)
                        ge(dve, w_split, 2 * (n + 2) + 1)
                        dve.tensor_tensor(wl[:, :], w32[:, :], wh[:, :], ALU.subtract).then_inc(w_split, 1)

                def normalise(n, s, qc):
                    e = 4 * n + qc
                    ge(dve, o_ready, e + 1)
                    o = p_o[:, 0:TPC * VW].rearrange("p (t w) -> p t w", w=VW)
                    dve.reciprocal(rcp[:, :], o[:, :, HD]).then_inc(rcp_done, 1)
                    ge(dve, rcp_done, e + 1)
                    dve.tensor_tensor(attn[:, cols(qc, TPC), cols(n, HD)], o[:, :, 0:HD],
                                      rcp[:, :].unsqueeze(2).to_broadcast([P, TPC, HD]),
                                      ALU.mult).then_inc(o_free, 1)

                def turn(n, s, qc):
                    m = 0
                    for kt in range(KT):
                        if kt == LAG - 1 and follows(n, qc):
                            normalise(*before(n, s, qc))
                        if has(n, 1):
                            g = 4 * (n + 1) + qc
                            for _ in range(MAX_SLOTS[kt]):
                                if m == 0:
                                    ge(dve, m_done, g)
                                ge(dve, m_ready, 16 * g + m + 1)
                                dve.tensor_reduce(part[:, m % TPC, m // TPC:m // TPC + 1], p_m[:, m % 2, :], AX,
                                                  ALU.max).then_inc(maxed, 1)
                                m += 1
                            if kt == 14:
                                ge(dve, maxed, 16 * (g + 1))
                                ge(dve, m_turned, g)
                                dve.tensor_reduce(negm[:, :], part[:, :, :], AX, ALU.max,
                                                  negate=True).then_inc(m_done, 1)
                        if has(n, 0) and kt - 1 in LO_DVE:
                            j, e = kt - 1, 4 * n + qc
                            if j in HI_DVE:
                                ge(dve, exp_done, done(HI_DVE, e, j))
                                dve.tensor_copy(ph[:, j % RW, :], pb[:, j % RP, :]).then_inc(hi_dve, 1)
                                ge(dve, hi_dve, done(HI_DVE, e, j))
                            else:
                                ge(dve, hi_act, done(HI_ACT, e, j))
                            dve.tensor_tensor(pl[:, j % RW, :], pb[:, j % RP, :], ph[:, j % RW, :],
                                              ALU.subtract).then_inc(lo_dve, 1)
                        if has(n, 2):
                            g, to = 4 * (n + 2) + qc, (s + 2) % SETS
                            c = cols(qc, CH)
                            if kt == 3:
                                ge(dve, qk_ready, g + 1)
                                ge(dve, r_ready, g)
                                dve.tensor_tensor(t1[:, :], qk[:, :], cos[:, c], ALU.mult).then_inc(t1_done, 1)
                            if kt == 8:
                                ge(dve, swapped, 64 * (g + 1))
                                ge(dve, lo_done, g)
                                dve.tensor_tensor(t2[:, :], qks[:, :], sin[:, c], ALU.mult).then_inc(t2_done, 1)
                            if kt == 13:
                                ge_both(dve, r_ready, g + 1, spread, SPREAD * g)
                                dve.tensor_copy(hi[:, :], r[:, :]).then_inc(hi_done, 1)
                            if kt == 10:
                                ge(dve, v_ready, g + 1)
                                ge(dve, v_done, g)
                                src = p_v[:, 0:TPC * HD].rearrange("p (t d) -> p t d", d=HD)
                                dve.tensor_tensor(v32[:, :, :], src, bv[:, cols(n + 2, 1), :].to_broadcast(
                                    [P, TPC, HD]), ALU.add).then_inc(v_biased, 1)
                            if kt == 11:
                                ge(dve, v_biased, g + 1)
                                dve.tensor_copy(vh[:, to, cols(qc, TPC), 0:HD], v32[:, :, :]).then_inc(vh_done, 1)
                run_heads(dve, head, turn)
                normalise(LAST, LAST % SETS, QC - 1)


def mha_out(nc, x_sb, ident, a, ln, attn, local, late):
    IC = HEADS * HD // P
    with Scope(nc, "ao_") as sc:
        wo = sc.sb("wo", [P, IC, D])
        bo = sc.sb("bo", [P, 1, D])
        xb = sc.sb("x_plus_bias", [P, NT, D])
        aT = sc.sb("attnT", [P, 2, IC, P])
        rows = sc.sb("rows", [P, NT, D])
        p_t = sc.ps("p_t", [P, 2, 2, CH])
        p_y = sc.ps("p_y", [P, 2, CH])
        w_in, biased, turned, copied_a, copied_b, y_ready, rows_ready = (
            sc.sem(n) for n in ("w_in", "biased", "turned", "copied_a", "copied_b", "y_ready", "rows_ready"))
        with nc.Block() as block:

            @block.sync
            def _(sp):
                sp.dma_start(bo[:, :, :], a["b_o"]).then_inc(w_in, 16)
                sp.dma_start(wo[:, :, :], a["wo_a"].rearrange("(c p) d -> p c d", p=P)).then_inc(w_in, 16)
                local.start(sp)
                late.start(sp)

            @block.tensor
            def _(pe):
                def turn(t):
                    if t >= 2:
                        pe.wait_ge(copied_a, t - 1)
                        pe.wait_ge(copied_b, t - 1)
                    for c in range(IC):
                        mm = pe.transpose(p_t[:, t % 2, c // 4, (c % 4) * P:(c % 4 + 1) * P],
                                          attn[:, t, c * P:(c + 1) * P], ident[:, :])
                    mm.then_inc(turned, 1)

                turn(0)
                pe.wait_ge(w_in, 32)
                for t in range(NT):
                    if t + 1 < NT:
                        turn(t + 1)
                    pe.wait_ge(copied_a, t + 1)
                    pe.wait_ge(copied_b, t + 1)
                    if t >= 2:
                        pe.wait_ge(rows_ready, t - 1)
                    for c in range(IC):
                        mm = pe.matmul(p_y[:, t % 2, 0:D], aT[:, t % 2, c, :], wo[:, c, :], start=(c == 0),
                                       stop=(c == IC - 1))
                    mm.then_inc(y_ready, 1)

            @block.scalar
            def _(act):
                for t in range(NT):
                    act.wait_ge(turned, t + 1)
                    if t >= 2:
                        act.wait_ge(y_ready, t - 1)
                    act.activation(aT[:, t % 2, 0:4, :], p_t[:, t % 2, 0, :].rearrange("p (c t) -> p c t", t=P),
                                   ACT.Copy).then_inc(copied_a, 1)

            @block.gpsimd
            def _(pool):
                pool.wait_ge(w_in, 32)
                pool.tensor_tensor(xb[:, :, :], x_sb[:, :, :], bo[:, :, :].to_broadcast([P, NT, D]),
                                   ALU.add).then_inc(biased, 1)

            @block.vector
            def _(dve):
                for t in range(NT):
                    dve.wait_ge(turned, t + 1)
                    if t >= 2:
                        dve.wait_ge(y_ready, t - 1)
                    dve.tensor_copy(aT[:, t % 2, 4:8, :],
                                    p_t[:, t % 2, 1, :].rearrange("p (c t) -> p c t", t=P)).then_inc(copied_b, 1)
                    if t == 1:
                        dve.wait_ge(biased, 1)
                    if t >= 1:
                        dve.wait_ge(y_ready, t)
                        dve.tensor_tensor(rows[:, t - 1, :], p_y[:, (t - 1) % 2, 0:D], xb[:, t - 1, :],
                                          ALU.add).then_inc(rows_ready, 1)
                dve.wait_ge(y_ready, NT)
                dve.tensor_tensor(rows[:, NT - 1, :], p_y[:, (NT - 1) % 2, 0:D], xb[:, NT - 1, :],
                                  ALU.add).then_inc(rows_ready, 1)
        layernorm_block(nc, ln, "aln_", rows, x_sb)


class LateWeights:

    def __init__(self, sc, a):
        GATE, HID = a["ww1"].shape[1], a["wg_t"].shape[1]
        rows = a["ww2_rep"].shape[1]
        self.cols = sc.sb("mix_cols", [P, a["mix_cols"].shape[1]])
        self.wx1 = sc.sb("wx1", list(a["wx1"].shape))
        self.wx2a = sc.sb("wx2a", [P, P])
        self.wx2b = sc.sb("wx2b", [a["wx2_t"].shape[0] - P, P])
        self.ww1 = sc.sb("ww1", [P, GATE])
        self.wg = sc.sb("wg", [P, D])
        self.ww2 = sc.sb("ww2", [GATE, rows])
        self.w_rkv = sc.sb("w_rkv", [P, 3, rows])
        self.scan_cols = sc.sb("scan_cols", [P, 2, rows // P])
        self.sel = sc.sb("sel", list(a["sel"].shape))
        self.wo = sc.sb("wo_c", [P, D])
        self.gn = sc.sb("gn", [P, 2, D])
        self.w_int = sc.sb("w_int", [P, 3, HID], I32)
        self.mix_in, self.scan_in, self.out_in, self.int_in = (
            sc.long_sem(n) for n in ("mix_in", "scan_in", "out_in", "int_in"))
        self.a = a

    MIX, SCAN, OUT, INT = 6 * 16, 4 * 16, 2 * 16, 3 * 16

    def start(self, sp):
        a = self.a
        for dst, src in ((self.cols[:, :], a["mix_cols"]), (self.wx1[:, :], a["wx1"]),
                         (self.wx2a[:, :], a["wx2_t"][0:P, :]), (self.wx2b[:, :], a["wx2_t"][P:, :]),
                         (self.ww1[:, :], a["ww1"]), (self.wg[:, :], a["wg"])):
            sp.dma_start(dst, src).then_inc(self.mix_in, 16)
        for dst, src in ((self.ww2[:, :], a["ww2_rep"]), (self.w_rkv[:, :, :], a["w_rkv_rep"]),
                         (self.scan_cols[:, :, :], a["scan_cols"]), (self.sel[:, :], a["sel"])):
            sp.dma_start(dst, src).then_inc(self.scan_in, 16)
        sp.dma_start(self.wo[:, :], a["wo_c"]).then_inc(self.out_in, 16)
        sp.dma_start(self.gn[:, :, :], a["gn"]).then_inc(self.out_in, 16)
        sp.dma_start(self.w_int[:, 0, :], a["wg_t"]).then_inc(self.int_in, 16)
        sp.dma_start(self.w_int[:, 1, :], a["wu_t"]).then_inc(self.int_in, 16)
        sp.dma_start(self.w_int[:, 2, :].rearrange("p (c d) -> p c d", d=D),
                     a["wd_t"].rearrange("(c p) d -> p c d", p=P)).then_inc(self.int_in, 16)


DEPTH = 2
HEADS_B, DH, WINDOW = 8, 64, 64
INNER = HEADS_B * DH
HALF = DH // 2
PAIRS = HEADS_B // 2
KEYS = WINDOW + P
GRP = 4
STAGES = 5
UNROLL = 4
PEEL = 2 * UNROLL
BF16 = mybir.dt.bfloat16
PROB_SCALE = 4096.0


def run_steps(eng, step):
    for j in range(PEEL):
        step(j, j % UNROLL)
    with eng.Fori(0, (NT - PEEL) // UNROLL) as turn:
        for u in range(UNROLL):
            step(turn * UNROLL + (PEEL + u), u)
    for j in range(NT, NT + STAGES):
        step(j, j % UNROLL)


def live(j, lag):
    return not isinstance(j, int) or 0 <= j - lag < NT


class LocalWeights:
    QUARTER = NT // 4

    def __init__(self, sc, a):
        hid = a["w2"].shape[1]
        hc = -(-hid // P)
        self.hid, self.a = hid, a
        self.wqkv = sc.sb("wqkv", [P, DEPTH, 3 * INNER])
        self.wo = sc.sb("wo", [P, DEPTH, PAIRS, D])
        self.raw_tab = sc.sb("rot_const", [P, 2, NT, 2, DH])
        self.scl = sc.sb("qk_scale", [P, DEPTH, 2, 2, DH])
        self.mask_f = sc.sb("mask_f32", [P, 2, 2 * KEYS])
        self.mask = sc.sb("mask", [P, 2, 2 * KEYS], BF16)
        self.identb = sc.sb("ident_bf16", [P, P], BF16)
        self.wqh = sc.sb("wqkv_hi", [P, 3 * INNER], F16)
        self.wql = sc.sb("wqkv_lo", [P, 3 * INNER], F16)
        self.tab = sc.sb("rot", [P, 2, NT, 2, DH])
        self.w1 = sc.sb("w1", [P, DEPTH, 2 * hid])
        self.w2 = sc.sb("w2", [P, DEPTH, hc, D])
        self.b1 = sc.sb("b1", [P, DEPTH, 2, hc])
        self.b2 = sc.sb("b2", [1, DEPTH, D])
        self.gb = sc.sb("ln_gb", [P, DEPTH, 2])
        self.qkv_in = [sc.long_sem(f"qkv_in{l}") for l in range(DEPTH)]
        self.mask_in = sc.long_sem("mask_in")
        self.tab_in = [sc.long_sem(f"tab_in{q}") for q in range(4)]
        self.ff_in = [sc.long_sem(f"ff_in{l}") for l in range(DEPTH)]
        self.FF = 16 * (4 + hc)

    def start(self, sp):
        a, n = self.a, self.QUARTER

        def attention(l):
            sp.dma_start(self.wqkv[:, l, :], a["wqkv"][l]).then_inc(self.qkv_in[l], 16)
            sp.dma_start(self.wo[:, l, :, :], a["wo_b"][l].rearrange("(c p) d -> p c d", p=P)).then_inc(
                self.qkv_in[l], 16)

        def feed_forward(l):
            sp.dma_start(self.gb[:, l, :], a["ln_gb"][l]).then_inc(self.ff_in[l], 16)
            sp.dma_start(self.w1[:, l, :], a["w1"][l]).then_inc(self.ff_in[l], 16)
            sp.dma_start(self.b1[:, l, :, :], a["b1"][l]).then_inc(self.ff_in[l], 16)
            sp.dma_start(self.b2[:, l, :], a["b2"][l:l + 1, :]).then_inc(self.ff_in[l], 16)
            for k, at in enumerate(range(0, self.hid, P)):
                rows = min(P, self.hid - at)
                sp.dma_start(self.w2[0:rows, l, k, :], a["w2"][l, at:at + rows, :]).then_inc(self.ff_in[l], 16)

        sp.dma_start(self.mask_f[:, :, :], a["mask"]).then_inc(self.mask_in, 16)
        sp.dma_start(self.scl[:, :, :, :, :], a["qk_scale"]).then_inc(self.mask_in, 16)
        attention(0)
        for q in range(4):
            sp.dma_start(self.raw_tab[:, :, q * n:(q + 1) * n, :, :],
                         a["rot"][:, :, q * n:(q + 1) * n, :, :]).then_inc(self.tab_in[q], 16)
        feed_forward(0)
        attention(1)
        feed_forward(1)

    def scale_table(self, dve, l, q, scaled):
        dve.wait_ge(self.tab_in[q], 16)
        ts = slice(q * self.QUARTER, (q + 1) * self.QUARTER)
        for s in range(2):
            for r in range(2):
                dve.tensor_tensor(self.tab[:, s, ts, r, :], self.raw_tab[:, s, ts, r, :],
                                  self.scl[:, l, s, r:r + 1, :].to_broadcast([P, self.QUARTER, DH]),
                                  ALU.mult).then_inc(scaled, 1)

    def prepare(self, dve, l, ident, made):
        if l == 0:
            dve.wait_ge(self.mask_in, 32)
            dve.tensor_copy(self.identb[:, :], ident[:, :]).then_inc(made, 1)
            dve.tensor_copy(self.mask[:, :, :], self.mask_f[:, :, :]).then_inc(made, 1)
        else:
            dve.nop().then_inc(made, 2)
        dve.wait_ge(self.qkv_in[l], 32)
        dve.tensor_copy(self.wqh[:, :], self.wqkv[:, l, :]).then_inc(made, 1)
        dve.wait_ge(made, 3)
        dve.tensor_tensor(self.wql[:, :], self.wqkv[:, l, :], self.wqh[:, :], ALU.subtract).then_inc(made, 1)
        self.scale_table(dve, l, 0, made)


def phase_local(nc, x_sb, ident, ln, lw):
    with Scope(nc, "b_") as sc:
        x0 = sc.sb("x_in", [P, NT, D])
        h_tok = sc.sb("h_tok", [P, NT + 1, D])
        with Scope(nc, "bi_") as si:
            kept = si.sem("kept")
            with nc.Block() as block:
                @block.vector
                def _(dve):
                    dve.tensor_copy(x0[:, :, :], x_sb[:, :, :]).then_inc(kept, 1)
                    dve.memset(h_tok[:, NT, :], 0.0)
                    dve.memset(h_tok[0:1, 0, D // 2:], 0.0)
        for l in range(DEPTH):
            shift_block(nc, f"bs{l}_", x_sb, h_tok, lambda dve, made: lw.prepare(dve, l, ident, made))
            local_attention(nc, l, x_sb, h_tok, ident, lw)
            shift_block(nc, f"bt{l}_", x_sb, h_tok)
            layernorm_block(nc, ln, f"bl{l}_", h_tok, h_tok)
            geglu(nc, l, x_sb, h_tok, ident, lw)
            clear_semaphores(nc)
        with Scope(nc, "br_") as si:
            rows = si.sb("rows", [P, NT, D])
            with nc.Block() as block:
                @block.vector
                def _(dve):
                    dve.tensor_tensor(rows[:, :, :], x_sb[:, :, :], x0[:, :, :], ALU.add)
            layernorm_block(nc, ln, "bln_", rows, x_sb)


def shift_block(nc, name, x_sb, h_tok, meanwhile=None):
    H = D // 2
    with Scope(nc, name) as sc:
        shifted = sc.sem("shifted")
        first_zeroed, made = sc.sem("first_zeroed"), sc.sem("made")
        with nc.Block() as block:
            @block.sync
            def _(sp):
                sp.dma_start(h_tok[1:P, 0:NT, H:], x_sb[0:P - 1, :, H:]).then_inc(shifted, 16)
                sp.dma_start(h_tok[0:1, 1:NT, H:], x_sb[P - 1:P, 0:NT - 1, H:]).then_inc(shifted, 16)
                sp.wait_ge(shifted, 32)

            @block.vector
            def _(dve):
                dve.tensor_copy(h_tok[:, 0:NT, 0:H], x_sb[:, :, 0:H])
                dve.memset(h_tok[0:1, 0, H:], 0.0).then_inc(first_zeroed, 1)
                if meanwhile:
                    meanwhile(dve, made)


def local_attention(nc, l, x_sb, h_tok, ident, lw):
    with Scope(nc, f"ba{l}_") as sc:
        wqh, wql, wo, tab, mask, identb = lw.wqh, lw.wql, lw.wo[:, l], lw.tab, lw.mask, lw.identb
        half_neg = sc.sb("minus_half", [P, 2 * HEADS_B])
        hs = sc.sb("h_tile", [P, 2, P])
        hTh = sc.sb("hT_hi", [P, 2, KEYS], F16)
        hTl = sc.sb("hT_lo", [P, 2, KEYS], F16)
        sq = sc.sb("sq", [P, 2 * INNER])
        ssq = sc.sb("ssq", [P, 2, 2 * HEADS_B])
        ssc = sc.sb("ssq_clamped", [P, 2, 2 * HEADS_B])
        rinv = sc.sb("rnorm", [P, 2, 2 * HEADS_B])
        t1 = sc.sb("rot_cos", [P, 2, 2 * INNER])
        t2 = sc.sb("rot_sin", [P, 2, 2 * INNER])
        t3 = sc.sb("rot_sum", [P, 2 * INNER])
        qk = sc.sb("qk", [P, 2, 2 * INNER])
        qT = sc.sb("qT", [P, 2, PAIRS, P])
        kT = sc.sb("kT", [P, 2, PAIRS, KEYS])
        vah = sc.sb("v_a_hi", [P, 4, INNER], F16)
        val = sc.sb("v_a_lo", [P, 4, INNER], F16)
        vbh = sc.sb("v_b_hi", [WINDOW, 4, INNER], F16)
        vbl = sc.sb("v_b_lo", [WINDOW, 4, INNER], F16)
        negmax = sc.sb("negmax", [P, 2, HEADS_B])
        pr = sc.sb("probs", [P, 2, HEADS_B, KEYS])
        rsum = sc.sb("rsum", [P, 2, HEADS_B])
        rcp = sc.sb("rcp", [P, 2, HEADS_B])
        ptah = sc.sb("probsT_a_hi", [P, HEADS_B, P], F16)
        ptal = sc.sb("probsT_a_lo", [P, HEADS_B, P], F16)
        ptbh = sc.sb("probsT_b_hi", [WINDOW, HEADS_B, P], F16)
        ptbl = sc.sb("probsT_b_lo", [WINDOW, HEADS_B, P], F16)
        at = sc.sb("attn", [P, 2, INNER])
        atT = sc.sb("attnT", [P, PAIRS, P])

        p_v = sc.ps("p_v", [P, CH])
        p_q = sc.ps("p_q", [P, CH])
        p_k = sc.ps("p_k", [P, CH])
        p_s = sc.ps("p_s", [P, 2, CH])
        p_p = sc.ps("p_p", [P, CH])
        p_o = sc.ps("p_o", [P, CH])
        p_x = sc.ps("p_x", [P, CH])
        (hTh_ready, vah_done, vbh_done, pth_done, tab_ready, mask_ready, hs_ready, hT_turned, hT_carry, hT_ready,
         qk_ready, squared, t_done, ssq_done, t3_done, clamped, rinv_done, roped, q_turned, k_turned, qT_ready,
         kT_ready, kT_carry, va_ready, va_done, vb_ready, vb_done, s_ready, max_done, exp_done, pt_turned, pt_done,
         o_ready, rcp_done, at_ready, at_turned, atT_ready, y_ready, x_updated) = (sc.sem(n) for n in (
             "hTh_ready", "vah_done", "vbh_done", "pth_done", "tab_ready", "mask_ready", "hs_ready", "hT_turned",
             "hT_carry", "hT_ready", "qk_ready", "squared", "t_done", "ssq_done", "t3_done", "clamped",
             "rinv_done", "roped", "q_turned", "k_turned", "qT_ready", "kT_ready", "kT_carry", "va_ready",
             "va_done", "vb_ready", "vb_done", "s_ready", "max_done", "exp_done", "pt_turned", "pt_done",
             "o_ready", "rcp_done", "at_ready", "at_turned", "atT_ready", "y_ready", "x_updated"))

        with nc.Block() as block:

            @block.gpsimd
            def _(pool):
                def stage(j, u):
                    ge(pool, hT_turned, j - 1, alone=tab_ready)
                    pool.tensor_copy(hs[:, u % 2, :], h_tok[:, j, :]).then_inc(hs_ready, 1)

                def hT_head(j, u):
                    ge(pool, hT_ready, j, alone=tab_ready)
                    ge(pool, vb_ready, j - 1, alone=tab_ready)
                    for part in (hTh, hTl):
                        pool.tensor_copy(part[:, u % 2, 0:WINDOW], part[:, (u + 1) % 2, P:KEYS]).then_inc(hT_carry, 1)

                def kT_head(t, u):
                    ge(pool, kT_ready, t, alone=tab_ready)
                    ge(pool, s_ready, 2 * (t - 1), alone=tab_ready)
                    pool.tensor_copy(kT[:, u % 2, :, 0:WINDOW],
                                     kT[:, (u + 1) % 2, :, P:KEYS]).then_inc(kT_carry, 1)

                pool.memset(half_neg[:, :], -0.5).then_inc(tab_ready, 1)
                pool.memset(hTh[:, 0, 0:WINDOW], 0.0).then_inc(hT_carry, 1)
                pool.memset(hTl[:, 0, 0:WINDOW], 0.0).then_inc(hT_carry, 1)
                pool.memset(kT[:, 0, :, 0:WINDOW], 0.0).then_inc(kT_carry, 1)
                stage(0, 0)

                def step(j, u):
                    if live(j, 0):
                        stage(j + 1, u + 1)
                    if live(j, 2) and not (isinstance(j, int) and j == 2):
                        kT_head(j - 2, u - 2)
                    if live(j, 0):
                        hT_head(j + 1, u + 1)
                        ge(pool, t_done, 3 * (j + 1))
                        ge(pool, roped, j)
                        pool.tensor_tensor(t3[:, :], t1[:, u % 2, :], t2[:, u % 2, :], ALU.add).then_inc(t3_done, 1)
                        ge(pool, ssq_done, j + 1, alone=tab_ready)
                        pool.tensor_scalar(ssc[:, u % 2, :], ssq[:, u % 2, :], 1e-24, None,
                                           ALU.max).then_inc(clamped, 1)
                        ge(pool, clamped, j + 1)
                        pool.tensor_tensor(rinv[:, u % 2, :], ssc[:, u % 2, :], half_neg[:, :],
                                           ALU.pow).then_inc(rinv_done, 1)
                        ge(pool, rinv_done, j + 1)
                        ge(pool, t3_done, j + 1)
                        ge(pool, k_turned, j - 1)
                        pool.tensor_tensor(qk[:, u % 2, :].rearrange("p (g d) -> p g d", d=DH),
                                           t3[:, :].rearrange("p (g d) -> p g d", d=DH),
                                           rinv[:, u % 2, :].unsqueeze(2).to_broadcast([P, 2 * HEADS_B, DH]),
                                           ALU.mult).then_inc(roped, 1)
                run_steps(pool, step)

            @block.tensor
            def _(pe):
                pe.wait_ge(lw.qkv_in[l], 32)
                pe.wait_ge(mask_ready, 2)

                def split_matmul(out, buf, tokens, which):
                    cs = slice(which * INNER, (which + 1) * INNER)
                    pe.matmul(out, hTh[:, buf, tokens], wqh[:, cs], start=True, stop=False)
                    pe.matmul(out, hTh[:, buf, tokens], wql[:, cs], start=False, stop=False)
                    return pe.matmul(out, hTl[:, buf, tokens], wqh[:, cs], start=False, stop=True)

                def turn_probs(t, u, g, tail):
                    n = 4 * t + 2 * g + tail
                    ge(pe, exp_done, HEADS_B * t + GRP * (g + 1), alone=mask_ready)
                    ge(pe, pt_done, n, alone=mask_ready)
                    for i in range(GRP):
                        h = GRP * g + i
                        src = pr[:, u % 2, h, P:KEYS] if tail else pr[:, u % 2, h, 0:P]
                        mm = pe.transpose(p_p[0:WINDOW if tail else P, i * P:(i + 1) * P], src, ident[:, :])
                    mm.then_inc(pt_turned, 1)

                def scores(t, u, g):
                    ge(pe, qT_ready, t + 1)
                    ge(pe, kT_ready, t + 1)
                    ge(pe, kT_carry, t + 1)
                    ge(pe, exp_done, HEADS_B * t + GRP * g)
                    for b in range(2):
                        pe.matmul(p_s[:, b, 0:2 * KEYS], identb[:, :],
                                  mask[:, 0 if isinstance(t, int) and t == 0 else 1, :], start=True, stop=False,
                                  skip_group_check=True)
                    for i in range(GRP):
                        h = GRP * g + i
                        rows = slice(DH * (h % 2), DH * (h % 2) + DH)
                        mm = pe.matmul(p_s[:, i % 2, (i // 2) * KEYS:(i // 2 + 1) * KEYS], qT[rows, u % 2, h // 2, :],
                                       kT[rows, u % 2, h // 2, :], start=False, stop=True, skip_group_check=True)
                    mm.then_inc(s_ready, 1)

                def step(j, u):
                    if live(j, 0):
                        ge(pe, hs_ready, j + 1)
                        ge(pe, vb_done, j - 1)
                        pe.transpose(p_v[:, 0:P], hs[:, u % 2, :], ident[:, :]).then_inc(hT_turned, 1)
                    if live(j, 4):
                        turn_probs(j - 4, u - 4, 0, 0)
                    if live(j, 3):
                        scores(j - 3, u - 3, 0)
                    if live(j, 2):
                        t, v = j - 2, u - 2
                        ge_both(pe, roped, t + 1, t_done, 3 * (min(j, NT) if isinstance(j, int) else j))
                        for s, (bank, turned) in enumerate(((p_q, q_turned), (p_k, k_turned))):
                            for c in range(PAIRS):
                                col = s * INNER + c * P
                                mm = pe.transpose(bank[:, c * P:(c + 1) * P], qk[:, v % 2, col:col + P], ident[:, :])
                            mm.then_inc(turned, 1)
                    if live(j, 5):
                        t = j - 5
                        ge(pe, at_ready, t + 1)
                        ge(pe, x_updated, t)
                        for c in range(PAIRS):
                            mm = pe.transpose(p_x[:, c * P:(c + 1) * P], at[:, (u - 5) % 2, c * P:(c + 1) * P],
                                              ident[:, :])
                        mm.then_inc(at_turned, 1)
                    if live(j, 4):
                        turn_probs(j - 4, u - 4, 0, 1)
                    if live(j, 1):
                        ge(pe, hT_carry, 2 * j)
                        ge(pe, vb_done, j - 1)
                        if live(j, 0):
                            ge(pe, hT_ready, j + 1)
                        split_matmul(p_v[:, :], (u - 1) % 2, slice(0, P), 2).then_inc(va_ready, 1)
                    if live(j, 0):
                        ge(pe, hT_ready, j + 1)
                        ge(pe, qT_ready, j - 1)
                        ge(pe, kT_ready, j - 1)
                        if not live(j, 2):
                            ge(pe, t_done, 3 * j)
                        split_matmul(p_q[:, :], u % 2, slice(WINDOW, KEYS), 0)
                        split_matmul(p_k[:, :], u % 2, slice(WINDOW, KEYS), 1).then_inc(qk_ready, 1)
                    if live(j, 4):
                        turn_probs(j - 4, u - 4, 1, 0)
                    if live(j, 5):
                        t = j - 5
                        ge(pe, atT_ready, t + 1)
                        for c in range(PAIRS):
                            mm = pe.matmul(p_x[:, 0:D], atT[:, c, :], wo[:, c, :], start=(c == 0),
                                           stop=(c == PAIRS - 1))
                        mm.then_inc(y_ready, 1)
                    if live(j, 1):
                        ge(pe, va_done, j)
                        split_matmul(p_v[0:WINDOW, :], (u - 1) % 2, slice(P, KEYS), 2).then_inc(vb_ready, 1)
                    if live(j, 4):
                        turn_probs(j - 4, u - 4, 1, 1)
                    if live(j, 3):
                        scores(j - 3, u - 3, 1)
                    if live(j, 4):
                        t, b = j - 4, (u - 4) % 4
                        ge(pe, pt_done, 4 * (t + 1))
                        ge(pe, vb_done, t + 1)
                        ge(pe, at_ready, t)
                        for h in range(HEADS_B):
                            cs = slice(h * DH, (h + 1) * DH)
                            parts = ((ptah, vah), (ptah, val), (ptal, vah), (ptbh, vbh), (ptbh, vbl), (ptbl, vbh))
                            for i, (p, v) in enumerate(parts):
                                mm = pe.matmul(p_o[:, cs], p[:, h, :], v[:, b, cs], start=(i == 0), stop=(i == 5))
                        mm.then_inc(o_ready, 1)
                run_steps(pe, step)

            @block.scalar
            def _(act):
                def high_probs(t, g, tail):
                    ge(act, pt_turned, 4 * t + 2 * g + tail + 1)
                    ge(act, o_ready, t)
                    dst, rows = (ptbh, WINDOW) if tail else (ptah, P)
                    act.activation(dst[:, GRP * g:GRP * g + GRP, :],
                                   p_p[0:rows, :].rearrange("p (h t) -> p h t", h=GRP), ACT.Copy,
                                   scale=PROB_SCALE).then_inc(pth_done, 1)

                def exps(t, u, g):
                    ge(act, max_done, 2 * t + g + 1)
                    ge(act, pt_turned, 4 * (t - 1))
                    for i in range(GRP):
                        h = GRP * g + i
                        act.activation(pr[:, u % 2, h, :], p_s[:, i % 2, (i // 2) * KEYS:(i // 2 + 1) * KEYS],
                                       ACT.Exp, bias=negmax[:, u % 2, h:h + 1],
                                       accum_out=rsum[:, u % 2, h:h + 1]).then_inc(exp_done, 1)

                def step(j, u):
                    if live(j, 0):
                        ge(act, hT_turned, j + 1)
                        ge(act, vb_ready, j - 1)
                        ge(act, hT_carry, 2 * j)
                        act.activation(hTh[:, u % 2, WINDOW:KEYS], p_v[:, 0:P], ACT.Copy).then_inc(hTh_ready, 1)
                    if live(j, 4):
                        high_probs(j - 4, 0, 0)
                    if live(j, 2):
                        t, v = j - 2, u - 2
                        ge(act, q_turned, t + 1)
                        ge(act, s_ready, 2 * (t - 1))
                        act.activation(qT[:, v % 2, :, :], p_q[:, :].rearrange("p (c t) -> p c t", c=PAIRS),
                                       ACT.Copy).then_inc(qT_ready, 1)
                        ge(act, k_turned, t + 1)
                        ge(act, kT_carry, t)
                        act.activation(kT[:, v % 2, :, WINDOW:KEYS], p_k[:, :].rearrange("p (c t) -> p c t", c=PAIRS),
                                       ACT.Copy).then_inc(kT_ready, 1)
                    if live(j, 5):
                        t = j - 5
                        ge(act, at_turned, t + 1)
                        ge(act, y_ready, t)
                        act.activation(atT[:, :, :], p_x[:, :].rearrange("p (c t) -> p c t", c=PAIRS),
                                       ACT.Copy, scale=1.0 / PROB_SCALE).then_inc(atT_ready, 1)
                    if live(j, 4):
                        high_probs(j - 4, 0, 1)
                    if live(j, 3):
                        exps(j - 3, u - 3, 0)
                    if live(j, 1):
                        ge(act, va_ready, j)
                        ge(act, o_ready, j - 4)
                        act.activation(vah[:, (u - 1) % 4, :], p_v[:, :], ACT.Copy).then_inc(vah_done, 1)
                    if live(j, 4):
                        high_probs(j - 4, 1, 0)
                    if live(j, 0):
                        ge(act, qk_ready, j + 1)
                        ge(act, ssq_done, j)
                        act.activation(sq[:, 0:INNER], p_q[:, :], ACT.Square).then_inc(squared, 1)
                        act.activation(sq[:, INNER:], p_k[:, :], ACT.Square).then_inc(squared, 1)
                    if live(j, 1):
                        ge(act, vb_ready, j)
                        act.activation(vbh[:, (u - 1) % 4, :], p_v[0:WINDOW, :], ACT.Copy).then_inc(vbh_done, 1)
                    if live(j, 4):
                        high_probs(j - 4, 1, 1)
                    if live(j, 3):
                        exps(j - 3, u - 3, 1)
                run_steps(act, step)

            @block.vector
            def _(dve):
                dve.nop().then_inc(mask_ready, 2)

                def low_probs(t, g, tail):
                    ge(dve, pth_done, 4 * t + 2 * g + tail + 1)
                    rows = WINDOW if tail else P
                    hi, dst = (ptbh, ptbl) if tail else (ptah, ptal)
                    hs_ = slice(GRP * g, GRP * g + GRP)
                    dve.scalar_tensor_tensor(dst[:, hs_, :], p_p[0:rows, :].rearrange("p (h t) -> p h t", h=GRP),
                                             PROB_SCALE, hi[:, hs_, :], ALU.mult, ALU.subtract).then_inc(pt_done, 1)

                def low_v(t, u, hi, lo, hi_done, lo_done, rows):
                    ge(dve, hi_done, t + 1)
                    dve.tensor_tensor(lo[:, u % 4, :], p_v[0:rows, :], hi[:, u % 4, :],
                                      ALU.subtract).then_inc(lo_done, 1)

                def maxes(t, u, g):
                    ge(dve, s_ready, 2 * t + g + 1)
                    ge(dve, exp_done, HEADS_B * (t - 1))
                    src = p_s[:, :, 0:2 * KEYS].rearrange("p b (i k) -> p b i k", i=2)
                    dve.tensor_reduce(negmax[:, u % 2, GRP * g:GRP * g + GRP].rearrange("p (i b) -> p b i", b=2),
                                      src, AX, ALU.max, negate=True).then_inc(max_done, 1)

                def rot(j, u, part):
                    for s, bank in ((0, p_q), (1, p_k)):
                        x3 = bank[:, :].rearrange("p (h d) -> p h d", d=DH)
                        tb = tab[:, 0 if part == 0 else 1, j, s, :]
                        if part == 0:
                            o, i, w = slice(0, DH), slice(0, DH), DH
                        else:
                            o = slice(0, HALF) if part == 1 else slice(HALF, DH)
                            i = slice(HALF, DH) if part == 1 else slice(0, HALF)
                            w = HALF
                        dst = (t1 if part == 0 else t2)[:, u % 2, s * INNER:(s + 1) * INNER].rearrange(
                            "p (h d) -> p h d", d=DH)
                        ins = dve.tensor_tensor(dst[:, :, o], x3[:, :, i],
                                                tb[:, o].unsqueeze(1).to_broadcast([P, HEADS_B, w]), ALU.mult)
                    ins.then_inc(t_done, 1)

                def step(j, u):
                    if isinstance(j, int) and j == lw.QUARTER:
                        dve.wait_ge(tab_ready, 1 + 4 * 3)
                    if live(j, 5):
                        t = j - 5
                        ge(dve, o_ready, t + 1)
                        dve.reciprocal(rcp[:, (u - 5) % 2, :], rsum[:, (u - 5) % 2, :]).then_inc(rcp_done, 1)
                        ge(dve, rcp_done, t + 1)
                        ge(dve, at_turned, t)
                        dve.tensor_tensor(at[:, (u - 5) % 2, :].rearrange("p (h d) -> p h d", d=DH),
                                          p_o[:, :].rearrange("p (h d) -> p h d", d=DH),
                                          rcp[:, (u - 5) % 2, :].unsqueeze(2).to_broadcast([P, HEADS_B, DH]),
                                          ALU.mult).then_inc(at_ready, 1)
                    if live(j, 0):
                        ge(dve, hTh_ready, j + 1)
                        dve.tensor_tensor(hTl[:, u % 2, WINDOW:KEYS], p_v[:, 0:P], hTh[:, u % 2, WINDOW:KEYS],
                                          ALU.subtract).then_inc(hT_ready, 1)
                    if live(j, 4):
                        low_probs(j - 4, 0, 0)
                    if live(j, 3):
                        maxes(j - 3, u - 3, 0)
                    if live(j, 4):
                        low_probs(j - 4, 0, 1)
                    if live(j, 1):
                        low_v(j - 1, u - 1, vah, val, vah_done, va_done, P)
                    if live(j, 4):
                        low_probs(j - 4, 1, 0)
                    if live(j, 0):
                        ge(dve, squared, 2 * (j + 1))
                        ge(dve, t3_done, j - 1)
                        rot(j, u, 0)
                    if live(j, 1):
                        low_v(j - 1, u - 1, vbh, vbl, vbh_done, vb_done, WINDOW)
                    if live(j, 4):
                        low_probs(j - 4, 1, 1)
                    if live(j, 3):
                        maxes(j - 3, u - 3, 1)
                    if live(j, 0):
                        rot(j, u, 1)
                        rot(j, u, 2)
                    if live(j, 5):
                        t = j - 5
                        ge(dve, y_ready, t + 1)
                        dve.tensor_tensor(x_sb[:, t, :], p_x[:, 0:D], x_sb[:, t, :], ALU.add).then_inc(x_updated, 1)
                    if live(j, 0):
                        ge(dve, clamped, j - 1)
                        dve.tensor_reduce(ssq[:, u % 2, :], sq[:, :].rearrange("p (g d) -> p g d", d=DH), AX,
                                          ALU.add).then_inc(ssq_done, 1)
                    if isinstance(j, int) and j < 3:
                        lw.scale_table(dve, l, j + 1, tab_ready)
                run_steps(dve, step)


def geglu(nc, l, x_sb, h_tok, ident, lw):
    HID = lw.hid
    chunks = [(k, min(P, HID - k)) for k in range(0, HID, P)]
    HC = len(chunks)
    STEPS = NCH * HC
    with Scope(nc, f"bg{l}_") as sc:
        w1, w2, b1, b2, gb = lw.w1[:, l], lw.w2[:, l], lw.b1[:, l], lw.b2[:, l], lw.gb[:, l]
        ones = sc.sb("ones", [1, P])
        hT = sc.sb("hT", [P, S])
        ge_act = sc.sb("gelu", [P, 2, CH])
        uT = sc.sb("uT", [P, 2, HC, CH])
        p_a = sc.ps("p_a", [P, 2, CH])
        p_g = sc.ps("p_g", [P, 2, CH])
        p_y = sc.ps("p_y", [P, 2, CH])
        p_x = sc.ps("p_x", [P, 2, CH])
        ones_set, turned, hT_ready, ag_ready, gelu_done, hidden, y_ready, x_updated = (
            sc.sem(n) for n in ("ones_set", "turned", "hT_ready", "ag_ready", "gelu_done", "hidden",
                                "y_ready", "x_updated"))
        with nc.Block() as block:

            @block.tensor
            def _(pe):
                for c in range(NCH):
                    if c >= 2:
                        pe.wait_ge(hT_ready, c - 1)
                    for t in range(TPC):
                        mm = pe.transpose(p_x[:, c % 2, t * P:(t + 1) * P], h_tok[:, c * TPC + t, :], ident[:, :])
                    mm.then_inc(turned, 1)

                def down(c):
                    pe.wait_ge(hidden, HC * (c + 1))
                    if c >= 2:
                        pe.wait_ge(x_updated, c - 1)
                    for t in range(TPC):
                        for k, (at, n) in enumerate(chunks):
                            pe.matmul(p_y[:, c % 2, t * P:(t + 1) * P], uT[0:n, c % 2, k, t * P:(t + 1) * P],
                                      w2[0:n, k, :], start=(k == 0), stop=False)
                        mm = pe.matmul(p_y[:, c % 2, t * P:(t + 1) * P], ones[:, :], b2[:, :], start=False, stop=True)
                    mm.then_inc(y_ready, 1)

                pe.wait_ge(lw.ff_in[l], lw.FF)
                pe.wait_ge(ones_set, 1)
                for c in range(NCH):
                    pe.wait_ge(hT_ready, c + 1)
                    for k, (at, n) in enumerate(chunks):
                        m = c * HC + k
                        if m >= 2:
                            pe.wait_ge(hidden, m - 1)
                        pe.matmul(p_g[0:n, m % 2, :], w1[:, HID + at:HID + at + n], hT[:, c * CH:(c + 1) * CH],
                                  start=True, stop=True)
                        pe.matmul(p_a[0:n, m % 2, :], w1[:, at:at + n], hT[:, c * CH:(c + 1) * CH],
                                  start=True, stop=True).then_inc(ag_ready, 1)
                        if c >= 1 and k == 1:
                            down(c - 1)
                down(NCH - 1)

            @block.scalar
            def _(act):
                act.wait_ge(lw.ff_in[l], lw.FF)
                for m in range(STEPS):
                    k, (at, n) = m % HC, chunks[m % HC]
                    act.wait_ge(ag_ready, m + 1)
                    if m >= 2:
                        act.wait_ge(hidden, m - 1)
                    act.activation(ge_act[0:n, m % 2, :], p_g[0:n, m % 2, :], ACT.Gelu,
                                   bias=b1[0:n, 1, k:k + 1]).then_inc(gelu_done, 1)

            @block.vector
            def _(dve):
                dve.memset(ones[:, :], 1.0).then_inc(ones_set, 1)
                dve.wait_ge(lw.ff_in[l], lw.FF)
                for c in range(NCH):
                    dve.wait_ge(turned, c + 1)
                    dve.tensor_scalar(hT[:, c * CH:(c + 1) * CH], p_x[:, c % 2, :], gb[:, 0:1], gb[:, 1:2],
                                      ALU.mult, ALU.add).then_inc(hT_ready, 1)

                def residual(c):
                    dve.wait_ge(y_ready, c + 1)
                    xs = x_sb[:, c * TPC:(c + 1) * TPC, :]
                    dve.tensor_tensor(xs, p_y[:, c % 2, :].rearrange("p (t d) -> p t d", d=D), xs,
                                      ALU.add).then_inc(x_updated, 1)

                for m in range(STEPS):
                    c, k = divmod(m, HC)
                    n = chunks[k][1]
                    dve.wait_ge(gelu_done, m + 1)
                    if c >= 2:
                        dve.wait_ge(y_ready, c - 1)
                    dve.scalar_tensor_tensor(uT[0:n, c % 2, k, :], p_a[0:n, m % 2, :], b1[0:n, 0, k:k + 1],
                                             ge_act[0:n, m % 2, :], ALU.add, ALU.mult).then_inc(hidden, 1)
                    if c >= 1 and k == 2:
                        residual(c - 1)
                residual(NCH - 1)


MIXES = 5
LR = 32
HEADS_C, QK_C, V_C = 16, 4, 8
HPC = P // (QK_C * V_C)
HCH = HEADS_C // HPC


def phase_rwkv(nc, x_sb, ident, a, ln, late):
    with Scope(nc, "c_") as sc:
        tw = sc.sb("tanh_w", [a["ww1"].shape[1], S])
        xi = sc.sb("x_mixed", [P, MIXES, S])
        g_sb = sc.sb("g", [P, S])
        g_th = sc.sb("g_tanh", [P, S])
        o_sb = sc.sb("o", [P, S])
        rwkv_mix(nc, x_sb, ident, a, late, xi, tw, g_sb, g_th)
        rwkv_scan(nc, a, late, xi, tw, o_sb)
        rwkv_out(nc, x_sb, ident, ln, late, o_sb, g_sb, g_th)


def rwkv_mix(nc, x_sb, ident, a, late, xi, tw, g_sb, g_th):
    GATE = a["ww1"].shape[1]
    with Scope(nc, "cm_") as sc:
        xTp = sc.sb("xT_padded", [P, S + 1])
        delta = sc.sb("delta", [P, S])
        z = sc.sb("z", [P, 2, CH])
        low_a = sc.sb("low_a", [P, 2, CH])
        low_b = sc.sb("low_b", [LR, 2, CH])
        tmp = sc.sb("tmp", [P, 2, CH])
        wx1, wx2a, wx2b, ww1, wg, cols = late.wx1, late.wx2a, late.wx2b, late.ww1, late.wg, late.cols
        p_x = sc.ps("p_x", [P, 2, CH])
        p_la = sc.ps("p_la", [P, CH])
        p_lb = sc.ps("p_lb", [P, CH])
        p_mu = sc.ps("p_mu", [P, 2, CH])
        p_tw = sc.ps("p_tw", [P, CH])
        p_g = sc.ps("p_g", [P, CH])
        (x_transposed, pad_set, xT_ready, delta_ready, z_ready, low_ready, tanh_low, mu_ready, tmp_ready,
         mixed, tw_ready, tw_done, g_ready, g_done) = (sc.sem(n) for n in (
             "x_transposed", "pad_set", "xT_ready", "delta_ready", "z_ready", "low_ready", "tanh_low",
             "mu_ready", "tmp_ready", "mixed", "tw_ready", "tw_done", "g_ready", "g_done"))
        with nc.Block() as block:

            @block.tensor
            def _(pe):
                for c in range(NCH):
                    if c >= 2:
                        pe.wait_ge(xT_ready, c - 1)
                    for t in range(TPC):
                        mm = pe.transpose(p_x[:, c % 2, t * P:(t + 1) * P], x_sb[:, c * TPC + t, :], ident[:, :])
                    mm.then_inc(x_transposed, 1)
                pe.wait_ge(late.mix_in, late.MIX)
                for c in range(NCH):
                    pe.wait_ge(z_ready, c + 1)
                    if c >= 1:
                        pe.wait_ge(tanh_low, 2 * c)
                    pe.matmul(p_la[:, :], wx1[:, 0:P], z[:, c % 2, :], start=True, stop=True).then_inc(low_ready, 1)
                    pe.matmul(p_lb[0:LR, :], wx1[:, P:P + LR], z[:, c % 2, :], start=True,
                              stop=True).then_inc(low_ready, 1)
                    pe.wait_ge(tanh_low, 2 * c + 2)
                    for i in range(MIXES):
                        n = MIXES * c + i
                        if n >= 2:
                            pe.wait_ge(tmp_ready, n - 1)
                        if i < 4:
                            lhs, rhs = wx2a[LR * i:LR * i + LR, :], low_a[LR * i:LR * i + LR, c % 2, :]
                        else:
                            lhs, rhs = wx2b[:, :], low_b[:, c % 2, :]
                        pe.matmul(p_mu[:, n % 2, :], lhs, rhs, start=True, stop=True).then_inc(mu_ready, 1)
                    cs = slice(c * CH, (c + 1) * CH)
                    pe.wait_ge(mixed, MIXES * c + 2)
                    if c >= 1:
                        pe.wait_ge(tw_done, c)
                        pe.wait_ge(g_done, 2 * c)
                    pe.matmul(p_tw[0:GATE, :], ww1[:, :], xi[:, 1, cs], start=True, stop=True).then_inc(tw_ready, 1)
                    pe.wait_ge(mixed, MIXES * c + 5)
                    for t in range(TPC):
                        tok = c * CH + t * P
                        mm = pe.matmul(p_g[:, t * P:(t + 1) * P], xi[:, 4, tok:tok + P], wg[:, :],
                                       start=True, stop=True)
                    mm.then_inc(g_ready, 1)

            @block.scalar
            def _(act):
                for c in range(NCH):
                    act.wait_ge(x_transposed, c + 1)
                    act.activation(xTp[:, 1 + c * CH:1 + (c + 1) * CH], p_x[:, c % 2, :],
                                   ACT.Copy).then_inc(xT_ready, 1)
                for c in range(NCH):
                    if c >= 2:
                        act.wait_ge(mu_ready, MIXES * (c - 1))
                    act.wait_ge(low_ready, 2 * c + 1)
                    act.activation(low_a[:, c % 2, :], p_la[:, :], ACT.Tanh).then_inc(tanh_low, 1)
                    act.wait_ge(low_ready, 2 * c + 2)
                    act.activation(low_b[:, c % 2, :], p_lb[0:LR, :], ACT.Tanh).then_inc(tanh_low, 1)
                    cs = slice(c * CH, (c + 1) * CH)
                    act.wait_ge(tw_ready, c + 1)
                    act.activation(tw[:, cs], p_tw[0:GATE, :], ACT.Tanh).then_inc(tw_done, 1)
                    act.wait_ge(g_ready, c + 1)
                    act.activation(g_th[:, cs], p_g[:, :], ACT.Tanh, scale=0.5).then_inc(g_done, 1)
                    act.activation(g_sb[:, cs], p_g[:, :], ACT.Copy).then_inc(g_done, 1)

            @block.vector
            def _(dve):
                dve.memset(xTp[:, 0:1], 0.0).then_inc(pad_set, 1)
                dve.wait_ge(pad_set, 1)
                dve.wait_ge(late.mix_in, late.MIX)

                def delta_z(c):
                    dve.wait_ge(xT_ready, c + 1)
                    dve.tensor_tensor(delta[:, c * CH:(c + 1) * CH], xTp[:, c * CH:(c + 1) * CH],
                                      xTp[:, 1 + c * CH:1 + (c + 1) * CH], ALU.subtract).then_inc(delta_ready, 1)
                    dve.wait_ge(delta_ready, c + 1)
                    if c >= 2:
                        dve.wait_ge(low_ready, 2 * (c - 1))
                    dve.scalar_tensor_tensor(z[:, c % 2, :], delta[:, c * CH:(c + 1) * CH], cols[:, 0:1],
                                             xTp[:, 1 + c * CH:1 + (c + 1) * CH], ALU.mult,
                                             ALU.add).then_inc(z_ready, 1)

                delta_z(0)
                for c in range(NCH):
                    if c + 1 < NCH:
                        delta_z(c + 1)
                    for i in range(MIXES):
                        n = MIXES * c + i
                        dve.wait_ge(mu_ready, n + 1)
                        if n >= 2:
                            dve.wait_ge(mixed, n - 1)
                        dve.scalar_tensor_tensor(tmp[:, n % 2, :], p_mu[:, n % 2, :], cols[:, 1 + i:2 + i],
                                                 delta[:, c * CH:(c + 1) * CH], ALU.add,
                                                 ALU.mult).then_inc(tmp_ready, 1)

            @block.gpsimd
            def _(pool):
                pool.wait_ge(xT_ready, NCH)
                for n in range(NCH * MIXES):
                    c, i = divmod(n, MIXES)
                    pool.wait_ge(tmp_ready, n + 1)
                    pool.tensor_tensor(xi[:, i, c * CH:(c + 1) * CH], tmp[:, n % 2, :],
                                       xTp[:, 1 + c * CH:1 + (c + 1) * CH], ALU.add).then_inc(mixed, 1)


def rwkv_scan(nc, a, late, xi, tw, o_sb):
    GATE = a["ww1"].shape[1]
    R_, K_, V_ = 0, 2, 3
    ROWS = HEADS_C * QK_C * V_C
    OC = HPC * V_C
    STEPS = NCH * HCH
    w, ww2, cols, sel = late.w_rkv, late.ww2, late.scan_cols, late.sel
    with Scope(nc, "cs_") as sc:
        ew = sc.sb("exp_w", [P, 2, CH])
        dec = sc.sb("decay", [P, 2, CH])
        v_sb = sc.sb("v", [P, 2, CH])
        kv = sc.sb("kv", [P, 2, CH])
        st = sc.sb("state", [P, HCH, 2, 1 + CH])
        m = sc.sb("m", [P, 2, CH])
        pr = sc.sb("pr", [P, 2, CH])
        p_w = sc.ps("p_w", [P, CH])
        p_k = sc.ps("p_k", [P, CH])
        p_v = sc.ps("p_v", [P, CH])
        p_r = sc.ps("p_r", [P, CH])
        p_o = sc.ps("p_o", [P, 2, CH])
        (w_ready, k_ready, v_ready, r_ready, exp_done, dec_done, v_done, kv_done, scanned, m_done, pr_done,
         zeroed, carried, o_ready, o_done) = (sc.sem(n) for n in (
             "w_ready", "k_ready", "v_ready", "r_ready", "exp_done", "dec_done", "v_done", "kv_done",
             "scanned", "m_done", "pr_done", "zeroed", "carried", "o_ready", "o_done"))
        with nc.Block() as block:

            @block.tensor
            def _(pe):
                pe.wait_ge(late.scan_in, late.SCAN)

                def out(n):
                    c, h = divmod(n, HCH)
                    pe.wait_ge(pr_done, n + 1)
                    if h == 0 and c >= 2:
                        pe.wait_ge(o_done, c - 1)
                    for t in range(TPC):
                        mm = pe.matmul(p_o[:, c % 2, t * P + h * OC:t * P + (h + 1) * OC],
                                       pr[:, n % 2, t * P:(t + 1) * P], sel[:, :], start=True, stop=True)
                    mm.then_inc(o_ready, 1)

                for n in range(STEPS):
                    c, h = divmod(n, HCH)
                    cs, rs = slice(c * CH, (c + 1) * CH), slice(h * P, (h + 1) * P)
                    if n >= 1:
                        pe.wait_ge(exp_done, n)
                    pe.matmul(p_w[:, :], ww2[:, rs], tw[:, cs], start=True, stop=True).then_inc(w_ready, 1)
                    if n >= 1:
                        pe.wait_ge(v_done, n)
                    pe.matmul(p_v[:, :], w[:, 2, rs], xi[:, V_, cs], start=True, stop=True).then_inc(v_ready, 1)
                    if n >= 1:
                        pe.wait_ge(kv_done, n)
                    pe.matmul(p_k[:, :], w[:, 1, rs], xi[:, K_, cs], start=True, stop=True).then_inc(k_ready, 1)
                    if n >= 1:
                        pe.wait_ge(pr_done, n)
                    pe.matmul(p_r[:, :], w[:, 0, rs], xi[:, R_, cs], start=True, stop=True).then_inc(r_ready, 1)
                    if n >= 1:
                        out(n - 1)
                out(STEPS - 1)

            @block.scalar
            def _(act):
                act.wait_ge(late.scan_in, late.SCAN)
                for n in range(STEPS):
                    h = n % HCH
                    act.wait_ge(w_ready, n + 1)
                    act.activation(ew[:, n % 2, :], p_w[:, :], ACT.Exp, bias=cols[:, 0, h:h + 1]).then_inc(exp_done, 1)
                    act.wait_ge(exp_done, n + 1)
                    if n >= 2:
                        act.wait_ge(scanned, n - 1)
                    act.activation(dec[:, n % 2, :], ew[:, n % 2, :], ACT.Exp, scale=-1.0).then_inc(dec_done, 1)
                    act.wait_ge(v_ready, n + 1)
                    if n >= 2:
                        act.wait_ge(kv_done, n - 1)
                    act.activation(v_sb[:, n % 2, :], p_v[:, :], ACT.Copy).then_inc(v_done, 1)
                    if h == HCH - 1:
                        c = n // HCH
                        if c >= 1:
                            act.wait_ge(o_ready, HCH * c)
                            act.activation(o_sb[:, (c - 1) * CH:c * CH], p_o[:, (c - 1) % 2, :],
                                           ACT.Copy).then_inc(o_done, 1)
                act.wait_ge(o_ready, STEPS)
                act.activation(o_sb[:, (NCH - 1) * CH:], p_o[:, (NCH - 1) % 2, :], ACT.Copy).then_inc(o_done, 1)

            @block.vector
            def _(dve):
                dve.wait_ge(late.scan_in, late.SCAN)
                dve.memset(st[:, :, 0, 0:1], 0.0).then_inc(zeroed, 1)
                dve.wait_ge(zeroed, 1)
                for n in range(STEPS):
                    c, h = divmod(n, HCH)
                    dve.wait_ge(v_done, n + 1)
                    dve.wait_ge(k_ready, n + 1)
                    dve.tensor_tensor(kv[:, n % 2, :], p_k[:, :], v_sb[:, n % 2, :], ALU.mult).then_inc(kv_done, 1)
                    dve.wait_ge(kv_done, n + 1)
                    dve.wait_ge(dec_done, n + 1)
                    if c >= 1:
                        dve.wait_ge(carried, n - HCH + 1)
                    dve.tensor_tensor_scan(st[:, h, c % 2, 1:], dec[:, n % 2, :], kv[:, n % 2, :],
                                           st[:, h, c % 2, 0:1], ALU.mult, ALU.add).then_inc(scanned, 1)
                    dve.wait_ge(scanned, n + 1)
                    dve.tensor_copy(st[:, h, (c + 1) % 2, 0:1], st[:, h, c % 2, CH:CH + 1]).then_inc(carried, 1)
                    dve.scalar_tensor_tensor(m[:, n % 2, :], kv[:, n % 2, :], cols[:, 1, h:h + 1],
                                             st[:, h, c % 2, 0:CH], ALU.mult, ALU.add).then_inc(m_done, 1)
                    dve.wait_ge(m_done, n + 1)
                    dve.wait_ge(r_ready, n + 1)
                    if n >= 2:
                        dve.wait_ge(o_ready, n - 1)
                    dve.tensor_tensor(pr[:, n % 2, :], m[:, n % 2, :], p_r[:, :], ALU.mult).then_inc(pr_done, 1)


def rwkv_out(nc, x_sb, ident, ln, late, o_sb, g_sb, g_th):
    NG = NT * HEADS_C
    wo, gn = late.wo, late.gn
    with Scope(nc, "co_") as sc:
        eps = sc.sb("eps", [P, 1])
        tot = sc.sb("tot", [P, NG])
        mean = sc.sb("mean", [P, NG])
        oc = sc.sb("centred", [P, S])
        sq = sc.sb("sq", [P, S])
        ssq = sc.sb("ssq", [P, NG])
        std = sc.sb("std", [P, NG])
        rstd = sc.sb("rstd", [P, NG])
        gate = sc.sb("gate", [P, S])
        oT = sc.sb("oT", [P, S])
        rows = sc.sb("rows", [P, NT, D])
        p_t = sc.ps("p_t", [P, 2, CH])
        p_y = sc.ps("p_y", [P, 2, CH])
        (step, squared, ssq_done, std_done, gated, transposed, oT_ready, y_ready, rows_ready) = (
            sc.sem(n) for n in ("dve_step", "squared", "ssq_done", "std_done", "gated", "transposed",
                                "oT_ready", "y_ready", "rows_ready"))
        heads = lambda t: t[:, :].rearrange("p (g v) -> p g v", v=V_C)
        tiles = lambda t: t[:, :].rearrange("p (t d) -> p t d", d=D)
        with nc.Block() as block:

            @block.vector
            def _(dve):
                dve.memset(eps[:, :], LN_EPS).then_inc(step, 1)
                dve.tensor_reduce(tot[:, :], heads(o_sb), AX, ALU.add).then_inc(step, 1)
                dve.wait_ge(step, 2)
                dve.tensor_scalar(mean[:, :], tot[:, :], 1.0 / V_C, None, ALU.mult).then_inc(step, 1)
                dve.wait_ge(step, 3)
                dve.tensor_tensor(heads(oc), heads(o_sb), mean[:, :].unsqueeze(2).to_broadcast([P, NG, V_C]),
                                  ALU.subtract).then_inc(step, 1)
                dve.scalar_tensor_tensor(gate[:, :], g_th[:, :], 1.0, g_sb[:, :], ALU.add,
                                         ALU.mult).then_inc(step, 1)
                dve.wait_ge(squared, 1)
                dve.tensor_reduce(ssq[:, :], heads(sq), AX, ALU.add).then_inc(ssq_done, 1)
                dve.wait_ge(std_done, 1)
                dve.reciprocal(rstd[:, :], std[:, :]).then_inc(step, 1)
                dve.wait_ge(step, 6)
                dve.tensor_tensor(heads(sq), heads(oc), rstd[:, :].unsqueeze(2).to_broadcast([P, NG, V_C]),
                                  ALU.mult).then_inc(step, 1)
                dve.wait_ge(late.out_in, late.OUT)
                dve.wait_ge(step, 7)
                dve.tensor_tensor(tiles(oc), tiles(sq), gn[:, 0:1, :].to_broadcast([P, NT, D]),
                                  ALU.mult).then_inc(step, 1)
                dve.wait_ge(step, 8)
                dve.tensor_tensor(tiles(sq), tiles(oc), gn[:, 1:2, :].to_broadcast([P, NT, D]),
                                  ALU.add).then_inc(step, 1)
                dve.wait_ge(step, 9)
                for c in range(NCH):
                    cs = slice(c * CH, (c + 1) * CH)
                    dve.scalar_tensor_tensor(oc[:, cs], sq[:, cs], 0.5, gate[:, cs], ALU.mult,
                                             ALU.mult).then_inc(gated, 1)
                for c in range(NCH):
                    dve.wait_ge(y_ready, c + 1)
                    dve.tensor_tensor(rows[:, c * TPC:(c + 1) * TPC, :],
                                      p_y[:, c % 2, :].rearrange("p (t d) -> p t d", d=D),
                                      x_sb[:, c * TPC:(c + 1) * TPC, :], ALU.add).then_inc(rows_ready, 1)

            @block.scalar
            def _(act):
                act.wait_ge(step, 4)
                act.activation(sq[:, :], oc[:, :], ACT.Square).then_inc(squared, 1)
                act.wait_ge(ssq_done, 1)
                act.activation(std[:, :], ssq[:, :], ACT.Sqrt, scale=1.0 / V_C, bias=eps[:, 0:1]).then_inc(std_done, 1)
                for c in range(NCH):
                    act.wait_ge(transposed, c + 1)
                    act.activation(oT[:, c * CH:(c + 1) * CH], p_t[:, c % 2, :], ACT.Copy).then_inc(oT_ready, 1)

            @block.tensor
            def _(pe):
                for c in range(NCH):
                    pe.wait_ge(gated, c + 1)
                    if c >= 2:
                        pe.wait_ge(oT_ready, c - 1)
                    for t in range(TPC):
                        mm = pe.transpose(p_t[:, c % 2, t * P:(t + 1) * P],
                                          oc[:, c * CH + t * P:c * CH + (t + 1) * P], ident[:, :])
                    mm.then_inc(transposed, 1)
                pe.wait_ge(late.out_in, late.OUT)
                for c in range(NCH):
                    pe.wait_ge(oT_ready, c + 1)
                    if c >= 2:
                        pe.wait_ge(rows_ready, c - 1)
                    for t in range(TPC):
                        mm = pe.matmul(p_y[:, c % 2, t * P:(t + 1) * P], oT[:, c * CH + t * P:c * CH + (t + 1) * P],
                                       wo[:, :], start=True, stop=True)
                    mm.then_inc(y_ready, 1)
        layernorm_block(nc, ln, "cln_", rows, x_sb)


def phase_int_ffn(nc, x_sb, ident, a, ln, late):
    HID = a["wg_t"].shape[1]
    HC = HID // P
    STEPS = NCH * HC
    SCALE = float(np.float32(1.0 / 127.0))
    with Scope(nc, "d_") as sc:
        wi = late.w_int
        wf = sc.sb("w_f32", [P, 3, HID])
        xT = sc.sb("xT", [P, S])
        th = sc.sb("tanh", [P, 2, CH])
        t1 = sc.sb("gate_act", [P, 2, CH])
        hT = sc.sb("hT", [P, 2, HC, CH])
        rows = sc.sb("rows", [P, NT, D])
        p_gate = sc.ps("p_gate", [P, 2, CH])
        p_up = sc.ps("p_up", [P, 2, CH])
        p_y = sc.ps("p_y", [P, 2, CH])
        p_x = sc.ps("p_x", [P, 2, CH])
        names = ("w_ready", "x_transposed", "xT_ready", "gate_up", "tanh_done", "act_done", "hidden",
                 "y_ready", "rows_ready")
        w_ready, x_transposed, xT_ready, gate_up, tanh_done, act_done, hidden, y_ready, rows_ready = (
            sc.sem(n) for n in names)
        with nc.Block() as block:

            @block.tensor
            def _(pe):
                for c in range(NCH):
                    if c >= 2:
                        pe.wait_ge(xT_ready, c - 1)
                    for t in range(TPC):
                        mm = pe.transpose(p_x[:, c % 2, t * P:(t + 1) * P], x_sb[:, c * TPC + t, :], ident[:, :])
                    mm.then_inc(x_transposed, 1)

                def down(c):
                    pe.wait_ge(hidden, HC * (c + 1))
                    if c >= 2:
                        pe.wait_ge(rows_ready, c - 1)
                    for t in range(TPC):
                        for k in range(HC):
                            mm = pe.matmul(p_y[:, c % 2, t * P:(t + 1) * P], hT[:, c % 2, k, t * P:(t + 1) * P],
                                           wf[:, 2, k * P:(k + 1) * P], start=(k == 0), stop=(k == HC - 1))
                    mm.then_inc(y_ready, 1)

                pe.wait_ge(w_ready, 3)
                for c in range(NCH):
                    pe.wait_ge(xT_ready, c + 1)
                    for k in range(HC):
                        n = c * HC + k
                        if n >= 2:
                            pe.wait_ge(hidden, n - 1)
                        pe.matmul(p_gate[:, n % 2, :], wf[:, 0, k * P:(k + 1) * P], xT[:, c * CH:(c + 1) * CH],
                                  start=True, stop=True)
                        pe.matmul(p_up[:, n % 2, :], wf[:, 1, k * P:(k + 1) * P], xT[:, c * CH:(c + 1) * CH],
                                  start=True, stop=True).then_inc(gate_up, 1)
                        if c >= 1 and k == 1:
                            down(c - 1)
                down(NCH - 1)

            @block.scalar
            def _(act):
                for c in range(NCH):
                    act.wait_ge(x_transposed, c + 1)
                    act.activation(xT[:, c * CH:(c + 1) * CH], p_x[:, c % 2, :], ACT.Copy).then_inc(xT_ready, 1)
                for n in range(STEPS):
                    act.wait_ge(gate_up, n + 1)
                    if n >= 2:
                        act.wait_ge(act_done, n - 1)
                    act.activation(th[:, n % 2, :], p_gate[:, n % 2, :], ACT.Tanh, scale=0.5).then_inc(tanh_done, 1)

            @block.vector
            def _(dve):
                dve.wait_ge(late.int_in, late.INT)
                for k in range(3):
                    dve.tensor_scalar(wf[:, k, :], wi[:, k, :], SCALE, None, ALU.mult).then_inc(w_ready, 1)

                def residual(c):
                    dve.wait_ge(y_ready, c + 1)
                    dve.tensor_tensor(rows[:, c * TPC:(c + 1) * TPC, :],
                                      p_y[:, c % 2, :].rearrange("p (t d) -> p t d", d=D),
                                      x_sb[:, c * TPC:(c + 1) * TPC, :], ALU.add).then_inc(rows_ready, 1)

                for n in range(STEPS):
                    c, k = divmod(n, HC)
                    dve.wait_ge(tanh_done, n + 1)
                    dve.scalar_tensor_tensor(t1[:, n % 2, :], th[:, n % 2, :], 1.0, p_gate[:, n % 2, :],
                                             ALU.add, ALU.mult).then_inc(act_done, 1)
                    dve.wait_ge(act_done, n + 1)
                    if c >= 2:
                        dve.wait_ge(y_ready, c - 1)
                    dve.scalar_tensor_tensor(hT[:, c % 2, k, :], t1[:, n % 2, :], 0.5, p_up[:, n % 2, :],
                                             ALU.mult, ALU.mult).then_inc(hidden, 1)
                    if c >= 1 and k == 2:
                        residual(c - 1)
                residual(NCH - 1)
        layernorm_block(nc, ln, "dln_", rows, x_sb)


def build(nc, a, out):
    Scope.used.clear()
    Scope.long.clear()
    with Scope(nc, "g_") as sc:
        x_sb = sc.sb("x", [P, NT, D])
        ident = sc.sb("ident", [P, P])
        ln = LayerNorm(sc)
        load_block(nc, x_sb, ident, a["x"], a["ident"])
        with Scope(nc, "cdw_", side="right") as late_scope:
            with Scope(nc, "bw_", side="right") as local_scope:
                local, late = phase_mha(nc, x_sb, ident, a, ln, local_scope, late_scope)
                clear_semaphores(nc)
                phase_local(nc, x_sb, ident, ln, local)
            phase_rwkv(nc, x_sb, ident, a, ln, late)
            phase_int_ffn(nc, x_sb, ident, a, ln, late)
        store_block(nc, x_sb, out)
    clear_semaphores(nc, all_of_them=True)


def _local_rotation_tables():
    f = np.float32
    half_idx = np.arange(0, DH, 2, dtype=f)
    inv_freq = f(1.0) / np.power(f(10000.0), half_idx / f(DH))
    t = np.arange(S, dtype=f)
    ang = np.tile(t[:, None] * inv_freq[None, :], 2)
    base = (half_idx + f(0.4 * DH)) / f(1.4 * DH)
    scale = np.tile(np.power(base[None, :].astype(np.float64), ((t - S // 2) / f(WINDOW // 2))[:, None]), 2)
    sign = np.where(np.arange(DH) < HALF, -1.0, 1.0)
    cos, sin = np.cos(ang.astype(np.float64)), np.sin(ang.astype(np.float64)) * sign
    both = np.stack([np.stack([w * 8.0 * scale, w / scale], 1) for w in (cos, sin)])
    return np.ascontiguousarray(both.reshape(2, NT, P, 2, DH).transpose(2, 0, 1, 3, 4).astype(f))


def _band_mask():
    q = np.arange(P)[:, None]
    k = np.arange(KEYS)[None, :] - WINDOW
    ok = (k <= q) & (k >= q - WINDOW)
    both = np.stack([ok & (k >= 0), ok])
    m = np.where(both, 0.0, -1e30).astype(np.float32)
    return np.ascontiguousarray(np.concatenate([m, m], -1).transpose(1, 0, 2))


def _rotation_tables():
    f = np.float32
    half = HD // 2
    freq = f(1.0) / np.power(f(10000.0), np.arange(half, dtype=f) / f(half))
    ang = (freq[:, None] * np.arange(S, dtype=f)[None, :]).astype(np.float64)
    cos, sin = np.cos(ang).astype(f), np.sin(ang).astype(f)
    return np.ascontiguousarray(np.tile(cos, (4, 1))), np.ascontiguousarray(np.concatenate([-sin, sin, -sin, sin]))


def _layouts(i):
    f = np.float32
    c = np.ascontiguousarray
    a = {"x": c(i["L0_attn_x"][0]), "ident": np.eye(P, dtype=f)}
    w = i["L0_attn_qkv_w"].reshape(D, 3, HEADS, HD)
    order = np.concatenate([np.arange(0, HD, 2), np.arange(1, HD, 2)])
    a["w_heads"] = c(np.concatenate([w[:, 0][..., order], w[:, 1][..., order], w[:, 2]], -1).transpose(1, 0, 2))
    b = i["L0_attn_qkv_b"].reshape(3, HEADS, HD)
    a["b_qk"] = c(np.concatenate([b[0][:, order], b[1][:, order]], -1).T)
    a["b_v"] = c(np.broadcast_to(b[2], (P, HEADS, HD)))
    a["cos"], a["sin"] = _rotation_tables()
    a["wo_a"] = i["L0_attn_out_w"]
    a["b_o"] = c(np.broadcast_to(i["L0_attn_out_b"], (P, 1, D)))
    a["rot"] = _local_rotation_tables()
    qk_scale = np.stack([i["L0_ffn_q_scale"], i["L0_ffn_k_scale"]], 1)
    a["qk_scale"] = c(np.broadcast_to(np.stack([qk_scale, np.roll(qk_scale, 32, -1)], 1), (P, 2, 2, 2, 64)))
    a["mask"] = _band_mask()
    a["wqkv"] = i["L0_ffn_wqkv"]
    a["wo_b"] = i["L0_ffn_wo"]
    a["ln_gb"] = c(np.stack([i["L0_ffn_ln_g"], i["L0_ffn_ln_b"]], -1))
    a["w1"] = i["L0_ffn_w1"]
    hid = i["L0_ffn_w2"].shape[1]
    b1 = np.zeros((2, 2, 3 * P), f)
    b1[:, :, :hid] = i["L0_ffn_b1"].reshape(2, 2, hid)
    a["b1"] = c(b1.reshape(2, 2, 3, P).transpose(0, 3, 1, 2))
    a["w2"] = i["L0_ffn_w2"]
    a["b2"] = i["L0_ffn_b2"]
    heads, qk, vd = 16, 4, 8
    over_v = lambda w: np.repeat(w, vd, axis=-1)
    over_qk = lambda w: np.repeat(w.reshape(w.shape[:-1] + (heads, 1, vd)), qk, axis=-2).reshape(w.shape[:-1] + (-1,))
    rows = lambda v: c(v.reshape(4, P).T)
    a["mix_cols"] = c(np.stack([i["L1_attn_mu_x"], *i["L1_attn_x_bias"]], 1))
    a["wx1"] = i["L1_attn_W_x1"]
    a["wx2_t"] = c(i["L1_attn_W_x2"].transpose(1, 2, 0).reshape(-1, D))
    a["ww1"] = i["L1_attn_W_w1"]
    a["wg"] = i["L1_attn_W_g"]
    a["ww2_rep"] = c(over_v(i["L1_attn_W_w2"]))
    a["w_rkv_rep"] = c(np.stack([over_v(i["L1_attn_W_r"]), over_v(i["L1_attn_W_k"]), over_qk(i["L1_attn_W_v"])], 1))
    a["scan_cols"] = c(np.stack([rows(over_v(i["L1_attn_b_w2"])), rows(over_v(i["L1_attn_u"].reshape(-1)))], 1))
    a["sel"] = c(np.eye(32, dtype=f).reshape(4, 1, 8, 32).repeat(4, 1).reshape(P, 32))
    a["wo_c"] = i["L1_attn_W_o"]
    a["gn"] = c(np.broadcast_to(np.stack([i["L1_attn_gn_w"], i["L1_attn_gn_b"]]), (P, 2, D)))
    a["wg_t"] = c(i["L1_ffn_w_gate"].T)
    a["wu_t"] = c(i["L1_ffn_w_up"].T)
    a["wd_t"] = c(i["L1_ffn_w_down"].T)
    return a


def kernel(**inputs):
    import concourse.bacc as bacc
    from concourse.bass_utils import run_bass_kernel_spmd

    arrays = _layouts({k: np.asarray(v) for k, v in inputs.items()})
    nc = bacc.Bacc("TRN2", target_bir_lowering=False, num_devices=1)
    aps = {n: nc.dram_tensor(f"in_{n}", v.shape, mybir.dt.from_np(v.dtype), kind="ExternalInput").ap()
           for n, v in arrays.items()}
    out = nc.dram_tensor("out", (S, D), F32, kind="ExternalOutput").ap()
    build(nc, aps, out)
    r = run_bass_kernel_spmd(nc, [{f"in_{n}": v for n, v in arrays.items()}], core_ids=[0])
    return r.results[0]["out"].reshape(1, S, D)
```
